# Optimizing a Trainium2 kernel written in Bass

```python
import numpy as np
import jax
import jax.numpy as jnp

def _softmax(x, axis=-1):
    return jax.nn.softmax(x, axis=axis)

def _gelu(x):
    return jax.nn.gelu(x, approximate=True)

def _silu(x):
    return jax.nn.silu(x)

def _sigmoid(x):
    return jax.nn.sigmoid(x)

def _layernorm(x, axis=-1, eps=1e-05):
    m = jnp.mean(x, axis=axis, keepdims=True)
    v = jnp.var(x, axis=axis, keepdims=True)
    return (x - m) / jnp.sqrt(v + eps)

def _scatter_add(tgt, idx, src, axis=0):
    return tgt.at[idx].add(src)

def _segment_sum(src, seg, n):
    return jax.ops.segment_sum(src, seg, n)
kernel_name = 'mk_gnn_preln_d2_gnn_r8_b59948'

def setup_inputs(seed: int=0):
    np.random.seed(seed)
    _w = jnp.asarray

    def _rec_inputs():
        import jax
        import jax.numpy as jnp
        _gk = jax.random.key(seed)
        x = -0.0003713 + 1 * jax.random.normal(jax.random.fold_in(_gk, 1), (6250, 256), jnp.float32)
        _s = jax.random.randint(jax.random.fold_in(_gk, 2), (100000,), 0, 6250, jnp.int32)
        _d = jax.random.randint(jax.random.fold_in(_gk, 3), (100000,), 0, 6250, jnp.int32)
        _loop = jnp.arange(6250, dtype=jnp.int32)
        src = jnp.concatenate([_s, _d, _loop])
        dst = jnp.concatenate([_d, _s, _loop])
        _o = jnp.argsort(dst, stable=True)
        src = src[_o]
        dst = dst[_o]
        edge_attr_16 = -0.000153872 + 1.00011 * jax.random.normal(jax.random.fold_in(_gk, 12), (206250, 16), jnp.float32)
        edge_attr_4 = 0.0007022 + 0.999661 * jax.random.normal(jax.random.fold_in(_gk, 13), (206250, 4), jnp.float32)
        edge_weight = jax.random.uniform(jax.random.fold_in(_gk, 15), (206250,), jnp.float32, 0.0, 0.999999)
        return (x, src, dst, edge_attr_16, edge_attr_4, edge_weight)
    x, src, dst, edge_attr_16, edge_attr_4, edge_weight = _rec_inputs()

    def _L0_gnn_setup():
        import jax, jax.numpy as jnp
        import numpy as np
        N_NODES = 6250
        N_EDGES = 100000
        D_IN = 256
        D_OUT = 256
        key = jax.random.key(seed)
        ks = jax.random.split(key, 7)
        stdv = 1.0 / np.sqrt(D_OUT)
        x = jax.random.normal(ks[0], (N_NODES, D_IN), dtype=jnp.float32)
        edge_src = jax.random.randint(ks[1], (N_EDGES,), 0, N_NODES, dtype=jnp.int32)
        edge_dst = jax.random.randint(ks[2], (N_EDGES,), 0, N_NODES, dtype=jnp.int32)
        edge_weight = jax.random.uniform(ks[3], (N_EDGES,), dtype=jnp.float32)
        W_self = jax.random.uniform(ks[4], (D_IN, D_OUT), minval=-stdv, maxval=stdv, dtype=jnp.float32)
        W_neighbor = jax.random.uniform(ks[5], (D_IN, D_OUT), minval=-stdv, maxval=stdv, dtype=jnp.float32)
        bias = jax.random.uniform(ks[6], (D_OUT,), minval=-stdv, maxval=stdv, dtype=jnp.float32)
        return {'x': x, 'edge_src': edge_src, 'edge_dst': edge_dst, 'edge_weight': edge_weight, 'W_self': W_self, 'W_neighbor': W_neighbor, 'bias': bias}
    _L0_gnn_all = _L0_gnn_setup()
    _L0_gnn_in = {k: v for k, v in _L0_gnn_all.items() if k in ('W_self', 'W_neighbor', 'bias')}
    del _L0_gnn_all

    def _L1_gnn_setup():
        import jax, jax.numpy as jnp
        import numpy as np
        N, E, C, R, HID = (6250, 62500, 64, 16, 64)
        key = jax.random.key(seed)
        ks = jax.random.split(key, 24)
        g = lambda k, shape, s=1.0: jax.random.normal(k, shape, dtype=jnp.float32) * s
        cs = C ** (-0.5)
        inp = {'h': g(ks[0], (N, 4 * C)), 'edge_index': jax.random.randint(ks[1], (2, E), 0, N), 'edge_sh': g(ks[2], (E, 4)), 'edge_rbf': g(ks[3], (E, R)), 'W_up0': g(ks[4], (C, C), cs), 'W_up1': g(ks[5], (C, C), cs), 'M1': g(ks[6], (R, HID), R ** (-0.5)), 'M2': g(ks[7], (HID, HID), HID ** (-0.5)), 'M3': g(ks[8], (HID, HID), HID ** (-0.5)), 'M4': g(ks[9], (HID, 4 * C), HID ** (-0.5)), 'W_lin0': g(ks[10], (C, C), cs), 'W_lin1': g(ks[11], (C, C), cs), 'Wsc0': g(ks[12], (C, C), cs), 'Wsc1': g(ks[13], (C, C), cs), 'Wc0': g(ks[14], (C, 5)), 'Wc1': g(ks[15], (C, 4)), 'WB0': g(ks[16], (C, C), cs), 'WB1': g(ks[17], (C, C), cs), 'gamma0': jnp.ones((C,), jnp.float32), 'beta0': jnp.zeros((C,), jnp.float32), 'gamma1': jnp.ones((C,), jnp.float32)}
        return inp
    _L1_gnn_all = _L1_gnn_setup()
    _L1_gnn_in = {k: v for k, v in _L1_gnn_all.items() if k in ('W_up0', 'W_up1', 'M1', 'M2', 'M3', 'M4', 'W_lin0', 'W_lin1', 'Wsc0', 'Wsc1', 'Wc0', 'Wc1', 'WB0', 'WB1', 'gamma0', 'beta0', 'gamma1')}
    del _L1_gnn_all
    return {'x': x, 'src': src, 'dst': dst, 'edge_attr_16': edge_attr_16, 'edge_attr_4': edge_attr_4, 'edge_weight': edge_weight, 'L0_gnn_W_self': _L0_gnn_in['W_self'], 'L0_gnn_W_neighbor': _L0_gnn_in['W_neighbor'], 'L0_gnn_bias': _L0_gnn_in['bias'], 'L1_gnn_W_up0': _L1_gnn_in['W_up0'], 'L1_gnn_W_up1': _L1_gnn_in['W_up1'], 'L1_gnn_M1': _L1_gnn_in['M1'], 'L1_gnn_M2': _L1_gnn_in['M2'], 'L1_gnn_M3': _L1_gnn_in['M3'], 'L1_gnn_M4': _L1_gnn_in['M4'], 'L1_gnn_W_lin0': _L1_gnn_in['W_lin0'], 'L1_gnn_W_lin1': _L1_gnn_in['W_lin1'], 'L1_gnn_Wsc0': _L1_gnn_in['Wsc0'], 'L1_gnn_Wsc1': _L1_gnn_in['Wsc1'], 'L1_gnn_Wc0': _L1_gnn_in['Wc0'], 'L1_gnn_Wc1': _L1_gnn_in['Wc1'], 'L1_gnn_WB0': _L1_gnn_in['WB0'], 'L1_gnn_WB1': _L1_gnn_in['WB1'], 'L1_gnn_gamma0': _L1_gnn_in['gamma0'], 'L1_gnn_beta0': _L1_gnn_in['beta0'], 'L1_gnn_gamma1': _L1_gnn_in['gamma1']}

def reference(x, src, dst, edge_attr_16, edge_attr_4, edge_weight, L0_gnn_W_self, L0_gnn_W_neighbor, L0_gnn_bias, L1_gnn_W_up0, L1_gnn_W_up1, L1_gnn_M1, L1_gnn_M2, L1_gnn_M3, L1_gnn_M4, L1_gnn_W_lin0, L1_gnn_W_lin1, L1_gnn_Wsc0, L1_gnn_Wsc1, L1_gnn_Wc0, L1_gnn_Wc1, L1_gnn_WB0, L1_gnn_WB1, L1_gnn_gamma0, L1_gnn_beta0, L1_gnn_gamma1):
    import jax
    import jax.numpy as jnp

    def _L0_gnn_ref(x, edge_src, edge_dst, edge_weight, W_self, W_neighbor, bias):
        import jax, jax.numpy as jnp
        import numpy as np
        N_NODES = 6250
        N_EDGES = 100000
        D_IN = 256
        D_OUT = 256
        act_self = x @ W_self
        support = x @ W_neighbor
        gathered = support[edge_src] * edge_weight[:, None]
        act_neighbor = jax.ops.segment_sum(gathered, edge_dst, num_segments=N_NODES)
        return act_self + act_neighbor + bias

    def _L1_gnn_ref(h, edge_index, edge_sh, edge_rbf, W_up0, W_up1, M1, M2, M3, M4, W_lin0, W_lin1, Wsc0, Wsc1, Wc0, Wc1, WB0, WB1, gamma0, beta0, gamma1):
        import jax, jax.numpy as jnp
        import numpy as np
        N, E, C, R, HID = (6250, 62500, 64, 16, 64)
        n = h.shape[0]
        h0 = h[:, :C]
        h1 = h[:, C:].reshape(n, C, 3)
        up0 = h0 @ W_up0
        up1 = jnp.einsum('ncx,cd->ndx', h1, W_up1)
        r = jax.nn.silu(edge_rbf @ M1)
        r = jax.nn.silu(r @ M2)
        r = jax.nn.silu(r @ M3)
        tpw = (r @ M4).reshape(-1, 4, C)
        snd, rcv = (edge_index[0], edge_index[1])
        x0 = up0[snd]
        x1 = up1[snd]
        sh0 = edge_sh[:, 0]
        sh1 = edge_sh[:, 1:]
        inv3 = 1.0 / jnp.sqrt(jnp.float32(3.0))
        m0e = tpw[:, 0] * x0 * sh0[:, None] + tpw[:, 3] * jnp.einsum('ecx,ex->ec', x1, sh1) * inv3
        m1e = tpw[:, 1][:, :, None] * x0[:, :, None] * sh1[:, None, :] + tpw[:, 2][:, :, None] * x1 * sh0[:, None, None]
        msg0 = jax.ops.segment_sum(m0e, rcv, num_segments=n)
        msg1 = jax.ops.segment_sum(m1e, rcv, num_segments=n)
        A0 = msg0 @ W_lin0
        A1 = jnp.einsum('ncx,cd->ndx', msg1, W_lin1)
        sc0 = h0 @ Wsc0
        sc1 = jnp.einsum('ncx,cd->ndx', h1, Wsc1)
        vv = jnp.sum(A1 * A1, -1)
        B0 = Wc0[:, 0] * A0 + Wc0[:, 1] * A0 * A0 + Wc0[:, 2] * vv + Wc0[:, 3] * A0 ** 3 + Wc0[:, 4] * A0 * vv
        B1 = (Wc1[:, 0] + Wc1[:, 1] * A0 + Wc1[:, 2] * A0 * A0 + Wc1[:, 3] * vv)[..., None] * A1
        o0 = B0 @ WB0 + sc0
        o1 = jnp.einsum('ncx,cd->ndx', B1, WB1) + sc1
        eps = jnp.float32(1e-05)
        mu = jnp.mean(o0, 0)
        xc = o0 - mu
        var = jnp.mean(xc * xc, 0)
        n0 = xc * jax.lax.rsqrt(var + eps) * gamma0 + beta0
        nrm1 = jnp.mean(jnp.sum(o1 * o1, -1) / 3.0, 0)
        n1 = o1 * (jax.lax.rsqrt(nrm1 + eps) * gamma1)[None, :, None]
        return jnp.concatenate([n0, n1.reshape(n, 3 * C)], -1)
    edge_index = jnp.stack([src, dst])
    h = jnp.maximum(_layernorm(x, axis=-1), 0.0)
    x = x + _L0_gnn_ref(h, src, dst, edge_weight, L0_gnn_W_self, L0_gnn_W_neighbor, L0_gnn_bias)
    h = jnp.maximum(_layernorm(x, axis=-1), 0.0)
    x = x + _L1_gnn_ref(h, edge_index, edge_attr_4, edge_attr_16, L1_gnn_W_up0, L1_gnn_W_up1, L1_gnn_M1, L1_gnn_M2, L1_gnn_M3, L1_gnn_M4, L1_gnn_W_lin0, L1_gnn_W_lin1, L1_gnn_Wsc0, L1_gnn_Wsc1, L1_gnn_Wc0, L1_gnn_Wc1, L1_gnn_WB0, L1_gnn_WB1, L1_gnn_gamma0, L1_gnn_beta0, L1_gnn_gamma1)
    return x

_drawn_inputs = setup_inputs


def setup_inputs(seed=0):
    import zlib

    import numpy as np

    out = dict(_drawn_inputs(seed))
    spreads = {'L1_gnn_gamma0': (1.0, 0.6), 'L1_gnn_beta0': (0.0, 0.697), 'L1_gnn_gamma1': (1.0, 0.2)}
    factors = {'L0_gnn_bias': 7.118, 'L1_gnn_Wsc0': 8.0, 'L1_gnn_Wsc1': 4.778}
    for name, (base, spread) in spreads.items():
        noise = np.random.default_rng([zlib.crc32(name.encode()), seed]).standard_normal(out[name].shape)
        drawn = base * np.exp(spread * noise) if base else spread * noise
        out[name] = jnp.asarray(drawn.astype(out[name].dtype))
    for name, factor in factors.items():
        out[name] = (out[name] * factor).astype(out[name].dtype)
    return out
```

```python
from contextlib import ExitStack

import concourse.bass as bass
from concourse import mybir

F32 = mybir.dt.float32
I32 = mybir.dt.int32
ALU = mybir.AluOpType
ACT = mybir.ActivationFunctionType
AX_X = mybir.AxisListType.X
ds = bass.ds

P = 128
N = 6250
E = 206250
D = 256
C = 64
R = 16
EPS = 1e-5

G = 4
SC = P * G
NU = -(-E // (2 * SC))
NSC = 2 * NU
EPAD = NU * 2 * SC
ETAIL = E - (NU - 1) * 2 * SC
ROUNDS = NU // 2
SROWS = NSC // 4
WU = 128
W = 32

T = 50
NPAD = T * P
LAST = N - (T - 2) * P
NCH = 5
TC = T // NCH
H = T // 2
HN = H * P
BN = 320
assert NU % 2 == 0 and SROWS * 4 == NSC and SC // 2 < ETAIL < SC


def bc(ap, axis, n):
    ap = ap.unsqueeze(axis)
    shape = list(ap.shape)
    shape[axis] = n
    return ap.to_broadcast(shape)


def build(nc, x, src, dst, attr16, attr4, weight, w_self, w_nb, bias, w_up0, w_up1, m1, m2, m3, m4,
          w_lin0, w_lin1, w_sc0, w_sc1, wc0, wc1, w_b0, w_b1, gamma0, beta0, gamma1, out):
    h_tab = nc.dram_tensor("h_tab", [NPAD, D], F32).ap()
    up_tab = nc.dram_tensor("up_tab", [NPAD, D], F32).ap()
    x2_tab = nc.dram_tensor("x2_tab", [NPAD, D], F32).ap()
    h2t_tab = nc.dram_tensor("h2t_tab", [P, T * D], F32).ap()
    r3_tab = nc.dram_tensor("r3_tab", [NU, P, 4 * P], F32).ap()
    src_tail = nc.dram_tensor("src_tail", [2 * SC], I32).ap()
    dst_tail = nc.dram_tensor("dst_tail", [2 * SC], I32).ap()
    w_tail = nc.dram_tensor("w_tail", [2 * SC], F32).ap()
    a4_tail = nc.dram_tensor("a4_tail", [2 * SC, 4], F32).ap()
    a16_tail = nc.dram_tensor("a16_tail", [2 * SC, R], F32).ap()

    E0 = (NU - 1) * 2 * SC

    def units(full, tail):
        if len(full.shape) == 1:
            return (full[0:E0].rearrange("(u j p g) -> u p j g", j=2, p=P, g=G),
                    tail.rearrange("(j p g) -> p j g", j=2, p=P))
        return (full[0:E0, :].rearrange("(u j p g) f -> u p j (g f)", j=2, p=P, g=G),
                tail.rearrange("(j p g) f -> p j (g f)", j=2, p=P))

    src_u, dst_u, w_u = units(src, src_tail), units(dst, dst_tail), units(weight, w_tail)
    a4_u, a16_u = units(attr4, a4_tail), units(attr16, a16_tail)

    def unit_of(view, u):
        if isinstance(u, int) and u == NU - 1:
            return view[1]
        return view[0][ds(u, 1), :, :, :].rearrange("o p j g -> (o p) j g")

    def row(ap):
        return ap.rearrange("p o n -> p (o n)")

    def rows(tab, t, n):
        return tab[ds(t * P, n * P), :].rearrange("(t p) d -> p t d", p=P)

    with ExitStack() as ctx:
        def sb(name, shape, dt=F32):
            return ctx.enter_context(nc.sbuf_tensor(name, shape, dt))

        def sem(name):
            return ctx.enter_context(nc.semaphore(name))

        acc = sb("acc", [P, 4, NPAD])
        work = sb("work", [P, T * D + 2560])
        mlp = sb("mlp", [P, 2560])
        ident = sb("ident", [P, P])
        ones = sb("ones", [P, P])
        win = sb("win", [P, WU])
        ws_sb = sb("ws_sb", [P, 2, D])
        wn_sb = sb("wn_sb", [P, 2, D])
        bias_sb = sb("bias_sb", [P, D])
        m1_sb = sb("m1_sb", [P, 4, P])
        m2_sb = sb("m2_sb", [P, P])
        m3_sb = sb("m3_sb", [P, P])
        m4_sb = sb("m4_sb", [P, 2, 4, C])
        up_sb = sb("up_sb", [P, 2, P])
        sc_sb = sb("sc_sb", [P, 2, P])
        lin_sb = sb("lin_sb", [P, 2, 2, P])
        wb_sb = sb("wb_sb", [P, 2, P])
        wc_sb = sb("wc_sb", [P, 9])
        gb_sb = sb("gb_sb", [P, 3, C])
        base0_i = sb("base0_i", [1, NSC], I32)
        base_i = sb("base_i", [1, NSC], I32)
        base0_f = sb("base0_f", [P, NSC])
        base_f = sb("base_f", [P, NSC])
        npass = sb("npass", [1, 2], I32)
        mv = sb("mv", [P, T, 6])
        lnt = sb("lnt", [P, 6, TC])
        rstd = sb("rstd", [P, T])
        nbias = sb("nbias", [P, T])
        eps_sb = sb("eps_sb", [P, 1])
        small = sb("small", [P, 32])
        ps = ctx.enter_context(nc.psum_tensor("ps", [P, 8, 512], F32))

        X = acc[:, 2:4, :].rearrange("p q n -> p (q n)").rearrange("p (t d) -> p t d", d=D)

        s_zero = sem("s_zero")
        s_wts = sem("s_wts")
        s_xin = [sem(f"s_xin{c}") for c in range(NCH)]
        s_tail = sem("s_tail")
        s_tail2 = sem("s_tail2")
        s_chk_in = sem("s_chk_in")
        s_v0 = sem("s_v0")
        s_ln = sem("s_ln")
        s_sq = sem("s_sq")
        s_lnt = sem("s_lnt")
        s_nb = sem("s_nb")
        s_h = sem("s_h")
        s_hst = [sem(f"s_hst{i}") for i in range(2)]
        s_ht_ps = sem("s_ht_ps")
        s_ht = sem("s_ht")
        s_self = sem("s_self")
        s_x1 = sem("s_x1")
        s_id = sem("s_id")
        s_bn = sem("s_bn")
        s_chk = sem("s_chk")
        s_cnt = sem("s_cnt")
        s_first = sem("s_first")
        s_bps = sem("s_bps")

        h_st = work[:, 0:2 * TC * D].rearrange("p (s t d) -> p s t d", s=2, t=TC)
        hT = work[:, 2 * TC * D:2 * TC * D + 2 * D].rearrange("p (s k n) -> p s k n", s=2, k=2)
        chk = acc[0:SROWS, 0, 0:4 * SC].rearrange("p (q e) -> p q e", q=4)
        chk_i = chk.bitcast(I32)
        cst = acc[:, 1, :]
        neg = acc[:, 1, 2048:2056].bitcast(I32)

        wts = [
            (ws_sb[:, :, :], w_self.rearrange("(k p) n -> p k n", p=P)),
            (wn_sb[:, :, :], w_nb.rearrange("(k p) n -> p k n", p=P)),
            (bias_sb[:, :], bias.unsqueeze(0).to_broadcast([P, D])),
        ]
        for g in range(8):
            wts.append((m1_sb[g * R:(g + 1) * R, g // 2, (g % 2) * C:(g % 2 + 1) * C], m1))
        m4v = m4.rearrange("h (b c) -> h b c", b=4)
        for lo in range(2):
            r = slice(lo * C, (lo + 1) * C)
            wts += [(m2_sb[r, r], m2), (m3_sb[r, r], m3),
                    (m4_sb[r, lo, 0:2, :], m4v[:, 0:2, :]), (m4_sb[r, lo, 2, :], m4v[:, 3, :]),
                    (m4_sb[r, lo, 3, :], m4v[:, 2, :])]
            wts += [(up_sb[r, 0, r], (w_up0, w_up1)[lo]), (up_sb[r, 1, r], w_up1),
                    (sc_sb[r, 0, r], (w_sc0, w_sc1)[lo]), (sc_sb[r, 1, r], w_sc1),
                    (wb_sb[r, 0, r], w_b0), (wb_sb[r, 1, r], w_b1),
                    (lin_sb[0:C, 0, lo, r], w_lin0), (lin_sb[C:P, 1, lo, r], w_lin1),
                    (wc_sb[r, 0:5], wc0), (wc_sb[r, 5:9], wc1)]
        for i, v in enumerate((gamma0, beta0, gamma1)):
            wts.append((gb_sb[:, i, :], v.unsqueeze(0).to_broadcast([P, C])))

        def ln_stats(c, step, done):
            st = mv[:, c * TC:(c + 1) * TC, :]
            nc.vector.tensor_tensor(lnt[:, 0, :], st[:, :, 1], st[:, :, 4], ALU.add).then_inc(s_lnt, 1)
            nc.vector.tensor_tensor(lnt[:, 2, :], st[:, :, 2], st[:, :, 5], ALU.add).then_inc(s_lnt, 1)
            step(nc.vector.tensor_tensor(lnt[:, 1, :], st[:, :, 1], st[:, :, 4], ALU.subtract))
            step(nc.vector.tensor_tensor(lnt[:, 3, :], lnt[:, 1, :], lnt[:, 1, :], ALU.mult))
            nc.vector.scalar_tensor_tensor(out=lnt[:, 5, :], in0=lnt[:, 3, :], scalar=float(D) / 4, in1=lnt[:, 2, :],
                                           op0=ALU.mult, op1=ALU.add).then_inc(done, 1)

        def ln_scale(c, step, done):
            t0 = c * TC
            step(nc.vector.reciprocal(rstd[:, t0:t0 + TC], rstd[:, t0:t0 + TC]))
            nc.vector.scalar_tensor_tensor(out=nbias[:, t0:t0 + TC], in0=lnt[:, 0, :], scalar=-0.5,
                                           in1=rstd[:, t0:t0 + TC], op0=ALU.mult, op1=ALU.mult).then_inc(done, 1)

        with nc.Block() as block:
            @block.sync
            def _(sp):
                sp.wait_ge(s_zero, 1)
                for c in range(NCH - 1):
                    sp.dma_start(X[:, c * TC:(c + 1) * TC, :], rows(x, c * TC, TC)).then_inc(s_xin[c], 16)
                c = (NCH - 1) * TC
                sp.dma_start(X[:, c:T - 2, :], rows(x, c, T - 2 - c)).then_inc(s_xin[NCH - 1], 16)
                sp.dma_start(X[0:LAST, T - 2, :], x[(T - 2) * P:N, :]).then_inc(s_xin[NCH - 1], 16)
                full = (SROWS - 1) * 4 * SC
                sp.wait_ge(s_zero, 2)
                sp.dma_start(chk_i[0:SROWS - 1, :, :], dst[0:full].rearrange("(p q e) -> p q e", q=4, e=SC)).then_inc(s_chk_in, 16)
                left = E - full
                q = left // SC
                r = left % SC
                sp.dma_start(chk_i[SROWS - 1:SROWS, 0:q, :], dst[full:full + q * SC].rearrange("(o q e) -> o q e", o=1, q=q)).then_inc(s_chk_in, 16)
                for i in (q, q + 1):
                    sp.dma_start(chk_i[SROWS - 1:SROWS, i, 0:r], dst[E - r:E].unsqueeze(0)).then_inc(s_chk_in, 16)
                    sp.dma_start(chk_i[SROWS - 1:SROWS, i, r:SC], dst[E - (SC - r):E].unsqueeze(0)).then_inc(s_chk_in, 16)
                with nc.allow_non_contiguous_dma(reason="one number in 512"):
                    sp.dma_start(base0_i[:, 0:NSC - 1], dst[0:(NSC - 2) * SC + 1:SC].unsqueeze(0)).then_inc(s_chk_in, 16)
                sp.dma_start(base0_i[:, NSC - 1:NSC], dst[E0:E0 + 1].unsqueeze(0)).then_inc(s_chk_in, 16)
                for c in range(NCH):
                    sp.wait_ge(s_h, (c + 1) * TC)
                    sp.dma_start(rows(h_tab, c * TC, TC), h_st[:, c % 2, :, :]).then_inc(s_hst[c % 2], 16)
                sp.wait_ge(s_hst[0], 16 * 3)
                sp.wait_ge(s_hst[1], 16 * 2)

            @block.gpsimd
            def _(pool):
                nc.gpsimd.iota(win_i := mlp[:, 0:WU].bitcast(I32), pattern=[[1, WU]], base=0, channel_multiplier=0).then_inc(s_id, 1)
                nc.gpsimd.memset(ident[:, :], 0.0).then_inc(s_id, 1)
                nc.gpsimd.memset(ones[:, :], 1.0).then_inc(s_id, 1)
                pool.wait_ge(s_id, 3)
                nc.gpsimd.affine_select(out=ident[:, :], in_=ident[:, :], compare_op=ALU.not_equal, fill=1.0, base=0,
                                        pattern=[[-1, P]], channel_multiplier=1).then_inc(s_id, 1)
                nc.gpsimd.tensor_copy(win[:, :], win_i).then_inc(s_id, 1)


            @block.scalar
            def _(act):
                act.wait_ge(s_zero, 2)
                for to, of in wts:
                    act.dma_start(to, of).then_inc(s_wts, 16)
                for tab, n in ((src_tail, 1), (w_tail, 1), (a4_tail, 4), (a16_tail, R)):
                    flat = tab if len(tab.shape) == 1 else tab.rearrange("e f -> (e f)")
                    fill = cst[:, 0:8 * n].bitcast(I32) if n == 1 and tab is src_tail else cst[:, 0:8 * n]
                    act.dma_start(flat.rearrange("(p f) -> p f", p=P), fill).then_inc(s_tail, 16)
                act.dma_start(dst_tail.rearrange("(p f) -> p f", p=P), neg).then_inc(s_tail, 16)
                act.wait_ge(s_tail, 16 * 5)
                for tab, of in ((src_tail, src), (dst_tail, dst), (w_tail, weight), (a4_tail, attr4), (a16_tail, attr16)):
                    if len(tab.shape) == 1:
                        act.dma_start(tab[0:ETAIL].unsqueeze(0), of[E0:E].unsqueeze(0)).then_inc(s_tail2, 16)
                    else:
                        act.dma_start(tab[0:ETAIL, :], of[E0:E, :]).then_inc(s_tail2, 16)
                for c in range(NCH):
                    t0 = c * TC
                    act.wait_ge(s_ln, c + 1)
                    nc.scalar.activation(rstd[:, t0:t0 + TC], lnt[:, 5, :], ACT.Sqrt, bias=eps_sb[:, 0:1],
                                         scale=1.0 / D).then_inc(s_sq, 1)
                    act.wait_ge(s_nb, c + 1)
                    if c >= 2:
                        act.wait_ge(s_hst[c % 2], 16 * (c // 2))
                        act.wait_ge(s_ht_ps, (c - 1) * TC)
                    with act.Fori(0, TC) as i:
                        nc.scalar.activation(row(h_st[:, c % 2, ds(i, 1), :]), row(X[:, ds(i + t0, 1), :]), ACT.Relu,
                                             bias=nbias[:, ds(i + t0, 1)], scale=rstd[:, ds(i + t0, 1)]).then_inc(s_h, 1)
                act.wait_ge(s_wts, 16 * len(wts))
                act.wait_ge(s_tail2, 16 * 5)

            @block.vector
            def _(dve):
                count = [0]

                def step(ins):
                    count[0] += 1
                    ins.then_inc(s_v0, 1)
                    dve.wait_ge(s_v0, count[0])

                step(nc.vector.memset(X[:, T - 2:T, :], 0.0))
                step(nc.vector.memset(eps_sb[:, :], EPS))
                dve.sem_inc(s_zero, 1)
                for tile in (m1_sb, m2_sb, m3_sb, m4_sb, up_sb, sc_sb, lin_sb, wb_sb):
                    nc.vector.memset(tile[:], 0.0).then_inc(s_v0, 1)
                nc.vector.memset(cst[:, 0:8 * R], 0.0).then_inc(s_v0, 1)
                count[0] += 9
                step(nc.vector.memset(neg, -1))
                dve.sem_inc(s_zero, 1)

                def add_self(c):
                    t0 = c * TC
                    with dve.Fori(0, TC // 2) as i:
                        for s in range(2):
                            dve.wait_ge(s_ht_ps, i * 2 + (t0 + s + 1))
                            dve.wait_ge(s_self, i * 2 + t0)
                            nc.vector.tensor_copy(hT[:, s, :, :].rearrange("p k n -> p (k n)"), ps[:, s, 0:D]).then_inc(s_ht, 1)
                        for s in range(2):
                            dve.wait_ge(s_self, i * 2 + (t0 + s + 1))
                            xt = row(X[:, ds(i * 2 + (t0 + s), 1), :])
                            nc.vector.tensor_tensor(xt, xt, ps[:, 2 + s, 0:D], ALU.add).then_inc(s_x1, 1)

                for c in range(NCH):
                    t0 = c * TC
                    dve.wait_ge(s_xin[c], 16 * (1 + (c == NCH - 1)))
                    with dve.Fori(0, TC) as i:
                        nc.vector.bn_stats(row(mv[:, ds(i + t0, 1), :]), row(X[:, ds(i + t0, 1), :])).then_inc(s_bn, 1)
                    dve.wait_ge(s_bn, t0 + TC)
                    ln_stats(c, step, s_ln)
                    dve.wait_ge(s_sq, c + 1)
                    ln_scale(c, step, s_nb)
                    if c >= 1:
                        add_self(c - 1)
                add_self(NCH - 1)
                dve.wait_ge(s_x1, T)
                dve.wait_ge(s_h, T)
                dve.wait_ge(s_wts, 16 * len(wts))
                nc.vector.tensor_tensor(X[:, 0:T - 2, :], X[:, 0:T - 2, :], bc(bias_sb[:, :], 1, T - 2), ALU.add).then_inc(s_v0, 1)
                nc.vector.tensor_tensor(X[0:LAST, T - 2, :], X[0:LAST, T - 2, :], bias_sb[0:LAST, :], ALU.add).then_inc(s_v0, 1)
                nc.vector.tensor_scalar(m4_sb[:, :, 2, :], m4_sb[:, :, 2, :], 3.0 ** -0.5, None, ALU.mult).then_inc(s_v0, 1)
                count[0] += 3

                dve.wait_ge(s_chk_in, 16 * 8)
                first, high, low, bad = (small[0:SROWS, 4 * k:4 * k + 4] for k in range(4))
                bad_u = small[0:SROWS, 16:18]
                step(nc.vector.tensor_copy(first, chk_i[:, :, 0]))
                step(nc.vector.tensor_reduce(high, chk_i, AX_X, ALU.max))
                step(nc.vector.tensor_reduce(low, chk_i, AX_X, ALU.min))
                step(nc.vector.tensor_tensor(bad_u, high[:, 1:4:2], first[:, 0:4:2], ALU.subtract))
                step(nc.vector.tensor_tensor(small[0:SROWS, 18:20], first[:, 0:4:2], low[:, 1:4:2], ALU.subtract))
                step(nc.vector.tensor_scalar(bad_u, bad_u, float(WU), None, ALU.is_ge))
                step(nc.vector.tensor_scalar(small[0:SROWS, 18:20], small[0:SROWS, 18:20], 0.0, None, ALU.is_gt))
                step(nc.vector.tensor_tensor(bad_u, bad_u, small[0:SROWS, 18:20], ALU.add))
                step(nc.vector.tensor_tensor(high, high, first, ALU.subtract))
                step(nc.vector.tensor_tensor(low, first, low, ALU.subtract))
                step(nc.vector.tensor_scalar(high, high, float(W), None, ALU.is_ge))
                step(nc.vector.tensor_scalar(low, low, 0.0, None, ALU.is_gt))
                step(nc.vector.tensor_tensor(bad, high, low, ALU.add))
                step(nc.vector.tensor_reduce(small[0:SROWS, 21:22], bad, AX_X, ALU.add))
                step(nc.vector.tensor_reduce(small[0:SROWS, 20:21], bad_u, AX_X, ALU.add))
                nc.vector.tensor_tensor(small[0:SROWS, 20:21], small[0:SROWS, 20:21], small[0:SROWS, 21:22], ALU.add).then_inc(s_chk, 1)
                dve.wait_ge(s_cnt, 1)
                step(nc.vector.tensor_scalar(small[:, 22:24], ps[:, 4, 0:2], 1.0, None, ALU.min))
                step(nc.vector.tensor_scalar(small[:, 24:26], small[:, 22:24], -1.0, 1.0, ALU.mult, ALU.add))
                for layer, w in enumerate((WU, W)):
                    step(nc.vector.tensor_scalar(small[0:1, 26 + layer:27 + layer], small[0:1, 22 + layer:23 + layer],
                                                 float(-(-N // w) - 1), 1.0, ALU.mult, ALU.add))
                step(nc.vector.tensor_copy(npass[:, :], small[0:1, 26:28]))
                nc.vector.tensor_copy(base_f[0:1, :], base0_i[:, :]).then_inc(s_first, 1)
                dve.wait_ge(s_bps, 1)
                step(nc.vector.tensor_copy(base0_f[:, :], ps[:, 5, 0:NSC]))
                dve.wait_ge(s_tail, 16 * 5)
                step(nc.vector.memset(acc[:, 0:2, :], 0.0))

            @block.tensor
            def _(pe):
                pe.wait_ge(s_id, 5)
                pe.wait_ge(s_wts, 16 * len(wts))
                for c in range(NCH):
                    t0 = c * TC
                    for i in range(TC // 2):
                        for s in range(2):
                            pe.wait_ge(s_h, i * 2 + (t0 + s + 1))
                            pe.wait_ge(s_ht, i * 2 + t0)
                            for k in range(2):
                                mm = nc.tensor.transpose(ps[:, s, k * P:(k + 1) * P],
                                                         row(h_st[:, c % 2, ds(i * 2 + s, 1), k * P:(k + 1) * P]), ident[:, :])
                            mm.then_inc(s_ht_ps, 1)
                        for s in range(2):
                            pe.wait_ge(s_ht, i * 2 + (t0 + s + 1))
                            pe.wait_ge(s_x1, i * 2 + t0)
                            for k in range(2):
                                mm = nc.tensor.matmul(ps[:, 2 + s, 0:D], hT[:, s, k, :], ws_sb[:, k, :],
                                                      start=(k == 0), stop=(k == 1))
                            mm.then_inc(s_self, 1)
                pe.wait_ge(s_chk, 1)
                nc.tensor.matmul(ps[:, 4, 0:2], ones[0:SROWS, :], small[0:SROWS, 20:22], start=True, stop=True).then_inc(s_cnt, 1)
                pe.wait_ge(s_first, 1)
                nc.tensor.matmul(ps[:, 5, 0:NSC], ones[0:1, :], base_f[0:1, :], start=True, stop=True).then_inc(s_bps, 1)

        rows_g = work[:, 0:2 * 8 * D].rearrange("p (s k d) -> p s k d", s=2, k=8)
        prod = work[:, 4096:8192].rearrange("p (j k b c) -> p j k b c", j=2, k=G, b=8)
        onehot = work[:, 8192:10240].rearrange("p (s k a w) -> p s k a w", s=2, k=8, a=4)
        hot_u = work[:, 8192:10240].rearrange("p (s k w) -> p s k w", s=2, k=8)
        eq = work[:, 10240:10496].rearrange("p (k w) -> p k w", w=W)
        eq_u = mlp[:, 1536:2560].rearrange("p (k w) -> p k w", w=WU)
        rel = work[:, 10496:10504]
        idx = work[:, 10504:10520].bitcast(I32).rearrange("p (s k) -> p s k", s=2)
        dsti = work[:, 10520:10536].bitcast(I32).rearrange("p (s k) -> p s k", s=2)
        wgt = work[:, 10536:10552].rearrange("p (s k) -> p s k", s=2)
        sh = work[:, 10560:10624].rearrange("p (s k) -> p s k", s=2)
        r3 = work[:, 10624:11648].rearrange("p (s n) -> p s n", s=2)
        attr = mlp[:, 0:256].rearrange("p (s n) -> p s n", s=2)
        attr_t = mlp[:, 256:384]
        r1 = mlp[:, 512:1024]
        r2 = mlp[:, 1024:1536]

        def edge_syms(ph):
            return dict(
                idx=[sem(f"idx{ph}_{s}") for s in range(2)],
                edge=[sem(f"edge{ph}_{s}") for s in range(2)],
                rad=[sem(f"rad{ph}_{s}") for s in range(2)],
                rad_used=[sem(f"rad_used{ph}_{s}") for s in range(2)],
                got=[[sem(f"got{ph}_{s}{j}") for j in range(2)] for s in range(2)],
                rel=sem(f"rel{ph}"), eq=sem(f"eq{ph}"),
                hot=[sem(f"hot{ph}_{s}") for s in range(2)],
                summed=[[sem(f"summed{ph}_{s}{j}") for j in range(2)] for s in range(2)],
                added=[sem(f"added{ph}_{j}") for j in range(2)],
                base=sem(f"base{ph}"),
            )

        def passes(eng, layer):
            return eng.value_load(npass[0:1, layer:layer + 1], min_val=1, max_val=-(-N // (WU, W)[layer]))

        def load_units(sp, layer, S, edge_views, rad_of, rad_to):
            def load(u, pz, k, s):
                use = pz * ROUNDS + k
                for j in range(2):
                    sp.wait_ge(S["got"][s][j], use * (16 * G))
                sp.dma_start(idx[:, s, :].rearrange("p (j g) -> p j g", g=G), unit_of(src_u, u)).then_inc(S["idx"][s], 16)
                sp.wait_ge(S["hot"][s], use)
                for to, view in edge_views:
                    sp.dma_start(to[:, s, :].rearrange("p (j g) -> p j g", j=2), unit_of(view, u)).then_inc(S["edge"][s], 16)
                sp.wait_ge(S["rad_used"][s], use)
                sp.dma_start(rad_to(s), rad_of(u)).then_inc(S["rad"][s], 16)

            with sp.Fori(0, passes(sp, layer)) as pz:
                with sp.Fori(0, ROUNDS - 1) as k:
                    for s in range(2):
                        load(k * 2 + s, pz, k, s)
                for s in range(2):
                    load(NU - 2 + s, pz, ROUNDS - 1, s)

        def gather_units(pool, layer, S, table, taken):
            with pool.Fori(0, passes(pool, layer)) as pz:
                with pool.Fori(0, ROUNDS) as k:
                    for s in range(2):
                        use = pz * ROUNDS + k
                        pool.wait_ge(taken[s], use)
                        pool.wait_ge(S["idx"][s], use * 16 + 16)
                        pool.sem_inc(s_turn, 1)
                        for j in range(2):
                            for g in range(G):
                                q = j * G + g
                                pool.indirect_dma_start(
                                    out=rows_g[:, s, q, :], out_offset=None, in_=table,
                                    in_offset=bass.IndirectOffsetOnAxis(ap=idx[:, s, q:q + 1], axis=0),
                                ).then_inc(S["got"][s][j], 16)

        def hot_steps(dve, S, u, use, s, layer):
            def step_rel():
                dve.wait_ge(S["edge"][s], use * 32 + 32)
                base = (bc(base_f[:, ds(u * 2, 1)], 2, G).to_broadcast([P, 2, G]), bc(base_f[:, ds(u * 2, 2)], 2, G))[layer]
                nc.vector.tensor_tensor(rel.rearrange("p (j g) -> p j g", j=2), dsti[:, s, :].rearrange("p (j g) -> p j g", j=2),
                                        base, ALU.subtract).then_inc(S["rel"], 1)

            def step_eq(gu):
                to, w = ((eq_u, WU), (eq, W))[layer]
                dve.wait_ge(S["rel"], gu + 1)
                nc.vector.tensor_tensor(to, bc(win[:, 0:w], 1, 8), bc(rel, 2, w), ALU.is_equal).then_inc(S["eq"], 1)

            def step_hot(gu):
                dve.wait_ge(S["eq"], gu + 1)
                dve.wait_ge(S["summed"][s][1], use)
                if layer == 0:
                    nc.vector.tensor_tensor(hot_u[:, s, :, :], eq_u, bc(wgt[:, s, :], 2, WU), ALU.mult).then_inc(S["hot"][s], 1)
                else:
                    for j in range(2):
                        v = sh[:, s, 16 * j:16 * j + 16].rearrange("p (k a) -> p k a", a=4)
                        last = nc.vector.tensor_tensor(onehot[:, s, 4 * j:4 * j + 4, :, :], bc(eq[:, 4 * j:4 * j + 4, :], 2, 4),
                                                       bc(v, 3, W), ALU.mult)
                    last.then_inc(S["hot"][s], 1)

            return step_rel, step_eq, step_hot

        def set_base(dve, S, layer, pz):
            w = float((WU, W)[layer])
            nc.vector.tensor_scalar(base_f[:, :], base_f[:, :], w, None, ALU.add).then_inc(S["base"], 1)
            nc.vector.tensor_scalar(base_i[:, :], base_i[:, :], w, None, ALU.add).then_inc(S["base"], 1)
            dve.wait_ge(S["base"], pz * 2 + 4)

        def first_base(dve, S, layer):
            nc.vector.tensor_scalar(base_f[:, :], base0_f[:, :], small[:, 24 + layer:25 + layer], None, ALU.mult).then_inc(S["base"], 1)
            dve.wait_ge(S["base"], 1)
            nc.vector.tensor_copy(base_i[:, :], base_f[0:1, :]).then_inc(S["base"], 1)
            dve.wait_ge(S["base"], 2)

        def add_window(dve, S, u, use, gu, s, j, q):
            b = dve.value_load(base_i[0:1, ds(u * 2 + j, 1)], min_val=0, max_val=N - 1)
            dve.wait_ge(S["summed"][s][j], use + 1)
            dve.wait_ge(S["added"][1 - j], gu + j)
            to = acc[:, 0:q, ds(b, W)]
            nc.vector.tensor_tensor(to, to, ps[:, 6 + j, 0:q * W].rearrange("p (q w) -> p q w", q=q), ALU.add).then_inc(S["added"][j], 1)

        s_turn = sem("s_turn")

        S = edge_syms(1)
        at_ready, z1_ready, r1_ready, z2_ready, r2_ready, z3_ready, r3_ready = (
            sem(n) for n in ("at_ready", "z1_ready", "r1_ready", "z2_ready", "r2_ready", "z3_ready", "r3_ready"))
        r3_stored = [sem(f"r3_stored{s}") for s in range(2)]

        with nc.Block() as block:
            @block.sync
            def _(sp):
                load_units(sp, 0, S, ((dsti, dst_u), (wgt, w_u)), lambda u: unit_of(a16_u, u),
                           lambda s: attr[:, s, :].rearrange("p (j n) -> p j n", j=2))

            @block.gpsimd
            def _(pool):
                gather_units(pool, 0, S, h_tab, [S["summed"][s][1] for s in range(2)])

            @block.vector
            def _(dve):
                first_base(dve, S, 0)
                with dve.Fori(0, passes(dve, 0)) as pz:
                    def hot(u, use, gu, s):
                        for part, arg in zip(hot_steps(dve, S, u, use, s, 0), ((), (gu,), (gu,))):
                            part(*arg)

                    def unit(k, s, last=False):
                        use, gu = pz * ROUNDS + k, pz * NU + k * 2 + s
                        if not last:
                            hot(k * 2 + s + 1, use + s, gu + 1, 1 - s)
                            turned(gu + 1, use + s, 1 - s)
                        b = dve.value_load(base_i[0:1, ds(k * 4 + 2 * s, 1)], min_val=0, max_val=N - 1)
                        dve.wait_ge(S["summed"][s][1], use + 1)
                        dve.wait_ge(S["added"][1 - s], use + s)
                        to = acc[:, 0:2, ds(b, WU)]
                        nc.vector.tensor_tensor(to, to, ps[:, 6 + s, 0:2 * WU].rearrange("p (h w) -> p h w", h=2),
                                                ALU.add).then_inc(S["added"][s], 1)

                    def turned(gu, use, s):
                        dve.wait_ge(S["rad_used"][s], use + 1)
                        dve.wait_ge(z1_ready, gu)
                        nc.vector.tensor_copy(attr_t, ps[:, 0, 0:P]).then_inc(at_ready, 1)

                    hot(0, pz * ROUNDS, pz * NU, 0)
                    turned(pz * NU, pz * ROUNDS, 0)
                    with dve.Fori(0, ROUNDS - 1) as k:
                        for s in range(2):
                            unit(k, s)
                    for s in range(2):
                        unit(ROUNDS - 1, s, last=(s == 1))
                    dve.wait_ge(S["added"][1], pz * ROUNDS + ROUNDS)
                    set_base(dve, S, 0, pz)

            @block.tensor
            def _(pe):
                def turn(s, use, gu):
                    pe.wait_ge(S["rad"][s], use * 16 + 16)
                    pe.wait_ge(at_ready, gu)
                    nc.tensor.transpose(ps[:, 0, 0:P], attr[:, s, :], ident[:, :]).then_inc(S["rad_used"][s], 1)

                def sums(s, j, use):
                    pe.wait_ge(S["got"][s][j], use * (16 * G) + 16 * G)
                    if j == 0:
                        pe.wait_ge(S["hot"][s], use + 1)
                        pe.wait_ge(S["added"][s], use)
                    for g in range(G):
                        q = j * G + g
                        for half in range(2):
                            mm = nc.tensor.matmul(ps[:, 6 + s, half * WU:(half + 1) * WU], rows_g[:, s, q, half * P:(half + 1) * P],
                                                  hot_u[:, s, q, :], start=(q == 0 and half == 0), stop=(q == 7 and half == 1))
                    mm.then_inc(S["summed"][s][j], 1)

                def unit(k, s, last=False):
                    use, gu = pz * ROUNDS + k, pz * NU + k * 2 + s
                    pe.wait_ge(at_ready, gu + 1)
                    pe.wait_ge(r1_ready, gu)
                    for q in range(4):
                        mm = nc.tensor.matmul(ps[:, 1, q * P:(q + 1) * P], m1_sb[:, q, :], attr_t, start=True, stop=True)
                    mm.then_inc(z1_ready, 1)
                    sums(s, 0, use)
                    if not last:
                        turn(1 - s, use + s, gu + 1)
                    pe.wait_ge(r1_ready, gu + 1)
                    pe.wait_ge(r2_ready, gu)
                    nc.tensor.matmul(ps[:, 2, :], m2_sb[:, :], r1, start=True, stop=True).then_inc(z2_ready, 1)
                    sums(s, 1, use)
                    pe.wait_ge(r2_ready, gu + 1)
                    pe.wait_ge(r3_ready, gu)
                    nc.tensor.matmul(ps[:, 3, :], m3_sb[:, :], r2, start=True, stop=True).then_inc(z3_ready, 1)

                with pe.Fori(0, passes(pe, 0)) as pz:
                    turn(0, pz * ROUNDS, pz * NU)
                    with pe.Fori(0, ROUNDS - 1) as k:
                        for s in range(2):
                            unit(k, s)
                    for s in range(2):
                        unit(ROUNDS - 1, s, last=(s == 1))

            @block.scalar
            def _(act):
                with act.Fori(0, passes(act, 0)) as pz:
                    with act.Fori(0, ROUNDS) as k:
                        for s in range(2):
                            use = pz * ROUNDS + k
                            gu = pz * NU + k * 2 + s
                            act.wait_ge(z1_ready, gu + 1)
                            act.wait_ge(z2_ready, gu)
                            nc.scalar.activation(r1, ps[:, 1, :], ACT.Silu).then_inc(r1_ready, 1)
                            act.wait_ge(z2_ready, gu + 1)
                            act.wait_ge(z3_ready, gu)
                            nc.scalar.activation(r2, ps[:, 2, :], ACT.Silu).then_inc(r2_ready, 1)
                            act.wait_ge(z3_ready, gu + 1)
                            act.wait_ge(r3_stored[s], use * 16)
                            nc.scalar.activation(r3[:, s, :], ps[:, 3, :], ACT.Silu).then_inc(r3_ready, 1)
                            act.wait_ge(r3_ready, gu + 1)
                            act.dma_start(r3_tab[ds(k * 2 + s, 1), :, :].rearrange("o p n -> (o p) n"), r3[:, s, :]).then_inc(r3_stored[s], 16)
                    for s in range(2):
                        act.wait_ge(r3_stored[s], pz * (16 * ROUNDS) + 16 * ROUNDS)

        t_agg = sem("t_agg")
        t_x2 = sem("t_x2")
        t_bn, t_v, t_ln, t_sq, t_nb = (sem(n) for n in ("t_bn", "t_v", "t_ln", "t_sq", "t_nb"))
        t_h = sem("t_h")
        t_tp = sem("t_tp")
        t_ht = sem("t_ht")
        t_up_ps = sem("t_up_ps")
        t_up = sem("t_up")
        t_st = [[sem(f"t_st{i}{s}") for s in range(2)] for i in range(2)]
        t_x2st = sem("t_x2st")

        stage = work[:, :].rearrange("p (a s t d) -> p a s t d", a=3, s=2, t=TC)
        h2p, h2t, ups = stage[:, 0], stage[:, 1], stage[:, 2]

        with nc.Block() as block:
            def store(sp, c):
                sp.wait_ge(t_ht, (c + 1) * TC)
                sp.dma_start(h2t_tab[:, c * TC * D:(c + 1) * TC * D],
                             h2t[:, c % 2].rearrange("p t d -> p (t d)")).then_inc(t_st[0][c % 2], 16)
                sp.wait_ge(t_up, (c + 1) * TC)
                sp.dma_start(rows(up_tab, c * TC, TC), ups[:, c % 2]).then_inc(t_st[1][c % 2], 16)

            @block.sync
            def _(sp):
                for c in range(NCH):
                    sp.wait_ge(t_x2, (c + 1) * TC)
                    sp.dma_start(rows(x2_tab, c * TC, TC), X[:, c * TC:(c + 1) * TC, :]).then_inc(t_x2st, 16)
                    if c >= 1:
                        store(sp, c - 1)
                store(sp, NCH - 1)
                sp.wait_ge(t_x2st, 16 * NCH)
                for i in range(2):
                    sp.wait_ge(t_st[i][0], 16 * 3)
                    sp.wait_ge(t_st[i][1], 16 * 2)

            @block.tensor
            def _(pe):
                def neighbors(c):
                    for i in range(TC // 2):
                        for s in range(2):
                            t = i * 2 + (c * TC + s)
                            pe.wait_ge(t_x2, i * 2 + c * TC)
                            for k in range(2):
                                mm = nc.tensor.matmul(ps[:, s, 0:D], acc[:, k, ds(t * P, P)], wn_sb[:, k, :],
                                                      start=(k == 0), stop=(k == 1))
                            mm.then_inc(t_agg, 1)

                neighbors(0)
                for c in range(NCH):
                    if c + 1 < NCH:
                        neighbors(c + 1)
                    for i in range(TC // 2):
                        for s in range(2):
                            t = i * 2 + (c * TC + s)
                            pe.wait_ge(t_h, t * 2 + 2)
                            pe.wait_ge(t_ht, i * 2 + c * TC)
                            for k in range(2):
                                mm = nc.tensor.transpose(ps[:, 2 + s, k * P:(k + 1) * P],
                                                         row(h2p[:, c % 2, ds(i * 2 + s, 1), k * P:(k + 1) * P]), ident[:, :])
                            mm.then_inc(t_tp, 1)
                    for i in range(TC // 2):
                        for s in range(2):
                            t = i * 2 + (c * TC + s)
                            pe.wait_ge(t_ht, t + 1)
                            pe.wait_ge(t_up, i * 2 + c * TC)
                            for k in range(2):
                                mm = nc.tensor.matmul(ps[:, 4 + s, k * P:(k + 1) * P],
                                                      row(h2t[:, c % 2, ds(i * 2 + s, 1), k * P:(k + 1) * P]), up_sb[:, k, :],
                                                      start=True, stop=True)
                            mm.then_inc(t_up_ps, 1)

            @block.vector
            def _(dve):
                count = [0]

                def step(ins):
                    count[0] += 1
                    ins.then_inc(t_v, 1)
                    dve.wait_ge(t_v, count[0])

                def x2_of(c):
                    with dve.Fori(0, TC // 2) as i:
                        for s in range(2):
                            t = i * 2 + (c * TC + s)
                            dve.wait_ge(t_agg, t + 1)
                            nc.vector.tensor_tensor(row(X[:, ds(t, 1), :]), row(X[:, ds(t, 1), :]), ps[:, s, 0:D], ALU.add).then_inc(t_x2, 1)
                    with dve.Fori(0, TC) as i:
                        dve.wait_ge(t_x2, i + (c * TC + 1))
                        nc.vector.bn_stats(row(mv[:, ds(i + c * TC, 1), :]), row(X[:, ds(i + c * TC, 1), :])).then_inc(t_bn, 1)
                    dve.wait_ge(t_bn, (c + 1) * TC)
                    ln_stats(c, step, t_ln)
                    dve.wait_ge(t_sq, c + 1)
                    ln_scale(c, step, t_nb)

                def ups_of(c):
                    if c >= 2:
                        dve.wait_ge(t_st[1][c % 2], 16 * (c // 2))
                    with dve.Fori(0, TC // 2) as i:
                        for s in range(2):
                            dve.wait_ge(t_up_ps, i * 2 + (c * TC + s + 1))
                            nc.vector.tensor_copy(row(ups[:, c % 2, ds(i * 2 + s, 1), :]), ps[:, 4 + s, 0:D]).then_inc(t_up, 1)

                x2_of(0)
                for c in range(NCH):
                    if c + 1 < NCH:
                        x2_of(c + 1)
                    ups_of(c)

            @block.scalar
            def _(act):
                for c in range(NCH):
                    t0 = c * TC
                    act.wait_ge(t_ln, c + 1)
                    nc.scalar.activation(rstd[:, t0:t0 + TC], lnt[:, 5, :], ACT.Sqrt, bias=eps_sb[:, 0:1],
                                         scale=1.0 / D).then_inc(t_sq, 1)
                    act.wait_ge(t_nb, c + 1)
                    if c >= 2:
                        act.wait_ge(t_tp, (c - 1) * TC)
                        act.wait_ge(t_st[0][c % 2], 16 * (c // 2))
                        act.wait_ge(t_up_ps, (c - 1) * TC)
                    with act.Fori(0, TC) as i:
                        xt = X[:, ds(i + t0, 1), :]
                        ht = h2p[:, c % 2, ds(i, 1), :]
                        how = dict(bias=nbias[:, ds(i + t0, 1)], scale=rstd[:, ds(i + t0, 1)])
                        nc.scalar.activation(row(ht[:, :, 0:C]), row(xt[:, :, 0:C]), ACT.Relu, **how).then_inc(t_h, 1)
                        nc.scalar.activation(ht[:, :, C:D].rearrange("p o (v c) -> p (o c) v", v=3),
                                             xt[:, :, C:D].rearrange("p o (c v) -> p (o c) v", v=3), ACT.Relu, **how).then_inc(t_h, 1)
                    with act.Fori(0, TC // 2) as i:
                        for s in range(2):
                            act.wait_ge(t_tp, i * 2 + (t0 + s + 1))
                            nc.scalar.activation(row(h2t[:, c % 2, ds(i * 2 + s, 1), :]), ps[:, 2 + s, 0:D], ACT.Copy).then_inc(t_ht, 1)

        S3 = edge_syms(3)
        s_clear = sem("s_clear")
        t_ready = [[sem(f"t_ready{s}{j}") for j in range(2)] for s in range(2)]
        S3["rad_used"] = [t_ready[s][1] for s in range(2)]
        prods = [[sem(f"prods{s}{j}") for j in range(2)] for s in range(2)]

        with nc.Block() as block:
            @block.sync
            def _(sp):
                load_units(sp, 1, S3, ((dsti, dst_u), (sh, a4_u)),
                           lambda u: r3_tab[ds(u, 1), :, :].rearrange("o p n -> (o p) n"), lambda s: r3[:, s, :])

            @block.gpsimd
            def _(pool):
                gather_units(pool, 1, S3, up_tab, [prods[s][1] for s in range(2)])

            @block.tensor
            def _(pe):
                def radial(s, j, use):
                    if j == 0:
                        pe.wait_ge(S3["rad"][s], use * 16 + 16)
                    pe.wait_ge(prods[1 - s][j], use + s)
                    for g in range(G):
                        n = 2 * j + g // 2
                        mm = nc.tensor.matmul(ps[:, 2 * j + g // 2, (g % 2) * D:(g % 2 + 1) * D], r3[:, s, n * P:(n + 1) * P],
                                              m4_sb[:, g % 2, :, :].rearrange("p b c -> p (b c)"), start=True, stop=True)
                    mm.then_inc(t_ready[s][j], 1)

                def sums(s, j, use, gu):
                    pe.wait_ge(prods[s][j], use + 1)
                    if j == 0:
                        pe.wait_ge(S3["hot"][s], use + 1)
                    pe.wait_ge(S3["added"][j], gu)
                    to = ps[:, 6 + j, 0:4 * W].rearrange("p (q w) -> p q w", q=4)
                    for g in range(G):
                        hot = onehot[:, s, j * G + g, :, :]
                        pair = prod[:, j, g, :, :].rearrange("p (b two) c -> p b (two c)", two=2)
                        nc.tensor.matmul(to.rearrange("p q w -> p (q w)"), pair[:, 0, :], hot.rearrange("p a w -> p (a w)"),
                                         start=(g == 0), stop=False)
                        for v in range(1, 4):
                            mm = nc.tensor.matmul(to[:, 0:v + 1:v, :], pair[:, v, :], hot[:, v::-v, :],
                                                  start=False, stop=(g == G - 1 and v == 3))
                    mm.then_inc(S3["summed"][s][j], 1)

                with pe.Fori(0, passes(pe, 1)) as pz:
                    radial(0, 0, pz * ROUNDS)
                    with pe.Fori(0, ROUNDS - 1) as k:
                        for s in range(2):
                            for j in range(2):
                                use, gu = pz * ROUNDS + k, pz * NU + k * 2 + s
                                s1, j1 = (s, 1) if j == 0 else (1 - s, 0)
                                radial(s1, j1, use + (s if j else 0))
                                sums(s, j, use, gu)
                    for s in range(2):
                        for j in range(2):
                            use, gu = pz * ROUNDS + (ROUNDS - 1), pz * NU + (NU - 2 + s)
                            if (s, j) != (1, 1):
                                s1, j1 = (s, 1) if j == 0 else (1 - s, 0)
                                radial(s1, j1, use + (s if j else 0))
                            sums(s, j, use, gu)

            @block.vector
            def _(dve):
                nc.vector.memset(acc[:, :, :], 0.0).then_inc(s_clear, 1)
                first_base(dve, S3, 1)
                dve.wait_ge(s_clear, 1)
                with dve.Fori(0, passes(dve, 1)) as pz:
                    def products(s, j, use):
                        dve.wait_ge(t_ready[s][j], use + 1)
                        dve.wait_ge(S3["got"][s][j], use * (16 * G) + 16 * G)
                        dve.wait_ge(S3["summed"][1 - s][j], use + s)
                        t = ps[:, 2 * j:2 * j + 2, :].rearrange("p a (g b c) -> p (a g) b c", g=2, b=4)
                        up = rows_g[:, s, j * G:(j + 1) * G, :].rearrange("p g (b c) -> p g b c", b=4)
                        for v in range(4):
                            b = 0 if v == 0 else 2
                            ins = nc.vector.tensor_tensor(prod[:, j, :, 2 * v:2 * v + 2, :], t[:, :, b:b + 2, :],
                                                          bc(up[:, :, v, :], 2, 2), ALU.mult)
                        ins.then_inc(prods[s][j], 1)

                    def unit(k, s, first=False, last=False):
                        use, gu = pz * ROUNDS + k, pz * NU + k * 2 + s
                        if not last:
                            rel_, eq_, hot_ = hot_steps(dve, S3, k * 2 + s + 1, use + s, 1 - s, 1)
                            rel_()
                        products(s, 0, use)
                        if not last:
                            eq_(gu + 1)
                        if not first:
                            add_window(dve, S3, k * 2 + s - 1, use - (1 - s), gu - 1, 1 - s, 1, 4)
                        products(s, 1, use)
                        if not last:
                            hot_(gu + 1)
                        add_window(dve, S3, k * 2 + s, use, gu, s, 0, 4)

                    rel_, eq_, hot_ = hot_steps(dve, S3, 0, pz * ROUNDS, 0, 1)
                    rel_()
                    eq_(pz * NU)
                    hot_(pz * NU)
                    unit(0, 0, first=True)
                    unit(0, 1)
                    with dve.Fori(1, ROUNDS - 1) as k:
                        for s in range(2):
                            unit(k, s)
                    unit(ROUNDS - 1, 0)
                    unit(ROUNDS - 1, 1, last=True)
                    add_window(dve, S3, NU - 1, pz * ROUNDS + (ROUNDS - 1), pz * NU + (NU - 1), 1, 1, 4)
                    dve.wait_ge(S3["added"][1], pz * NU + NU)
                    set_base(dve, S3, 1, pz)

        X2 = work[:, 0:T * D].rearrange("p (t d) -> p t d", d=D)
        spare = work[:, T * D:]
        el = [mlp, spare]
        a0 = [e[:, 0:BN] for e in el]
        sq = [e[:, BN:4 * BN].rearrange("p (v n) -> p v n", v=3) for e in el]
        hu = [e[:, 4 * BN:5 * BN] for e in el]
        hw = [e[:, 5 * BN:6 * BN] for e in el]
        hp = [e[:, 6 * BN:7 * BN] for e in el]
        h2s = mlp[:, 0:4 * D].rearrange("p (s h d) -> p s h d", s=2, h=2)
        osq = spare[:, 0:12 * C].rearrange("p (s h d) -> p s h d", s=2, h=2)
        tot = mlp[:, 4 * D:4 * D + 8 * C].rearrange("p (h d) -> p h d", h=2)
        par = mlp[:, 1536:1536 + 2 * C].rearrange("p (a c) -> p a c", a=2)
        mean = mlp[:, 1664:1664 + C]
        stat = mlp[:, 1728:1728 + 2 * C].rearrange("p (a c) -> p a c", a=2)
        scl = mlp[:, 1856:1856 + D].rearrange("p (q c) -> p q c", q=4)
        O = acc[:, :, HN:].rearrange("p q (t h c) -> p q t h c", t=H, h=2)
        O0 = acc[:, 0, HN:].rearrange("p (n c) -> p n c", c=C)
        xsq = acc[:, 1, 0:HN]
        NB = HN // BN

        u_x2 = sem("u_x2")
        u_beta = sem("u_beta")
        u_lin = [sem(f"u_lin{s}") for s in range(2)]
        u_in = [sem(f"u_in{s}") for s in range(2)]
        u_el = sem("u_el")
        u_h2 = [sem(f"u_h2{s}") for s in range(2)]
        u_o = [sem(f"u_o{s}") for s in range(2)]
        u_cp = [sem(f"u_cp{s}") for s in range(2)]
        u_ad = [sem(f"u_ad{s}") for s in range(2)]
        u_z = sem("u_z")
        u_v = sem("u_v")
        u_par = sem("u_par")
        u_mean = sem("u_mean")
        u_xc = sem("u_xc")
        u_xsq = sem("u_xsq")
        u_var = sem("u_var")
        u_st = sem("u_st")
        u_rt = sem("u_rt")
        u_fin = sem("u_fin")
        u_out = sem("u_out")

        h2v = h2t_tab.rearrange("p (h t d) -> p h t d", h=2, d=D)

        with nc.Block() as block:
            @block.sync
            def _(sp):
                sp.dma_start(X2, rows(x2_tab, 0, T)).then_inc(u_x2, 16)

                def load(i, k, s):
                    sp.wait_ge(u_o[s], k)
                    sp.dma_start(h2s[:, s, :, :], h2v[:, :, ds(i, 1), :].rearrange("p h o d -> p (h o) d")).then_inc(u_h2[s], 16)

                sp.wait_ge(u_el, 9 * NB)
                with sp.Fori(0, H // 2) as k:
                    for s in range(2):
                        load(k * 2 + s, k, s)
                load(H - 1, H // 2, 0)
                for n in range(NCH):
                    for h in range(2):
                        sp.wait_ge(u_fin, 2 * n + h + 1)
                        t = h * H + n * 5
                        m = min(5, T - 2 - t)
                        sp.dma_start(out[t * P:(t + m) * P, :].rearrange("(t p) d -> p t d", p=P), X2[:, t:t + m, :]).then_inc(u_out, 16)
                sp.dma_start(out[(T - 2) * P:N, :], X2[0:LAST, T - 2, :]).then_inc(u_out, 16)
                sp.wait_ge(u_out, 16 * (2 * NCH + 1))

            @block.gpsimd
            def _(pool):
                pool.wait_ge(u_x2, 16)
                nc.gpsimd.tensor_tensor(X2[:, :, 0:C], X2[:, :, 0:C], bc(gb_sb[:, 1, :], 1, T), ALU.add).then_inc(u_beta, 1)

            @block.tensor
            def _(pe):
                with pe.Fori(0, NB // 2) as k:
                    for s in range(2):
                        n = (k * 2 + s) * BN
                        pe.wait_ge(u_el, k * 18)
                        for q in range(4):
                            for h in range(2):
                                mm = nc.tensor.matmul(ps[:, 4 * s + q, 0:BN], lin_sb[:, min(q, 1), h, :],
                                                      acc[:, q, ds(n + h * HN, BN)], start=(h == 0), stop=(h == 1))
                        mm.then_inc(u_lin[s], 1)
                pe.wait_ge(u_el, 9 * NB)

                def pair(i, k, s):
                    o = ps[:, s, :].rearrange("p (h d) -> p h d", h=2)
                    pe.wait_ge(u_cp[s], k * 2)
                    for q in range(4):
                        nc.tensor.matmul(o[:, :, q * C:(q + 1) * C], acc[:, q, ds(i * P, P)], wb_sb[:, min(q, 1), :],
                                         start=(q == 0), stop=False)
                    pe.wait_ge(u_h2[s], k * 16 + 16)
                    for h in range(2):
                        for b in range(2):
                            mm = nc.tensor.matmul(o[:, h, b * P:(b + 1) * P], h2s[:, s, h, b * P:(b + 1) * P], sc_sb[:, b, :],
                                                  start=False, stop=(h == 1 and b == 1))
                    mm.then_inc(u_o[s], 1)

                for k in range(H // 2):
                    for s in range(2):
                        pair(k * 2 + s, k, s)
                pair(H - 1, H // 2, 0)
                pe.wait_ge(u_par, 1)
                nc.tensor.matmul(ps[:, 4, 0:C], ones[:, :], par[:, 0, :], start=True, stop=True).then_inc(u_mean, 1)
                pe.wait_ge(u_par, 2)
                nc.tensor.matmul(ps[:, 5, 0:2 * C], ones[:, :], par.rearrange("p a c -> p (a c)"), start=True, stop=True).then_inc(u_var, 1)

            @block.scalar
            def _(act):
                with act.Fori(0, NB // 2) as k:
                    for s in range(2):
                        act.wait_ge(u_lin[s], k + 1)
                        act.wait_ge(u_el, k * 18)
                        b = 4 * s
                        for to, col in ((hu[s], (3, 1)), (hp[s], (7, 6)), (hw[s], (4, 2))):
                            nc.scalar.activation(to, ps[:, b, 0:BN], ACT.Identity, scale=wc_sb[:, col[0]:col[0] + 1],
                                                 bias=wc_sb[:, col[1]:col[1] + 1]).then_inc(u_in[s], 1)
                        nc.scalar.activation(a0[s], ps[:, b, 0:BN], ACT.Copy).then_inc(u_in[s], 1)
                        nc.scalar.activation(sq[s], ps[:, b + 1:b + 4, 0:BN], ACT.Square).then_inc(u_in[s], 1)

                act.wait_ge(u_el, 9 * NB)

                def pair(i, k, s):
                    o = ps[:, s, :].rearrange("p (h q c) -> p q h c", h=2, q=4)
                    act.wait_ge(u_o[s], k + 1)
                    act.wait_ge(u_ad[s], k * 2)
                    nc.scalar.activation(osq[:, s, :, :], ps[:, s, :].rearrange("p (h d) -> p h d", h=2)[:, :, C:D],
                                         ACT.Square).then_inc(u_cp[s], 1)
                    nc.scalar.activation(O[:, :, ds(i, 1), :, :].rearrange("p q o h c -> p (q o) h c"), o, ACT.Copy).then_inc(u_cp[s], 1)

                with act.Fori(0, H // 2) as k:
                    for s in range(2):
                        pair(k * 2 + s, k, s)
                pair(H - 1, H // 2, 0)
                act.wait_ge(u_xc, 1)
                nc.scalar.activation(xsq, acc[:, 0, HN:], ACT.Square).then_inc(u_xsq, 1)
                act.wait_ge(u_st, 1)
                nc.scalar.activation(stat, stat, ACT.Sqrt, bias=eps_sb[:, 0:1]).then_inc(u_rt, 1)

            @block.vector
            def _(dve):
                with dve.Fori(0, NB // 2) as k:
                    for s in range(2):
                        b, base = 4 * s, k * 18 + 9 * s
                        L = ds((k * 2 + s) * BN, BN)

                        def after(m):
                            dve.wait_ge(u_el, base + m)

                        dve.wait_ge(u_in[s], k * 5 + 5)
                        vv, gq = sq[s][:, 0, :], sq[s][:, 1, :]
                        nc.vector.tensor_tensor(vv, vv, sq[s][:, 1, :], ALU.add).then_inc(u_el, 1)
                        nc.vector.tensor_tensor(hu[s], hu[s], a0[s], ALU.mult).then_inc(u_el, 1)
                        nc.vector.tensor_tensor(hp[s], hp[s], a0[s], ALU.mult).then_inc(u_el, 1)
                        after(1)
                        nc.vector.tensor_tensor(vv, vv, sq[s][:, 2, :], ALU.add).then_inc(u_el, 1)
                        after(2)
                        nc.vector.scalar_tensor_tensor(out=hu[s], in0=hu[s], scalar=wc_sb[:, 0:1], in1=a0[s],
                                                       op0=ALU.add, op1=ALU.mult).then_inc(u_el, 1)
                        after(4)
                        nc.vector.tensor_tensor(hw[s], hw[s], vv, ALU.mult).then_inc(u_el, 1)
                        nc.vector.scalar_tensor_tensor(out=gq, in0=vv, scalar=wc_sb[:, 8:9], in1=hp[s],
                                                       op0=ALU.mult, op1=ALU.add).then_inc(u_el, 1)
                        after(6)
                        nc.vector.tensor_tensor(acc[:, 0, L], hu[s], hw[s], ALU.add).then_inc(u_el, 1)
                        after(7)
                        nc.vector.scalar_tensor_tensor(out=acc[:, 1:4, L], in0=bc(gq, 1, 3), scalar=wc_sb[:, 5:6],
                                                       in1=ps[:, b + 1:b + 4, 0:BN], op0=ALU.add, op1=ALU.mult).then_inc(u_el, 1)
                dve.wait_ge(u_el, 9 * NB)
                nc.vector.memset(tot[:, :, :], 0.0).then_inc(u_z, 1)
                dve.wait_ge(u_z, 1)

                def pair(i, k, s):
                    dve.wait_ge(u_cp[s], k * 2 + 2)
                    dve.wait_ge(u_ad[1 - s], k * 2 + 2 * s)
                    nc.vector.tensor_tensor(tot[:, :, 0:C], tot[:, :, 0:C],
                                            O[:, 0, ds(i, 1), :, :].rearrange("p o h c -> p (o h) c"), ALU.add).then_inc(u_ad[s], 1)
                    nc.vector.tensor_tensor(tot[:, :, C:D], tot[:, :, C:D], osq[:, s, :, :], ALU.add).then_inc(u_ad[s], 1)

                with dve.Fori(0, H // 2) as k:
                    for s in range(2):
                        pair(k * 2 + s, k, s)
                pair(H - 1, H // 2, 0)
                dve.wait_ge(u_ad[0], 2 * (H // 2) + 2)
                dve.wait_ge(u_cp[0], 2 * (H // 2) + 2)
                dve.wait_ge(u_cp[1], 2 * (H // 2))
                count = [0]

                def step(ins):
                    count[0] += 1
                    ins.then_inc(u_v, 1)
                    dve.wait_ge(u_v, count[0])

                nc.vector.tensor_tensor(par[:, 0, :], tot[:, 0, 0:C], tot[:, 1, 0:C], ALU.add).then_inc(u_par, 1)
                step(nc.vector.tensor_tensor(tot[:, 0, C:D], tot[:, 0, C:D], tot[:, 1, C:D], ALU.add))
                step(nc.vector.tensor_reduce(par[:, 1, :], tot[:, 0, C:D].rearrange("p (v c) -> p c v", v=3), AX_X, ALU.add))
                dve.wait_ge(u_mean, 1)
                step(nc.vector.tensor_scalar(mean, ps[:, 4, 0:C], 1.0 / N, None, ALU.mult))
                step(nc.vector.tensor_tensor(O0, O0, bc(mean, 1, T), ALU.subtract))
                step(nc.vector.memset(O[:, 0, H - 1, 1, :], 0.0))
                step(nc.vector.memset(small[:, 0:1], 0.0))
                step(nc.vector.memset(small[0:LAST, 0:1], 1.0))
                nc.vector.tensor_scalar(O[:, 0, H - 2, 1, :], O[:, 0, H - 2, 1, :], small[:, 0:1], None, ALU.mult).then_inc(u_xc, 1)
                dve.wait_ge(u_xsq, 1)
                nc.vector.tensor_reduce(par[:, 0, :], xsq.rearrange("p (n c) -> p c n", c=C), AX_X, ALU.add).then_inc(u_par, 1)
                dve.wait_ge(u_var, 1)
                step(nc.vector.tensor_scalar(stat[:, 0, :], ps[:, 5, 0:C], 1.0 / N, None, ALU.mult))
                nc.vector.tensor_scalar(stat[:, 1, :], ps[:, 5, C:2 * C], 1.0 / (3 * N), None, ALU.mult).then_inc(u_st, 1)
                dve.wait_ge(u_rt, 1)
                step(nc.vector.reciprocal(stat, stat))
                step(nc.vector.tensor_tensor(scl[:, 0, :], stat[:, 0, :], gb_sb[:, 0, :], ALU.mult))
                step(nc.vector.tensor_tensor(scl[:, 1, :], stat[:, 1, :], gb_sb[:, 2, :], ALU.mult))
                step(nc.vector.tensor_copy(scl[:, 2:4, :], bc(scl[:, 1, :], 1, 2)))
                dve.wait_ge(u_beta, 1)
                for n in range(NCH):
                    for h in range(2):
                        o = O[:, :, 5 * n:5 * n + 5, h, :]
                        xt = X2[:, h * H + 5 * n:h * H + 5 * n + 5, :]
                        step(nc.vector.tensor_tensor(o, o, bc(scl, 2, 5), ALU.mult))
                        nc.vector.tensor_tensor(xt[:, :, 0:C], xt[:, :, 0:C], o[:, 0, :, :], ALU.add).then_inc(u_v, 1)
                        count[0] += 1
                        xv = xt[:, :, C:D].rearrange("p t (c v) -> p v t c", v=3)
                        nc.vector.tensor_tensor(xv, xv, o[:, 1:4, :, :], ALU.add).then_inc(u_fin, 1)


_INS = (("x", "x"), ("src", "src"), ("dst", "dst"), ("attr16", "edge_attr_16"), ("attr4", "edge_attr_4"), ("weight", "edge_weight"),
        ("w_self", "L0_gnn_W_self"), ("w_nb", "L0_gnn_W_neighbor"), ("bias", "L0_gnn_bias"), ("w_up0", "L1_gnn_W_up0"),
        ("w_up1", "L1_gnn_W_up1"), ("m1", "L1_gnn_M1"), ("m2", "L1_gnn_M2"), ("m3", "L1_gnn_M3"), ("m4", "L1_gnn_M4"),
        ("w_lin0", "L1_gnn_W_lin0"), ("w_lin1", "L1_gnn_W_lin1"), ("w_sc0", "L1_gnn_Wsc0"), ("w_sc1", "L1_gnn_Wsc1"),
        ("wc0", "L1_gnn_Wc0"), ("wc1", "L1_gnn_Wc1"), ("w_b0", "L1_gnn_WB0"), ("w_b1", "L1_gnn_WB1"),
        ("gamma0", "L1_gnn_gamma0"), ("beta0", "L1_gnn_beta0"), ("gamma1", "L1_gnn_gamma1"))


def kernel(**inputs):
    import numpy as np
    import concourse.bacc as bacc
    from concourse.bass_utils import run_bass_kernel_spmd

    nc = bacc.Bacc("TRN2", target_bir_lowering=False, num_devices=1)
    arrays, args = {}, {}
    for arg, name in _INS:
        a = np.ascontiguousarray(inputs[name])
        arrays["in_" + name] = a
        args[arg] = nc.dram_tensor("in_" + name, a.shape, mybir.dt.from_np(a.dtype), kind="ExternalInput").ap()
    args["out"] = nc.dram_tensor("out_0", (N, D), F32, kind="ExternalOutput").ap()
    build(nc, **args)
    r = run_bass_kernel_spmd(nc, [arrays], core_ids=[0])
    return r.results[0]["out_0"]
```

```python
from contextlib import ExitStack

import concourse.bass as bass
from concourse import mybir

F32 = mybir.dt.float32
I32 = mybir.dt.int32
ALU = mybir.AluOpType
ACT = mybir.ActivationFunctionType
AX_X = mybir.AxisListType.X
ds = bass.ds

P = 128
N = 6250
E = 206250
D = 256
C = 64
R = 16
EPS = 1e-5

G = 4
SC = P * G
NU = -(-E // (2 * SC))
NSC = 2 * NU
EPAD = NU * 2 * SC
ETAIL = E - (NU - 1) * 2 * SC
ROUNDS = NU // 2
SROWS = NSC // 4
WU = 128
W = 32

T = 50
NPAD = T * P
LAST = N - (T - 2) * P
NCH = 5
TC = T // NCH
H = T // 2
HN = H * P
NT = T - 1
BN = 320
assert T == NCH * TC and TC % 2 == 0 and 0 < LAST < P and NT < ROUNDS - 1
assert NU % 2 == 0 and SROWS * 4 == NSC and SC // 2 < ETAIL < SC


def bc(ap, axis, n):
    ap = ap.unsqueeze(axis)
    shape = list(ap.shape)
    shape[axis] = n
    return ap.to_broadcast(shape)


def build(nc, x, src, dst, attr16, attr4, weight, w_self, w_nb, bias, w_up0, w_up1, m1, m2, m3, m4,
          w_lin0, w_lin1, w_sc0, w_sc1, wc0, wc1, w_b0, w_b1, gamma0, beta0, gamma1, out):
    h_tab = nc.dram_tensor("h_tab", [NPAD, D], F32).ap()
    up_tab = nc.dram_tensor("up_tab", [NPAD, D], F32).ap()
    x2_tab = nc.dram_tensor("x2_tab", [NPAD, D], F32).ap()
    h2t_tab = nc.dram_tensor("h2t_tab", [P, T * D], F32).ap()
    r3_tab = nc.dram_tensor("r3_tab", [NU, P, 4 * P], F32).ap()
    src_tail = nc.dram_tensor("src_tail", [2 * SC], I32).ap()
    dst_tail = nc.dram_tensor("dst_tail", [2 * SC], I32).ap()
    w_tail = nc.dram_tensor("w_tail", [2 * SC], F32).ap()
    a4_tail = nc.dram_tensor("a4_tail", [2 * SC, 4], F32).ap()
    a16_tail = nc.dram_tensor("a16_tail", [2 * SC, R], F32).ap()
    tails = ((src_tail, src), (dst_tail, dst), (w_tail, weight), (a4_tail, attr4), (a16_tail, attr16))

    E0 = (NU - 1) * 2 * SC

    def units(full, tail):
        if len(full.shape) == 1:
            return (full[0:E0].rearrange("(u j p g) -> u p j g", j=2, p=P, g=G),
                    tail.rearrange("(j p g) -> p j g", j=2, p=P))
        return (full[0:E0, :].rearrange("(u j p g) f -> u p j (g f)", j=2, p=P, g=G),
                tail.rearrange("(j p g) f -> p j (g f)", j=2, p=P))

    src_u, dst_u, w_u = units(src, src_tail), units(dst, dst_tail), units(weight, w_tail)
    a4_u, a16_u = units(attr4, a4_tail), units(attr16, a16_tail)

    def unit_of(view, u):
        if isinstance(u, int) and u == NU - 1:
            return view[1]
        return view[0][ds(u, 1), :, :, :].rearrange("o p j g -> (o p) j g")

    def row(ap):
        return ap.rearrange("p o n -> p (o n)")

    def rows(tab, t, n):
        return tab[ds(t * P, n * P), :].rearrange("(t p) d -> p t d", p=P)

    with ExitStack() as ctx:
        def sb(name, shape, dt=F32):
            return ctx.enter_context(nc.sbuf_tensor(name, shape, dt))

        def sem(name):
            return ctx.enter_context(nc.semaphore(name))

        acc = sb("acc", [P, 4, NPAD])
        work = sb("work", [P, T * D + 2560])
        mlp = sb("mlp", [P, 2560])
        ident = sb("ident", [P, P])
        ones = sb("ones", [P, P])
        win = sb("win", [P, WU])
        ws_sb = sb("ws_sb", [P, 2, D])
        wn_sb = sb("wn_sb", [P, 2, D])
        bias_sb = sb("bias_sb", [1, D])
        m1_sb = sb("m1_sb", [P, 4, P])
        m2_sb = sb("m2_sb", [P, P])
        m3_sb = sb("m3_sb", [P, P])
        m4_sb = sb("m4_sb", [P, 2, 4, C])
        up_sb = sb("up_sb", [P, 2, P])
        sc_sb = sb("sc_sb", [P, 2, P])
        lin_sb = sb("lin_sb", [P, 3, 2, P])
        wb_sb = sb("wb_sb", [P, 2, P])
        wc_sb = sb("wc_sb", [P, 9])
        gb_sb = sb("gb_sb", [P, 3, C])
        base0_i = sb("base0_i", [1, NSC], I32)
        base_i = sb("base_i", [1, NSC], I32)
        base0_f = sb("base0_f", [P, NSC])
        base_f = sb("base_f", [P, NSC])
        npass = sb("npass", [1, 2], I32)
        mv = sb("mv", [P, T, 6])
        lnt = sb("lnt", [P, 6, TC])
        rstd = sb("rstd", [P, T])
        nbias = sb("nbias", [P, T])
        eps_sb = sb("eps_sb", [P, 1])
        small = sb("small", [P, 32])
        ps = ctx.enter_context(nc.psum_tensor("ps", [P, 8, 512], F32))

        X = acc[:, 2:4, :].rearrange("p q n -> p (q n)").rearrange("p (t d) -> p t d", d=D)

        s_zx = sem("s_zx")
        s_zw = sem("s_zw")
        s_xin = [sem(f"s_xin{c}") for c in range(NCH)]
        s_wts = sem("s_wts")
        s_wts2 = sem("s_wts2")
        s_fill = sem("s_fill")
        s_tail = sem("s_tail")
        s_chk_in = sem("s_chk_in")
        s_v0 = sem("s_v0")
        s_ln = sem("s_ln")
        s_sq = sem("s_sq")
        s_lnt = sem("s_lnt")
        s_nb = sem("s_nb")
        s_h = sem("s_h")
        s_hst = sem("s_hst")
        s_id = sem("s_id")
        s_acc0 = sem("s_acc0")
        s_bn = sem("s_bn")
        s_chk = sem("s_chk")
        s_chk_ps = sem("s_chk_ps")

        h_st = work[:, 0:T * D].rearrange("p (t d) -> p t d", d=D)
        chk = mlp[0:SROWS, 0:4 * SC].rearrange("p (q e) -> p q e", q=4)
        chk_i = chk.bitcast(I32)
        cst = work[:, T * D:T * D + 8 * R]
        neg = work[:, T * D + 8 * R:T * D + 8 * R + 8].bitcast(I32)
        win_i = work[:, T * D + 256:T * D + 256 + WU].bitcast(I32)

        wts = [(ws_sb[:, :, :], w_self.rearrange("(k p) n -> p k n", p=P)), (bias_sb[:, :], bias.unsqueeze(0))]
        for g in range(8):
            wts.append((m1_sb[g * R:(g + 1) * R, g // 2, (g % 2) * C:(g % 2 + 1) * C], m1))
        wts2 = [(wn_sb[:, :, :], w_nb.rearrange("(k p) n -> p k n", p=P))]
        m4v = m4.rearrange("h (b c) -> h b c", b=4)
        for lo in range(2):
            r = slice(lo * C, (lo + 1) * C)
            wts += [(m2_sb[r, r], m2), (m3_sb[r, r], m3)]
            wts2 += [(m4_sb[r, lo, 0:2, :], m4v[:, 0:2, :]), (m4_sb[r, lo, 2, :], m4v[:, 3, :]),
                     (m4_sb[r, lo, 3, :], m4v[:, 2, :])]
            wts2 += [(up_sb[r, 0, r], (w_up0, w_up1)[lo]), (up_sb[r, 1, r], w_up1),
                     (sc_sb[r, 0, r], (w_sc0, w_sc1)[lo]), (sc_sb[r, 1, r], w_sc1),
                     (wb_sb[r, 0, r], w_b0), (wb_sb[r, 1, r], w_b1),
                     (lin_sb[0:C, 0, lo, r], w_lin0), (lin_sb[C:P, 1, lo, r], w_lin1), (lin_sb[0:C, 2, lo, r], w_lin1),
                     (wc_sb[r, 0:5], wc0), (wc_sb[r, 5:9], wc1)]
        for i, v in enumerate((gamma0, beta0, gamma1)):
            wts2.append((gb_sb[:, i, :], v.unsqueeze(0).to_broadcast([P, C])))

        def ln_stats(c, step, done):
            st = mv[:, c * TC:(c + 1) * TC, :]
            nc.vector.tensor_tensor(lnt[:, 0, :], st[:, :, 1], st[:, :, 4], ALU.add).then_inc(s_lnt, 1)
            nc.vector.tensor_tensor(lnt[:, 2, :], st[:, :, 2], st[:, :, 5], ALU.add).then_inc(s_lnt, 1)
            step(nc.vector.tensor_tensor(lnt[:, 1, :], st[:, :, 1], st[:, :, 4], ALU.subtract))
            step(nc.vector.tensor_tensor(lnt[:, 3, :], lnt[:, 1, :], lnt[:, 1, :], ALU.mult))
            nc.vector.scalar_tensor_tensor(out=lnt[:, 5, :], in0=lnt[:, 3, :], scalar=float(D) / 4, in1=lnt[:, 2, :],
                                           op0=ALU.mult, op1=ALU.add).then_inc(done, 1)

        def ln_scale(c, step, done):
            t0 = c * TC
            step(nc.vector.reciprocal(rstd[:, t0:t0 + TC], rstd[:, t0:t0 + TC]))
            nc.vector.scalar_tensor_tensor(out=nbias[:, t0:t0 + TC], in0=lnt[:, 0, :], scalar=-0.5,
                                           in1=rstd[:, t0:t0 + TC], op0=ALU.mult, op1=ALU.mult).then_inc(done, 1)

        with nc.Block() as block:
            @block.sync
            def _(sp):
                sp.wait_ge(s_zx, 1)
                for c in range(NCH - 1):
                    sp.dma_start(X[:, c * TC:(c + 1) * TC, :], rows(x, c * TC, TC)).then_inc(s_xin[c], 16)
                c = (NCH - 1) * TC
                if c < T - 2:
                    sp.dma_start(X[:, c:T - 2, :], rows(x, c, T - 2 - c)).then_inc(s_xin[NCH - 1], 16)
                sp.dma_start(X[0:LAST, T - 2, :], x[(T - 2) * P:N, :]).then_inc(s_xin[NCH - 1], 16)
                full = (SROWS - 1) * 4 * SC
                sp.dma_start(chk_i[0:SROWS - 1, :, :], dst[0:full].rearrange("(p q e) -> p q e", q=4, e=SC)).then_inc(s_chk_in, 16)
                left = E - full
                q = left // SC
                r = left % SC
                sp.dma_start(chk_i[SROWS - 1:SROWS, 0:q, :], dst[full:full + q * SC].rearrange("(o q e) -> o q e", o=1, q=q)).then_inc(s_chk_in, 16)
                for i in (q, q + 1):
                    sp.dma_start(chk_i[SROWS - 1:SROWS, i, 0:r], dst[E - r:E].unsqueeze(0)).then_inc(s_chk_in, 16)
                    sp.dma_start(chk_i[SROWS - 1:SROWS, i, r:SC], dst[E - (SC - r):E].unsqueeze(0)).then_inc(s_chk_in, 16)
                with nc.allow_non_contiguous_dma(reason="one number in 512"):
                    sp.dma_start(base0_i[:, 0:NSC - 1], dst[0:(NSC - 2) * SC + 1:SC].unsqueeze(0)).then_inc(s_chk_in, 16)
                sp.dma_start(base0_i[:, NSC - 1:NSC], dst[E0:E0 + 1].unsqueeze(0)).then_inc(s_chk_in, 16)
                for c in range(NCH):
                    sp.wait_ge(s_h, (c + 1) * TC)
                    sp.dma_start(rows(h_tab, c * TC, TC), h_st[:, c * TC:(c + 1) * TC, :]).then_inc(s_hst, 16)
                    if c == 0:
                        sp.wait_ge(s_fill, 16 * 5)
                        for tab, of in tails:
                            if len(tab.shape) == 1:
                                sp.dma_start(tab[0:ETAIL].unsqueeze(0), of[E0:E].unsqueeze(0)).then_inc(s_tail, 16)
                            else:
                                sp.dma_start(tab[0:ETAIL, :], of[E0:E, :]).then_inc(s_tail, 16)
                sp.wait_ge(s_hst, 16 * NCH)
                sp.wait_ge(s_tail, 16 * 5)

            @block.gpsimd
            def _(pool):
                nc.gpsimd.iota(win_i, pattern=[[1, WU]], base=0, channel_multiplier=0).then_inc(s_id, 1)
                nc.gpsimd.memset(ident[:, :], 0.0).then_inc(s_id, 1)
                nc.gpsimd.memset(ones[:, :], 1.0).then_inc(s_id, 1)
                pool.wait_ge(s_id, 3)
                nc.gpsimd.affine_select(out=ident[:, :], in_=ident[:, :], compare_op=ALU.not_equal, fill=1.0, base=0,
                                        pattern=[[-1, P]], channel_multiplier=1).then_inc(s_id, 1)
                nc.gpsimd.tensor_copy(win[:, :], win_i).then_inc(s_id, 1)
                zeroed = (m4_sb, up_sb, sc_sb, lin_sb, wb_sb)
                for tile in zeroed:
                    nc.gpsimd.memset(tile[:], 0.0).then_inc(s_id, 1)
                pool.wait_ge(s_id, 5 + len(zeroed))
                for to, of in wts2:
                    pool.dma_start(to, of).then_inc(s_wts2, 16)
                nc.gpsimd.memset(acc[:, 0:2, :], 0.0).then_inc(s_acc0, 1)
                pool.wait_ge(s_wts2, 16 * len(wts2))

            @block.scalar
            def _(act):
                act.wait_ge(s_zw, 1)
                for tab, of in tails:
                    flat = tab if len(tab.shape) == 1 else tab.rearrange("e f -> (e f)")
                    n = 1 if len(tab.shape) == 1 else tab.shape[1]
                    fill = neg if tab is dst_tail else cst[:, 0:8].bitcast(I32) if tab is src_tail else cst[:, 0:8 * n]
                    act.dma_start(flat.rearrange("(p f) -> p f", p=P), fill).then_inc(s_fill, 16)
                for to, of in wts:
                    act.dma_start(to, of).then_inc(s_wts, 16)
                for c in range(NCH):
                    t0 = c * TC
                    act.wait_ge(s_ln, c + 1)
                    nc.scalar.activation(rstd[:, t0:t0 + TC], lnt[:, 5, :], ACT.Sqrt, bias=eps_sb[:, 0:1],
                                         scale=1.0 / D).then_inc(s_sq, 1)
                    act.wait_ge(s_nb, c + 1)
                    with act.Fori(0, 2) as i:
                        for m in range(TC // 2):
                            t = i * (TC // 2) + (t0 + m)
                            nc.scalar.activation(row(h_st[:, ds(t, 1), :]), row(X[:, ds(t, 1), :]), ACT.Relu,
                                                 bias=nbias[:, ds(t, 1)], scale=rstd[:, ds(t, 1)]).then_inc(s_h, 1)
                act.wait_ge(s_wts, 16 * len(wts))

            @block.vector
            def _(dve):
                count = [0]

                def step(ins):
                    count[0] += 1
                    ins.then_inc(s_v0, 1)
                    dve.wait_ge(s_v0, count[0])

                step(nc.vector.memset(X[:, T - 2:T, :], 0.0))
                dve.sem_inc(s_zx, 1)
                for to, value in ((m1_sb[:], 0.0), (m2_sb[:], 0.0), (m3_sb[:], 0.0), (cst, 0.0), (neg, -1)):
                    nc.vector.memset(to, value).then_inc(s_v0, 1)
                count[0] += 5
                step(nc.vector.memset(eps_sb[:, :], EPS))
                dve.sem_inc(s_zw, 1)

                for c in range(NCH):
                    t0 = c * TC
                    dve.wait_ge(s_xin[c], 16 * (1 + (c == NCH - 1 and c * TC < T - 2)))
                    with dve.Fori(0, 2) as i:
                        for m in range(TC // 2):
                            t = i * (TC // 2) + (t0 + m)
                            nc.vector.bn_stats(row(mv[:, ds(t, 1), :]), row(X[:, ds(t, 1), :])).then_inc(s_bn, 1)
                    dve.wait_ge(s_bn, t0 + TC)
                    if c >= 1:
                        dve.wait_ge(s_nb, c)
                    ln_stats(c, step, s_ln)
                    dve.wait_ge(s_sq, c + 1)
                    ln_scale(c, step, s_nb)

                dve.wait_ge(s_chk_in, 16 * 8)
                first, high, low, bad = (small[0:SROWS, 4 * k:4 * k + 4] for k in range(4))
                high_u, low_u = small[0:SROWS, 16:18], small[0:SROWS, 18:20]
                nc.vector.tensor_copy(base_f[0:1, :], base0_i[:, :]).then_inc(s_chk, 1)
                nc.vector.tensor_copy(first, chk_i[:, :, 0]).then_inc(s_v0, 1)
                nc.vector.tensor_reduce(high, chk_i, AX_X, ALU.max).then_inc(s_v0, 1)
                nc.vector.tensor_reduce(low, chk_i, AX_X, ALU.min).then_inc(s_v0, 1)
                count[0] += 3
                dve.wait_ge(s_v0, count[0])
                nc.vector.tensor_tensor(high_u, high[:, 1:4:2], first[:, 0:4:2], ALU.subtract).then_inc(s_v0, 1)
                nc.vector.tensor_tensor(low_u, first[:, 0:4:2], low[:, 1:4:2], ALU.subtract).then_inc(s_v0, 1)
                count[0] += 2
                step(nc.vector.tensor_tensor(bad, high, first, ALU.subtract))
                step(nc.vector.tensor_tensor(low, first, low, ALU.subtract))
                nc.vector.tensor_scalar(high_u, high_u, float(WU), None, ALU.is_ge).then_inc(s_v0, 1)
                nc.vector.tensor_scalar(low_u, low_u, 0.0, None, ALU.is_gt).then_inc(s_v0, 1)
                nc.vector.tensor_scalar(bad, bad, float(W), None, ALU.is_ge).then_inc(s_v0, 1)
                count[0] += 3
                step(nc.vector.tensor_scalar(low, low, 0.0, None, ALU.is_gt))
                nc.vector.tensor_tensor(high_u, high_u, low_u, ALU.add).then_inc(s_v0, 1)
                count[0] += 1
                step(nc.vector.tensor_tensor(bad, bad, low, ALU.add))
                nc.vector.tensor_reduce(small[0:SROWS, 21:22], bad, AX_X, ALU.add).then_inc(s_v0, 1)
                count[0] += 1
                step(nc.vector.tensor_reduce(small[0:SROWS, 20:21], high_u, AX_X, ALU.add))
                nc.vector.tensor_tensor(small[0:SROWS, 20:21], small[0:SROWS, 20:21], small[0:SROWS, 21:22], ALU.add).then_inc(s_chk, 1)
                dve.wait_ge(s_chk_ps, 1)
                nc.vector.tensor_copy(base0_f[:, :], ps[:, 5, 0:NSC]).then_inc(s_v0, 1)
                count[0] += 1
                dve.wait_ge(s_chk_ps, 2)
                step(nc.vector.tensor_scalar(small[:, 22:24], ps[:, 4, 0:2], 1.0, None, ALU.min))
                nc.vector.tensor_scalar(small[:, 24:26], small[:, 22:24], -1.0, 1.0, ALU.mult, ALU.add).then_inc(s_v0, 1)
                count[0] += 1
                for layer, w in enumerate((WU, W)):
                    step(nc.vector.tensor_scalar(small[0:1, 26 + layer:27 + layer], small[0:1, 22 + layer:23 + layer],
                                                 float(-(-N // w) - 1), 1.0, ALU.mult, ALU.add))
                step(nc.vector.tensor_copy(npass[:, :], small[0:1, 26:28]))

            @block.tensor
            def _(pe):
                pe.wait_ge(s_id, 5)
                pe.wait_ge(s_chk, 1)
                nc.tensor.matmul(ps[:, 5, 0:NSC], ones[0:1, :], base_f[0:1, :], start=True, stop=True).then_inc(s_chk_ps, 1)
                pe.wait_ge(s_chk, 2)
                nc.tensor.matmul(ps[:, 4, 0:2], ones[0:SROWS, :], small[0:SROWS, 20:22], start=True, stop=True).then_inc(s_chk_ps, 1)

        rows_g = work[:, 0:2 * 8 * D].rearrange("p (s k d) -> p s k d", s=2, k=8)
        prod = work[:, 4096:7168].rearrange("p (j k b c) -> p j k b c", j=2, k=G, b=6)
        x1s = work[:, 7168:8704].rearrange("p (j v g c) -> p j v g c", j=2, v=3, g=G)
        y = work[:, 8704:8960].rearrange("p (g c) -> p g c", g=G)
        onehot = mlp[:, :].rearrange("p (s k a w) -> p s k a w", s=2, k=8, a=5)
        hot_u = work[:, 8192:10240].rearrange("p (s k w) -> p s k w", s=2, k=8)
        eq_u = mlp[:, 1536:2560].rearrange("p (k w) -> p k w", w=WU)
        rel = work[:, 10496:10504]
        idx = work[:, 10504:10520].bitcast(I32).rearrange("p (s k) -> p s k", s=2)
        dsti = work[:, 10520:10536].bitcast(I32).rearrange("p (s k) -> p s k", s=2)
        wgt = work[:, 10536:10552].rearrange("p (s k) -> p s k", s=2)
        sh = work[:, 10560:10624].rearrange("p (s k) -> p s k", s=2)
        r3 = work[:, 10624:11648].rearrange("p (s n) -> p s n", s=2)
        xt_in, ht_in, hT = (work[:, 4096 + k * D:4096 + (k + 1) * D] for k in range(3))
        attr = mlp[:, 0:256].rearrange("p (s n) -> p s n", s=2)
        attr_t = mlp[:, 256:384]
        r1 = mlp[:, 512:1024]
        r2 = mlp[:, 1024:1536]

        def edge_syms(ph):
            return dict(
                idx=[sem(f"idx{ph}_{s}") for s in range(2)],
                edge=[sem(f"edge{ph}_{s}") for s in range(2)],
                rad=[sem(f"rad{ph}_{s}") for s in range(2)],
                rad_used=[sem(f"rad_used{ph}_{s}") for s in range(2)],
                got=[[sem(f"got{ph}_{s}{j}") for j in range(2)] for s in range(2)],
                rel=sem(f"rel{ph}"), eq=sem(f"eq{ph}"),
                hot=[sem(f"hot{ph}_{s}") for s in range(2)],
                summed=[[sem(f"summed{ph}_{s}{j}") for j in range(2)] for s in range(2)],
                added=[sem(f"added{ph}_{j}") for j in range(2)],
                base=sem(f"base{ph}"),
                settled=sem(f"settled{ph}"),
                fresh=sem(f"fresh{ph}"),
            )

        def passes(eng, layer):
            return eng.value_load(npass[0:1, layer:layer + 1], min_val=1, max_val=-(-N // (WU, W)[layer]))

        def load_units(sp, layer, S, edge_views, rad_of, rad_to, edge_used, load_tile=None):
            def load(u, pz, k, s):
                use = pz * ROUNDS + k
                for j in range(2):
                    sp.wait_ge(S["got"][s][j], k * (16 * G))
                sp.dma_start(idx[:, s, :].rearrange("p (j g) -> p j g", g=G), unit_of(src_u, u)).then_inc(S["idx"][s], 16)
                for used in edge_used:
                    sp.wait_ge(used[s], use)
                for to, view in edge_views:
                    sp.dma_start(to[:, s, :].rearrange("p (j g) -> p j g", j=2), unit_of(view, u)).then_inc(S["edge"][s], 16)
                sp.wait_ge(S["rad_used"][s], use)
                sp.dma_start(rad_to(s), rad_of(u)).then_inc(S["rad"][s], 16)

            with sp.Fori(0, passes(sp, layer)) as pz:
                sp.wait_ge(S["fresh"], pz)
                sp.sem_inc(s_turn, 1)
                if load_tile:
                    with sp.Fori(0, NT - 1) as k:
                        for s in range(2):
                            load(k * 2 + s, pz, k, s)
                        load_tile(k, pz)
                    for s in range(2):
                        load((NT - 1) * 2 + s, pz, NT - 1, s)
                    load_tile(NT - 1, pz)
                with sp.Fori(NT if load_tile else 0, ROUNDS - 1) as k:
                    for s in range(2):
                        load(k * 2 + s, pz, k, s)
                for s in range(2):
                    load(NU - 2 + s, pz, ROUNDS - 1, s)
                sp.sem_inc(S["settled"], 1)

        def gather_units(pool, layer, S, table, taken, waiters):
            with pool.Fori(0, passes(pool, layer)) as pz:
                with pool.Fori(0, ROUNDS) as k:
                    for s in range(2):
                        use = pz * ROUNDS + k
                        pool.wait_ge(S["idx"][s], use * 16 + 16)
                        for j in range(2):
                            pool.wait_ge(taken[s][j], use)
                            pool.sem_inc(s_turn, 1)
                            for g in range(G):
                                q = j * G + g
                                pool.indirect_dma_start(
                                    out=rows_g[:, s, q, :], out_offset=None, in_=table,
                                    in_offset=bass.IndirectOffsetOnAxis(ap=idx[:, s, q:q + 1], axis=0),
                                ).then_inc(S["got"][s][j], 16)
                for s in range(2):
                    for j in range(2):
                        pool.wait_ge(S["got"][s][j], 16 * G * ROUNDS)
                pool.wait_ge(S["settled"], pz * waiters + waiters)
                pool.sem_inc(s_turn, 1)
                pool.dma_reset()
                for s in range(2):
                    for j in range(2):
                        pool.sem_clear(S["got"][s][j])
                pool.sem_inc(S["fresh"], 1)

        def hot_steps(dve, S, u, use, s, layer):
            def step_rel():
                dve.wait_ge(S["edge"][s], use * 32 + 32)
                base = (bc(base_f[:, ds(u * 2, 1)], 2, G).to_broadcast([P, 2, G]), bc(base_f[:, ds(u * 2, 2)], 2, G))[layer]
                nc.vector.tensor_tensor(rel.rearrange("p (j g) -> p j g", j=2), dsti[:, s, :].rearrange("p (j g) -> p j g", j=2),
                                        base, ALU.subtract).then_inc(S["rel"], 1)

            def step_eq(gu):
                to, w = ((eq_u, WU), (onehot[:, s, :, 4, :], W))[layer]
                dve.wait_ge(S["rel"], gu + 1)
                if layer == 1:
                    dve.wait_ge(S["summed"][s][1], use)
                nc.vector.tensor_tensor(to, bc(win[:, 0:w], 1, 8), bc(rel, 2, w), ALU.is_equal).then_inc(S["eq"], 1)

            def step_hot(gu):
                dve.wait_ge(S["eq"], gu + 1)
                if layer == 0:
                    dve.wait_ge(S["summed"][s][1], use)
                    nc.vector.tensor_tensor(hot_u[:, s, :, :], eq_u, bc(wgt[:, s, :], 2, WU), ALU.mult).then_inc(S["hot"][s], 1)
                else:
                    for j in range(2):
                        v = sh[:, s, 16 * j:16 * j + 16].rearrange("p (k a) -> p k a", a=4)
                        last = nc.vector.tensor_tensor(onehot[:, s, 4 * j:4 * j + 4, 0:4, :], bc(onehot[:, s, 4 * j:4 * j + 4, 4, :], 2, 4),
                                                       bc(v, 3, W), ALU.mult)
                    last.then_inc(S["hot"][s], 1)

            return step_rel, step_eq, step_hot

        def set_base(dve, S, layer, pz):
            w = float((WU, W)[layer])
            nc.vector.tensor_scalar(base_f[:, :], base_f[:, :], w, None, ALU.add).then_inc(S["base"], 1)
            nc.vector.tensor_scalar(base_i[:, :], base_i[:, :], w, None, ALU.add).then_inc(S["base"], 1)
            dve.wait_ge(S["base"], pz * 2 + 4)

        def first_base(dve, S, layer):
            nc.vector.tensor_scalar(base_f[:, :], base0_f[:, :], small[:, 24 + layer:25 + layer], None, ALU.mult).then_inc(S["base"], 1)
            dve.wait_ge(S["base"], 1)
            nc.vector.tensor_copy(base_i[:, :], base_f[0:1, :]).then_inc(S["base"], 1)
            dve.wait_ge(S["base"], 2)

        s_turn = sem("s_turn")

        S = edge_syms(1)
        at_ready, z1_ready, r1_ready, z2_ready, r2_ready, z3_ready, r3_ready = (
            sem(n) for n in ("at_ready", "z1_ready", "r1_ready", "z2_ready", "r2_ready", "z3_ready", "r3_ready"))
        tile_in = sem("tile_in")
        tile_tp = sem("tile_tp")
        tile_ht = sem("tile_ht")
        tile_self = sem("tile_self")
        tile_x1 = sem("tile_x1")
        r3_stored = [sem(f"r3_stored{s}") for s in range(2)]

        with nc.Block() as block:
            @block.sync
            def _(sp):
                def load_tile(k, pz):
                    sp.wait_ge(tile_x1, pz * NT + k)
                    if isinstance(k, int):
                        sp.dma_start(xt_in[0:LAST, :], x[k * P:N, :]).then_inc(tile_in, 16)
                    else:
                        sp.dma_start(xt_in, x[ds(k * P, P), :]).then_inc(tile_in, 16)
                    sp.dma_start(ht_in, h_tab[ds(k * P, P), :]).then_inc(tile_in, 16)

                load_units(sp, 0, S, ((dsti, dst_u), (wgt, w_u)), lambda u: unit_of(a16_u, u),
                           lambda s: attr[:, s, :].rearrange("p (j n) -> p j n", j=2), [S["hot"]], load_tile)

            @block.gpsimd
            def _(pool):
                gather_units(pool, 0, S, h_tab, S["summed"], 2)

            @block.vector
            def _(dve):
                first_base(dve, S, 0)
                with dve.Fori(0, passes(dve, 0)) as pz:
                    def hot(u, use, gu, s):
                        for part, arg in zip(hot_steps(dve, S, u, use, s, 0), ((), (gu,), (gu,))):
                            part(*arg)

                    def unit(k, s, last=False, tile=False):
                        use, gu = pz * ROUNDS + k, pz * NU + k * 2 + s
                        if not last:
                            hot(k * 2 + s + 1, use + s, gu + 1, 1 - s)
                            turned(gu + 1, use + s, 1 - s)
                        b = dve.value_load(base_i[0:1, ds(k * 4 + 2 * s, 1)], min_val=0, max_val=N - 1)
                        dve.wait_ge(S["summed"][s][1], use + 1)
                        dve.wait_ge(S["added"][1 - s], use + s)
                        to = acc[:, 0:2, ds(b, WU)]
                        nc.vector.tensor_tensor(to, to, ps[:, 6 + s, 0:2 * WU].rearrange("p (h w) -> p h w", h=2),
                                                ALU.add).then_inc(S["added"][s], 1)
                        if tile:
                            done = pz * NT + k
                            if s == 0:
                                dve.wait_ge(tile_tp, done + 1)
                                dve.wait_ge(tile_self, done)
                                nc.vector.tensor_copy(hT, ps[:, 4, 0:D]).then_inc(tile_ht, 1)
                            else:
                                dve.wait_ge(tile_self, done + 1)
                                nc.vector.tensor_tensor(row(X[:, ds(k, 1), :]), xt_in, ps[:, 5, 0:D], ALU.add).then_inc(tile_x1, 1)

                    def turned(gu, use, s):
                        dve.wait_ge(S["rad_used"][s], use + 1)
                        dve.wait_ge(z1_ready, gu)
                        nc.vector.tensor_copy(attr_t, ps[:, 0, 0:P]).then_inc(at_ready, 1)

                    hot(0, pz * ROUNDS, pz * NU, 0)
                    turned(pz * NU, pz * ROUNDS, 0)
                    with dve.Fori(0, NT) as k:
                        for s in range(2):
                            unit(k, s, tile=True)
                    with dve.Fori(NT, ROUNDS - 1) as k:
                        for s in range(2):
                            unit(k, s)
                    for s in range(2):
                        unit(ROUNDS - 1, s, last=(s == 1))
                    dve.wait_ge(S["added"][1], pz * ROUNDS + ROUNDS)
                    set_base(dve, S, 0, pz)

            @block.tensor
            def _(pe):
                def turn(s, use, gu):
                    pe.wait_ge(S["rad"][s], use * 16 + 16)
                    pe.wait_ge(at_ready, gu)
                    nc.tensor.transpose(ps[:, 0, 0:P], attr[:, s, :], ident[:, :]).then_inc(S["rad_used"][s], 1)

                def sums(s, j, k, use):
                    pe.wait_ge(S["got"][s][j], k * (16 * G) + 16 * G)
                    if j == 0:
                        pe.wait_ge(S["hot"][s], use + 1)
                        pe.wait_ge(S["added"][s], use)
                    for g in range(G):
                        q = j * G + g
                        for half in range(2):
                            mm = nc.tensor.matmul(ps[:, 6 + s, half * WU:(half + 1) * WU], rows_g[:, s, q, half * P:(half + 1) * P],
                                                  hot_u[:, s, q, :], start=(q == 0 and half == 0), stop=(q == 7 and half == 1))
                    mm.then_inc(S["summed"][s][j], 1)

                def tile_part(k, s):
                    done = pz * NT + k
                    if s == 0:
                        pe.wait_ge(tile_in, done * 32 + 32)
                        pe.wait_ge(tile_ht, done)
                        for b in range(2):
                            mm = nc.tensor.transpose(ps[:, 4, b * P:(b + 1) * P], ht_in[:, b * P:(b + 1) * P], ident[:, :])
                        mm.then_inc(tile_tp, 1)
                    else:
                        pe.wait_ge(tile_ht, done + 1)
                        pe.wait_ge(tile_x1, done)
                        nc.tensor.matmul(ps[:, 5, 0:D], ones[0:1, :], bias_sb[:, :], start=True, stop=False)
                        for b in range(2):
                            mm = nc.tensor.matmul(ps[:, 5, 0:D], hT[:, b * P:(b + 1) * P], ws_sb[:, b, :], start=False, stop=(b == 1))
                        mm.then_inc(tile_self, 1)

                def unit(k, s, last=False, tile=False):
                    use, gu = pz * ROUNDS + k, pz * NU + k * 2 + s
                    pe.wait_ge(at_ready, gu + 1)
                    pe.wait_ge(r1_ready, gu)
                    for q in range(4):
                        mm = nc.tensor.matmul(ps[:, 1, q * P:(q + 1) * P], m1_sb[:, q, :], attr_t, start=True, stop=True)
                    mm.then_inc(z1_ready, 1)
                    sums(s, 0, k, use)
                    if not last:
                        turn(1 - s, use + s, gu + 1)
                    pe.wait_ge(r1_ready, gu + 1)
                    pe.wait_ge(r2_ready, gu)
                    nc.tensor.matmul(ps[:, 2, :], m2_sb[:, :], r1, start=True, stop=True).then_inc(z2_ready, 1)
                    if tile:
                        tile_part(k, s)
                    sums(s, 1, k, use)
                    pe.wait_ge(r2_ready, gu + 1)
                    pe.wait_ge(r3_ready, gu)
                    nc.tensor.matmul(ps[:, 3, :], m3_sb[:, :], r2, start=True, stop=True).then_inc(z3_ready, 1)

                with pe.Fori(0, passes(pe, 0)) as pz:
                    pe.wait_ge(S["fresh"], pz)
                    turn(0, pz * ROUNDS, pz * NU)
                    with pe.Fori(0, NT) as k:
                        for s in range(2):
                            unit(k, s, tile=True)
                    with pe.Fori(NT, ROUNDS - 1) as k:
                        for s in range(2):
                            unit(k, s)
                    for s in range(2):
                        unit(ROUNDS - 1, s, last=(s == 1))
                    pe.sem_inc(S["settled"], 1)

            @block.scalar
            def _(act):
                with act.Fori(0, passes(act, 0)) as pz:
                    with act.Fori(0, ROUNDS) as k:
                        for s in range(2):
                            use = pz * ROUNDS + k
                            gu = pz * NU + k * 2 + s
                            act.wait_ge(z1_ready, gu + 1)
                            act.wait_ge(z2_ready, gu)
                            nc.scalar.activation(r1, ps[:, 1, :], ACT.Silu).then_inc(r1_ready, 1)
                            act.wait_ge(z2_ready, gu + 1)
                            act.wait_ge(z3_ready, gu)
                            nc.scalar.activation(r2, ps[:, 2, :], ACT.Silu).then_inc(r2_ready, 1)
                            act.wait_ge(z3_ready, gu + 1)
                            act.wait_ge(r3_stored[s], use * 16)
                            nc.scalar.activation(r3[:, s, :], ps[:, 3, :], ACT.Silu).then_inc(r3_ready, 1)
                            act.wait_ge(r3_ready, gu + 1)
                            act.dma_start(r3_tab[ds(k * 2 + s, 1), :, :].rearrange("o p n -> (o p) n"), r3[:, s, :]).then_inc(r3_stored[s], 16)
                    for s in range(2):
                        act.wait_ge(r3_stored[s], pz * (16 * ROUNDS) + 16 * ROUNDS)

        t_clr = sem("t_clr")
        t_agg = sem("t_agg")
        t_x2 = sem("t_x2")
        t_bn, t_v, t_ln, t_sq, t_nb = (sem(n) for n in ("t_bn", "t_v", "t_ln", "t_sq", "t_nb"))
        t_h = sem("t_h")
        t_tp = sem("t_tp")
        t_ht = sem("t_ht")
        t_up_ps = sem("t_up_ps")
        t_up = sem("t_up")
        t_st = [[sem(f"t_st{i}{s}") for s in range(2)] for i in range(2)]
        t_x2st = [sem(f"t_x2st{i}") for i in range(2)]
        CH = -(-(T // 2) // TC)
        s_clear = sem("s_clear")

        stage = work[:, :].rearrange("p (a s t d) -> p a s t d", a=3, s=2, t=TC)
        h2p, h2t, ups = stage[:, 0], stage[:, 1], stage[:, 2]
        PC = TC // 2

        def flat(ap):
            return ap.rearrange("p t d -> p (t d)")

        with nc.Block() as block:
            def store(sp, c):
                sp.wait_ge(t_ht, (c + 1) * PC)
                sp.dma_start(h2t_tab[:, c * TC * D:(c + 1) * TC * D],
                             h2t[:, c % 2].rearrange("p t d -> p (t d)")).then_inc(t_st[0][c % 2], 16)
                sp.wait_ge(t_up, (c + 1) * PC)
                sp.dma_start(rows(up_tab, c * TC, TC), ups[:, c % 2]).then_inc(t_st[1][c % 2], 16)

            @block.sync
            def _(sp):
                for c in range(NCH):
                    sp.wait_ge(t_x2, (c + 1) * PC)
                    sp.dma_start(rows(x2_tab, c * TC, TC), X[:, c * TC:(c + 1) * TC, :]).then_inc(t_x2st[c >= CH], 16)
                    if c >= 1:
                        store(sp, c - 1)
                store(sp, NCH - 1)
                sp.wait_ge(t_x2st[0], 16 * CH)
                sp.wait_ge(t_x2st[1], 16 * (NCH - CH))
                for i in range(2):
                    for s in range(2):
                        sp.wait_ge(t_st[i][s], 16 * ((NCH + 1 - s) // 2))

            @block.gpsimd
            def _(pool):
                pool.wait_ge(t_nb, CH)
                pool.wait_ge(t_h, 2 * TC * CH)
                pool.wait_ge(t_x2st[0], 16 * CH)
                nc.gpsimd.memset(acc[:, 2, :], 0.0).then_inc(s_clear, 1)
                pool.wait_ge(t_agg, T // 2)
                nc.gpsimd.memset(acc[:, 0:2, :], 0.0).then_inc(s_clear, 1)

            @block.tensor
            def _(pe):
                def neighbors(c):
                    for n in range(PC):
                        pair = c * PC + n
                        if pair >= 2:
                            pe.wait_ge(t_x2, pair - 1)
                        for half in range(2):
                            for k in range(2):
                                mm = nc.tensor.matmul(ps[:, pair % 2, half * D:(half + 1) * D],
                                                      acc[:, k, ds((pair * 2 + half) * P, P)], wn_sb[:, k, :],
                                                      start=(k == 0), stop=(k == 1))
                        mm.then_inc(t_agg, 1)

                neighbors(0)
                for c in range(NCH):
                    if c + 1 < NCH:
                        neighbors(c + 1)
                    for n in range(PC + 1):
                        if n < PC:
                            pair = c * PC + n
                            pe.wait_ge(t_h, pair * 4 + 4)
                            if pair >= 2:
                                pe.wait_ge(t_ht, pair - 1)
                            for m in range(4):
                                mm = nc.tensor.transpose(ps[:, 2 + pair % 2, m * P:(m + 1) * P],
                                                         h2p[:, c % 2, 2 * n + m // 2, (m % 2) * P:(m % 2 + 1) * P], ident[:, :])
                            mm.then_inc(t_tp, 1)
                        if n >= 1:
                            pair = c * PC + n - 1
                            pe.wait_ge(t_ht, pair + 1)
                            if pair >= 2:
                                pe.wait_ge(t_up, pair - 1)
                            for m in range(4):
                                mm = nc.tensor.matmul(ps[:, 4 + pair % 2, m * P:(m + 1) * P],
                                                      h2t[:, c % 2, 2 * n - 2 + m // 2, (m % 2) * P:(m % 2 + 1) * P], up_sb[:, m % 2, :],
                                                      start=True, stop=True)
                            mm.then_inc(t_up_ps, 1)

            @block.vector
            def _(dve):
                count = [0]

                def step(ins):
                    count[0] += 1
                    ins.then_inc(t_v, 1)
                    dve.wait_ge(t_v, count[0])

                nc.vector.memset(X[:, T - 1, :], 0.0).then_inc(t_clr, 1)
                nc.vector.memset(small[:, 0:1], 0.0).then_inc(t_clr, 1)
                dve.wait_ge(t_clr, 2)
                nc.vector.memset(small[0:LAST, 0:1], 1.0).then_inc(t_clr, 1)
                dve.wait_ge(t_clr, 3)
                nc.vector.tensor_scalar(X[:, T - 2, :], X[:, T - 2, :], small[:, 0:1], None, ALU.mult).then_inc(t_clr, 1)
                nc.vector.tensor_scalar(m4_sb[:, :, 2, :], m4_sb[:, :, 2, :], 3.0 ** -0.5, None, ALU.mult).then_inc(t_clr, 1)
                dve.wait_ge(t_clr, 5)

                def x2_of(c):
                    for n in range(PC + 1):
                        if n < PC:
                            pair = c * PC + n
                            dve.wait_ge(t_agg, pair + 1)
                            xt = flat(X[:, 2 * pair:2 * pair + 2, :])
                            nc.vector.tensor_tensor(xt, xt, ps[:, pair % 2, :], ALU.add).then_inc(t_x2, 1)
                        if n >= 1:
                            pair = c * PC + n - 1
                            dve.wait_ge(t_x2, pair + 1)
                            for t in (2 * pair, 2 * pair + 1):
                                nc.vector.bn_stats(mv[:, t, :], X[:, t, :]).then_inc(t_bn, 1)
                    dve.wait_ge(t_bn, (c + 1) * TC)
                    if c >= 1:
                        dve.wait_ge(t_nb, c)
                    ln_stats(c, step, t_ln)

                def ups_of(c):
                    if c >= 2:
                        dve.wait_ge(t_st[1][c % 2], 16 * (c // 2))
                    for n in range(PC):
                        pair = c * PC + n
                        dve.wait_ge(t_up_ps, pair + 1)
                        nc.vector.tensor_copy(flat(ups[:, c % 2, 2 * n:2 * n + 2, :]), ps[:, 4 + pair % 2, :]).then_inc(t_up, 1)

                for c in range(NCH + 1):
                    if c < NCH:
                        x2_of(c)
                        dve.wait_ge(t_sq, c + 1)
                        ln_scale(c, step, t_nb)
                    if c >= 1:
                        ups_of(c - 1)

            @block.scalar
            def _(act):
                def deviation(c):
                    act.wait_ge(t_ln, c + 1)
                    nc.scalar.activation(rstd[:, c * TC:(c + 1) * TC], lnt[:, 5, :], ACT.Sqrt, bias=eps_sb[:, 0:1],
                                         scale=1.0 / D).then_inc(t_sq, 1)

                deviation(0)
                for c in range(NCH):
                    t0 = c * TC
                    act.wait_ge(t_nb, c + 1)
                    if c >= 2:
                        act.wait_ge(t_tp, (c - 1) * PC)
                    for i in range(TC):
                        xt, ht = X[:, t0 + i, :], h2p[:, c % 2, i, :]
                        how = dict(bias=nbias[:, t0 + i:t0 + i + 1], scale=rstd[:, t0 + i:t0 + i + 1])
                        nc.scalar.activation(ht[:, 0:C], xt[:, 0:C], ACT.Relu, **how).then_inc(t_h, 1)
                        nc.scalar.activation(ht[:, C:D].rearrange("p (v c) -> p c v", v=3),
                                             xt[:, C:D].rearrange("p (c v) -> p c v", v=3), ACT.Relu, **how).then_inc(t_h, 1)
                    if c + 1 < NCH:
                        deviation(c + 1)
                    if c >= 2:
                        act.wait_ge(t_st[0][c % 2], 16 * (c // 2))
                        act.wait_ge(t_up_ps, (c - 1) * PC)
                    for n in range(PC):
                        pair = c * PC + n
                        act.wait_ge(t_tp, pair + 1)
                        nc.scalar.activation(flat(h2t[:, c % 2, 2 * n:2 * n + 2, :]), ps[:, 2 + pair % 2, :], ACT.Copy).then_inc(t_ht, 1)

        S3 = edge_syms(3)
        t_ready = [[sem(f"t_ready{s}{j}") for j in range(2)] for s in range(2)]
        S3["rad_used"] = [t_ready[s][1] for s in range(2)]
        prods = [[sem(f"prods{s}{j}") for j in range(2)] for s in range(2)]
        scaled = [[sem(f"scaled{s}{j}") for j in range(2)] for s in range(2)]
        y_part = sem("y_part")
        y_ready = [sem(f"y_ready{j}") for j in range(2)]
        add_one = sem("add_below")

        with nc.Block() as block:
            @block.sync
            def _(sp):
                load_units(sp, 1, S3, ((dsti, dst_u), (sh, a4_u)),
                           lambda u: r3_tab[ds(u, 1), :, :].rearrange("o p n -> (o p) n"), lambda s: r3[:, s, :],
                           [S3["hot"], [scaled[s][1] for s in range(2)]])

            @block.gpsimd
            def _(pool):
                gather_units(pool, 1, S3, up_tab, prods, 3)

            @block.scalar
            def _(act):
                with act.Fori(0, passes(act, 1)) as pz:
                    act.wait_ge(S3["fresh"], pz)
                    with act.Fori(0, ROUNDS) as k:
                        for s in range(2):
                            for j in range(2):
                                use, gu = pz * ROUNDS + k, pz * NU + k * 2 + s
                                if j == 0:
                                    act.wait_ge(S3["edge"][s], use * 32 + 32)
                                act.wait_ge(S3["got"][s][j], k * (16 * G) + 16 * G)
                                act.wait_ge(y_ready[j], gu)
                                for g in range(G):
                                    q = j * G + g
                                    for v in range(3):
                                        a = 4 * q + v + 1
                                        last = nc.scalar.activation(x1s[:, j, v, g, :], rows_g[:, s, q, (v + 1) * C:(v + 2) * C],
                                                                    ACT.Copy, scale=sh[:, s, a:a + 1])
                                last.then_inc(scaled[s][j], 1)
                    act.sem_inc(S3["settled"], 1)

            @block.tensor
            def _(pe):
                def radial(s, j, use):
                    if j == 0:
                        pe.wait_ge(S3["rad"][s], use * 16 + 16)
                    pe.wait_ge(prods[1 - s][j], use + s)
                    for g in range(G):
                        n = 2 * j + g // 2
                        mm = nc.tensor.matmul(ps[:, 2 * j + g // 2, (g % 2) * D:(g % 2 + 1) * D], r3[:, s, n * P:(n + 1) * P],
                                              m4_sb[:, g % 2, :, :].rearrange("p b c -> p (b c)"), start=True, stop=True)
                    mm.then_inc(t_ready[s][j], 1)

                def sums(s, j, use, gu):
                    pe.wait_ge(prods[s][j], use + 1)
                    if j == 0:
                        pe.wait_ge(S3["hot"][s], use + 1)
                    pe.wait_ge(S3["added"][j], gu)
                    bank = ps[:, 6 + j, :]
                    for g in range(G):
                        hot = onehot[:, s, j * G + g, :, :]
                        pair = prod[:, j, g, :, :].rearrange("p (b two) c -> p b (two c)", two=2)
                        nc.tensor.matmul(bank[:, 0:4 * W], pair[:, 2, :], hot[:, 1:5, :].rearrange("p a w -> p (a w)"),
                                         start=(g == 0), stop=False)
                        nc.tensor.matmul(bank[:, 4 * W:5 * W], pair[:, 0, :], hot[:, 0, :], start=False, stop=False)
                        mm = nc.tensor.matmul(bank[:, 5 * W:6 * W], pair[:, 1, :], hot[:, 0, :], start=False, stop=(g == G - 1))
                    mm.then_inc(S3["summed"][s][j], 1)

                with pe.Fori(0, passes(pe, 1)) as pz:
                    radial(0, 0, pz * ROUNDS)
                    with pe.Fori(0, ROUNDS - 1) as k:
                        for s in range(2):
                            for j in range(2):
                                use, gu = pz * ROUNDS + k, pz * NU + k * 2 + s
                                s1, j1 = (s, 1) if j == 0 else (1 - s, 0)
                                radial(s1, j1, use + (s if j else 0))
                                sums(s, j, use, gu)
                    for s in range(2):
                        for j in range(2):
                            use, gu = pz * ROUNDS + (ROUNDS - 1), pz * NU + (NU - 2 + s)
                            if (s, j) != (1, 1):
                                s1, j1 = (s, 1) if j == 0 else (1 - s, 0)
                                radial(s1, j1, use + (s if j else 0))
                            sums(s, j, use, gu)

            @block.vector
            def _(dve):
                first_base(dve, S3, 1)
                with dve.Fori(0, passes(dve, 1)) as pz:
                    dve.wait_ge(S3["fresh"], pz)
                    def products(s, j, k, use, gu):
                        t = ps[:, 2 * j:2 * j + 2, :].rearrange("p a (g b c) -> p (a g) b c", g=2, b=4)
                        up = rows_g[:, s, j * G:(j + 1) * G, :].rearrange("p g (b c) -> p g b c", b=4)
                        to = prod[:, j, :, :, :]
                        dve.wait_ge(scaled[s][j], use + 1)
                        dve.wait_ge(prods[(s + 1 - j) % 2][1 - j], use + (s if j == 0 else 1))
                        nc.vector.tensor_tensor(y, x1s[:, j, 0], x1s[:, j, 1], ALU.add).then_inc(y_part, 1)
                        dve.wait_ge(t_ready[s][j], use + 1)
                        dve.wait_ge(S3["got"][s][j], k * (16 * G) + 16 * G)
                        dve.wait_ge(S3["summed"][1 - s][j], use + s)
                        nc.vector.tensor_tensor(to[:, :, 0:6:5, :], t[:, :, 0:2, :], bc(up[:, :, 0, :], 2, 2), ALU.mult)
                        dve.wait_ge(y_part, gu * 2 + (j + 1))
                        nc.vector.tensor_tensor(y, y, x1s[:, j, 2], ALU.add).then_inc(y_ready[j], 1)
                        nc.vector.tensor_tensor(to[:, :, 1:4, :], bc(t[:, :, 3, :], 2, 3), up[:, :, 1:4, :], ALU.mult)
                        dve.wait_ge(y_ready[j], gu + 1)
                        nc.vector.tensor_tensor(to[:, :, 4, :], t[:, :, 2, :], y, ALU.mult).then_inc(prods[s][j], 1)

                    def add_window(u, use, gu, s, j):
                        b = dve.value_load(base_i[0:1, ds(u * 2 + j, 1)], min_val=0, max_val=N - 1)
                        dve.wait_ge(S3["summed"][s][j], use + 1)
                        dve.wait_ge(S3["added"][1 - j], gu + j)
                        sums = ps[:, 6 + j, 0:6 * W].rearrange("p (q w) -> p q w", q=6)
                        below, m0, both = acc[C:P, 0:3, ds(b, W)], acc[0:C, 0, ds(b, W)], acc[:, 0:3:2, ds(b, W)]
                        nc.vector.tensor_tensor(below, below, sums[C:P, 0:3, :], ALU.add).then_inc(add_one, 1)
                        nc.vector.tensor_tensor(m0, m0, sums[0:C, 3, :], ALU.add).then_inc(add_one, 1)
                        dve.wait_ge(add_one, gu * 4 + (2 * j + 2))
                        nc.vector.tensor_tensor(both, both, sums[:, 4:6, :], ALU.add).then_inc(S3["added"][j], 1)

                    def unit(k, s, first=False, last=False):
                        use, gu = pz * ROUNDS + k, pz * NU + k * 2 + s
                        if not last:
                            rel_, eq_, hot_ = hot_steps(dve, S3, k * 2 + s + 1, use + s, 1 - s, 1)
                            rel_()
                        products(s, 0, k, use, gu)
                        if not first:
                            add_window(k * 2 + s - 1, use - (1 - s), gu - 1, 1 - s, 1)
                        if not last:
                            eq_(gu + 1)
                        products(s, 1, k, use, gu)
                        if not last:
                            hot_(gu + 1)
                        add_window(k * 2 + s, use, gu, s, 0)

                    rel_, eq_, hot_ = hot_steps(dve, S3, 0, pz * ROUNDS, 0, 1)
                    rel_()
                    eq_(pz * NU)
                    hot_(pz * NU)
                    unit(0, 0, first=True)
                    unit(0, 1)
                    with dve.Fori(1, ROUNDS - 1) as k:
                        for s in range(2):
                            unit(k, s)
                    unit(ROUNDS - 1, 0)
                    unit(ROUNDS - 1, 1, last=True)
                    add_window(NU - 1, pz * ROUNDS + (ROUNDS - 1), pz * NU + (NU - 1), 1, 1)
                    dve.sem_inc(S3["settled"], 1)
                    dve.wait_ge(S3["added"][1], pz * NU + NU)
                    set_base(dve, S3, 1, pz)

        X2 = work[:, 0:T * D].rearrange("p (t d) -> p t d", d=D)
        spare = work[:, T * D:]
        el = [mlp, spare]
        a0 = [e[:, 0:BN] for e in el]
        sq = [e[:, BN:4 * BN].rearrange("p (v n) -> p v n", v=3) for e in el]
        hu = [e[:, 4 * BN:5 * BN] for e in el]
        hw = [e[:, 5 * BN:6 * BN] for e in el]
        hp = [e[:, 6 * BN:7 * BN] for e in el]
        h2s = mlp[:, 0:4 * D].rearrange("p (s h d) -> p s h d", s=2, h=2)
        osq = spare[:, 0:12 * C].rearrange("p (s h d) -> p s h d", s=2, h=2)
        tot = mlp[:, 4 * D:4 * D + 8 * C].rearrange("p (h d) -> p h d", h=2)
        par = mlp[:, 1536:1536 + 2 * C].rearrange("p (a c) -> p a c", a=2)
        mean = mlp[:, 1664:1664 + C]
        stat = mlp[:, 1728:1728 + 2 * C].rearrange("p (a c) -> p a c", a=2)
        scl = mlp[:, 1856:1856 + D].rearrange("p (q c) -> p q c", q=4)
        O = acc[:, :, HN:].rearrange("p q (t h c) -> p q t h c", t=H, h=2)
        O0 = acc[:, 0, HN:].rearrange("p (n c) -> p n c", c=C)
        xsq = acc[:, 1, 0:HN]
        NB = HN // BN
        TH = H // NCH

        u_x2 = sem("u_x2")
        u_beta = sem("u_beta")
        u_lin = [sem(f"u_lin{s}") for s in range(2)]
        u_in = [sem(f"u_in{s}") for s in range(2)]
        u_el = [sem(f"u_el{s}") for s in range(2)]
        u_h2 = [sem(f"u_h2{s}") for s in range(2)]
        u_o = [sem(f"u_o{s}") for s in range(2)]
        u_cp = [sem(f"u_cp{s}") for s in range(2)]
        u_ad = [sem(f"u_ad{s}") for s in range(2)]
        u_z = sem("u_z")
        u_v = sem("u_v")
        u_par = sem("u_par")
        u_mean = sem("u_mean")
        u_xc = sem("u_xc")
        u_xsq = sem("u_xsq")
        u_var = sem("u_var")
        u_st = sem("u_st")
        u_rt = sem("u_rt")
        u_fin = sem("u_fin")
        u_fin1 = sem("u_fin1")
        u_out = sem("u_out")

        h2v = h2t_tab.rearrange("p (h t d) -> p h t d", h=2, d=D)

        groups = [(n, h) for n in range(NCH) for h in range(2)]
        POOL = 3
        u_scl1 = sem("u_scl1")
        u_prod = sem("u_prod")
        u_prod_pool = sem("u_prod_pool")
        u_fin_pool = sem("u_fin_pool")
        prods_done = {u_prod: 0, u_prod_pool: 0}

        def add_parts(eng, ops, some, q, done):
            made = u_prod_pool if ops is nc.gpsimd else u_prod

            def parts(n, h):
                o = O[:, q:q + 1 + 2 * q, TH * n:TH * n + TH, h, :]
                xt = X2[:, h * H + TH * n:h * H + TH * n + TH, :]
                return o, xt[:, :, 0:C].unsqueeze(1) if q == 0 else xt[:, :, C:D].rearrange("p t (c v) -> p v t c", v=3)

            for m in range(len(some) + 1):
                if m < len(some):
                    o, _ = parts(*some[m])
                    ops.tensor_tensor(o, o, bc(bc(scl[:, q, :], 1, TH), 1, 1 + 2 * q), ALU.mult).then_inc(made, 1)
                    prods_done[made] += 1
                if m >= 1:
                    o, xt = parts(*some[m - 1])
                    eng.wait_ge(made, prods_done[made] - (m < len(some)))
                    ops.tensor_tensor(xt, xt, o, ALU.add).then_inc(done, 1)

        with nc.Block() as block:
            @block.sync
            def _(sp):
                sp.dma_start(X2, rows(x2_tab, 0, T)).then_inc(u_x2, 16)

                def load(i, k, s):
                    sp.wait_ge(u_o[s], k)
                    sp.dma_start(h2s[:, s, :, :], h2v[:, :, ds(i, 1), :].rearrange("p h o d -> p (h o) d")).then_inc(u_h2[s], 16)

                for s in range(2):
                    sp.wait_ge(u_el[s], 9 * NB // 2)
                with sp.Fori(0, H // 2) as k:
                    for s in range(2):
                        load(k * 2 + s, k, s)
                load(H - 1, H // 2, 0)
                stores = 1
                for n in range(NCH):
                    for h in range(2):
                        i = 2 * n + h
                        pooled = min(max(i + 1 - NCH, 0), POOL)
                        if pooled:
                            sp.wait_ge(u_fin_pool, pooled)
                        sp.wait_ge(u_fin1, i + 1 - pooled)
                        sp.wait_ge(u_fin, i + 1)
                        t = h * H + n * TH
                        m = min(TH, T - 2 - t)
                        if m > 0:
                            stores += 1
                            sp.dma_start(out[t * P:(t + m) * P, :].rearrange("(t p) d -> p t d", p=P), X2[:, t:t + m, :]).then_inc(u_out, 16)
                sp.dma_start(out[(T - 2) * P:N, :], X2[0:LAST, T - 2, :]).then_inc(u_out, 16)
                sp.wait_ge(u_out, 16 * stores)

            @block.gpsimd
            def _(pool):
                pool.wait_ge(u_x2, 16)
                nc.gpsimd.tensor_tensor(X2[:, :, 0:C], X2[:, :, 0:C], bc(gb_sb[:, 1, :], 1, T), ALU.add).then_inc(u_beta, 1)
                pool.wait_ge(u_scl1, 1)
                add_parts(pool, nc.gpsimd, groups[NCH:NCH + POOL], 1, u_fin_pool)

            @block.tensor
            def _(pe):
                with pe.Fori(0, NB // 2) as k:
                    for s in range(2):
                        n = (k * 2 + s) * BN
                        pe.wait_ge(u_el[s], k * 9)
                        for q, parts in enumerate((((0, 0),), ((0, 1),), ((1, 1), (2, 2)), ((2, 1),))):
                            for h in range(2):
                                for b, wl in parts:
                                    mm = nc.tensor.matmul(ps[:, 4 * s + q, 0:BN], lin_sb[:, wl, h, :], acc[:, b, ds(n + h * HN, BN)],
                                                          start=(h == 0 and (b, wl) == parts[0]), stop=(h == 1 and (b, wl) == parts[-1]))
                        mm.then_inc(u_lin[s], 1)
                for s in range(2):
                    pe.wait_ge(u_el[s], 9 * NB // 2)

                def pair(i, k, s):
                    o = ps[:, s, :].rearrange("p (h d) -> p h d", h=2)
                    pe.wait_ge(u_cp[s], k * 2)
                    for q in range(4):
                        nc.tensor.matmul(o[:, :, q * C:(q + 1) * C], acc[:, q, ds(i * P, P)], wb_sb[:, min(q, 1), :],
                                         start=(q == 0), stop=False)
                    pe.wait_ge(u_h2[s], k * 16 + 16)
                    for h in range(2):
                        for b in range(2):
                            mm = nc.tensor.matmul(o[:, h, b * P:(b + 1) * P], h2s[:, s, h, b * P:(b + 1) * P], sc_sb[:, b, :],
                                                  start=False, stop=(h == 1 and b == 1))
                    mm.then_inc(u_o[s], 1)

                for k in range(H // 2):
                    for s in range(2):
                        pair(k * 2 + s, k, s)
                pair(H - 1, H // 2, 0)
                pe.wait_ge(u_par, 1)
                nc.tensor.matmul(ps[:, 4, 0:C], ones[:, :], par[:, 0, :], start=True, stop=True).then_inc(u_mean, 1)
                pe.wait_ge(u_par, 2)
                nc.tensor.matmul(ps[:, 5, 0:C], ones[:, :], par[:, 1, :], start=True, stop=True).then_inc(u_var, 1)
                pe.wait_ge(u_par, 3)
                nc.tensor.matmul(ps[:, 6, 0:C], ones[:, :], par[:, 0, :], start=True, stop=True).then_inc(u_var, 1)

            @block.scalar
            def _(act):
                with act.Fori(0, NB // 2) as k:
                    for s in range(2):
                        act.wait_ge(u_lin[s], k + 1)
                        act.wait_ge(u_el[s], k * 9)
                        b = 4 * s

                        def line(to, slope, offset):
                            nc.scalar.activation(to, ps[:, b, 0:BN], ACT.Identity, scale=wc_sb[:, slope:slope + 1],
                                                 bias=wc_sb[:, offset:offset + 1]).then_inc(u_in[s], 1)

                        nc.scalar.activation(a0[s], ps[:, b, 0:BN], ACT.Copy).then_inc(u_in[s], 1)
                        line(hu[s], 3, 1)
                        line(hp[s], 7, 6)
                        nc.scalar.activation(sq[s], ps[:, b + 1:b + 4, 0:BN], ACT.Square).then_inc(u_in[s], 1)
                        line(hw[s], 4, 2)

                for s in range(2):
                    act.wait_ge(u_el[s], 9 * NB // 2)

                def pair(i, k, s):
                    o = ps[:, s, :].rearrange("p (h q c) -> p q h c", h=2, q=4)
                    act.wait_ge(u_o[s], k + 1)
                    act.wait_ge(u_ad[s], k * 2)
                    nc.scalar.activation(osq[:, s, :, :], ps[:, s, :].rearrange("p (h d) -> p h d", h=2)[:, :, C:D],
                                         ACT.Square).then_inc(u_cp[s], 1)
                    nc.scalar.activation(O[:, :, ds(i, 1), :, :].rearrange("p q o h c -> p (q o) h c"), o, ACT.Copy).then_inc(u_cp[s], 1)

                with act.Fori(0, H // 2) as k:
                    for s in range(2):
                        pair(k * 2 + s, k, s)
                pair(H - 1, H // 2, 0)
                act.wait_ge(u_st, 1)
                nc.scalar.activation(stat[:, 1, :], stat[:, 1, :], ACT.Sqrt, bias=eps_sb[:, 0:1]).then_inc(u_rt, 1)
                act.wait_ge(u_xc, 1)
                nc.scalar.activation(xsq, acc[:, 0, HN:], ACT.Square).then_inc(u_xsq, 1)
                act.wait_ge(u_st, 2)
                nc.scalar.activation(stat[:, 0, :], stat[:, 0, :], ACT.Sqrt, bias=eps_sb[:, 0:1]).then_inc(u_rt, 1)

            @block.vector
            def _(dve):
                with dve.Fori(0, NB // 2) as k:
                    for s in range(2):
                        b = 4 * s
                        L = ds((k * 2 + s) * BN, BN)

                        def after(m):
                            dve.wait_ge(u_el[s], k * 9 + m)

                        vv, gq = sq[s][:, 0, :], sq[s][:, 1, :]
                        dve.wait_ge(u_in[s], k * 5 + 2)
                        nc.vector.tensor_tensor(hu[s], hu[s], a0[s], ALU.mult).then_inc(u_el[s], 1)
                        dve.wait_ge(u_in[s], k * 5 + 3)
                        nc.vector.tensor_tensor(hp[s], hp[s], a0[s], ALU.mult).then_inc(u_el[s], 1)
                        after(1)
                        nc.vector.scalar_tensor_tensor(out=hu[s], in0=hu[s], scalar=wc_sb[:, 0:1], in1=a0[s],
                                                       op0=ALU.add, op1=ALU.mult).then_inc(u_el[s], 1)
                        dve.wait_ge(u_in[s], k * 5 + 4)
                        nc.vector.tensor_tensor(vv, vv, sq[s][:, 1, :], ALU.add).then_inc(u_el[s], 1)
                        after(4)
                        nc.vector.tensor_tensor(vv, vv, sq[s][:, 2, :], ALU.add).then_inc(u_el[s], 1)
                        dve.wait_ge(u_in[s], k * 5 + 5)
                        after(5)
                        nc.vector.tensor_tensor(hw[s], hw[s], vv, ALU.mult).then_inc(u_el[s], 1)
                        nc.vector.scalar_tensor_tensor(out=gq, in0=vv, scalar=wc_sb[:, 8:9], in1=hp[s],
                                                       op0=ALU.mult, op1=ALU.add).then_inc(u_el[s], 1)
                        after(6)
                        nc.vector.tensor_tensor(acc[:, 0, L], hu[s], hw[s], ALU.add).then_inc(u_el[s], 1)
                        after(7)
                        nc.vector.scalar_tensor_tensor(out=acc[:, 1:4, L], in0=bc(gq, 1, 3), scalar=wc_sb[:, 5:6],
                                                       in1=ps[:, b + 1:b + 4, 0:BN], op0=ALU.add, op1=ALU.mult).then_inc(u_el[s], 1)
                for s in range(2):
                    dve.wait_ge(u_el[s], 9 * NB // 2)
                nc.vector.memset(tot[:, :, :], 0.0).then_inc(u_z, 1)
                dve.wait_ge(u_z, 1)

                def pair(i, k, s):
                    dve.wait_ge(u_cp[s], k * 2 + 2)
                    dve.wait_ge(u_ad[1 - s], k * 2 + 2 * s)
                    nc.vector.tensor_tensor(tot[:, :, 0:C], tot[:, :, 0:C],
                                            O[:, 0, ds(i, 1), :, :].rearrange("p o h c -> p (o h) c"), ALU.add).then_inc(u_ad[s], 1)
                    nc.vector.tensor_tensor(tot[:, :, C:D], tot[:, :, C:D], osq[:, s, :, :], ALU.add).then_inc(u_ad[s], 1)

                with dve.Fori(0, H // 2) as k:
                    for s in range(2):
                        pair(k * 2 + s, k, s)
                pair(H - 1, H // 2, 0)
                dve.wait_ge(u_ad[0], 2 * (H // 2) + 2)
                dve.wait_ge(u_cp[0], 2 * (H // 2) + 2)
                dve.wait_ge(u_cp[1], 2 * (H // 2))
                count = [0]

                def step(ins):
                    count[0] += 1
                    ins.then_inc(u_v, 1)
                    dve.wait_ge(u_v, count[0])

                nc.vector.tensor_tensor(par[:, 0, :], tot[:, 0, 0:C], tot[:, 1, 0:C], ALU.add).then_inc(u_par, 1)
                step(nc.vector.tensor_tensor(tot[:, 0, C:D], tot[:, 0, C:D], tot[:, 1, C:D], ALU.add))
                nc.vector.tensor_reduce(par[:, 1, :], tot[:, 0, C:D].rearrange("p (v c) -> p c v", v=3), AX_X, ALU.add).then_inc(u_par, 1)
                dve.wait_ge(u_par, 2)
                dve.wait_ge(u_mean, 1)
                nc.vector.tensor_scalar(mean, ps[:, 4, 0:C], 1.0 / N, None, ALU.mult).then_inc(u_v, 1)
                count[0] += 1
                dve.wait_ge(u_var, 1)
                nc.vector.tensor_scalar(stat[:, 1, :], ps[:, 5, 0:C], 1.0 / (3 * N), None, ALU.mult).then_inc(u_st, 1)
                dve.wait_ge(u_v, count[0])
                step(nc.vector.tensor_tensor(O0, O0, bc(mean, 1, T), ALU.subtract))
                step(nc.vector.memset(O[:, 0, H - 1, 1, :], 0.0))
                nc.vector.tensor_scalar(O[:, 0, H - 2, 1, :], O[:, 0, H - 2, 1, :], small[:, 0:1], None, ALU.mult).then_inc(u_xc, 1)
                dve.wait_ge(u_rt, 1)
                step(nc.vector.reciprocal(stat[:, 1, :], stat[:, 1, :]))
                nc.vector.tensor_tensor(scl[:, 1, :], stat[:, 1, :], gb_sb[:, 2, :], ALU.mult).then_inc(u_scl1, 1)
                dve.wait_ge(u_scl1, 1)
                dve.wait_ge(u_x2, 16)
                dve.wait_ge(u_beta, 1)
                add_parts(dve, nc.vector, groups[0:2], 1, u_fin1)
                dve.wait_ge(u_xsq, 1)
                nc.vector.tensor_reduce(par[:, 0, :], xsq.rearrange("p (n c) -> p c n", c=C), AX_X, ALU.add).then_inc(u_par, 1)
                add_parts(dve, nc.vector, groups[2:3], 1, u_fin1)
                dve.wait_ge(u_var, 2)
                nc.vector.tensor_scalar(stat[:, 0, :], ps[:, 6, 0:C], 1.0 / N, None, ALU.mult).then_inc(u_st, 1)
                add_parts(dve, nc.vector, groups[3:4], 1, u_fin1)
                dve.wait_ge(u_rt, 2)
                step(nc.vector.reciprocal(stat[:, 0, :], stat[:, 0, :]))
                step(nc.vector.tensor_tensor(scl[:, 0, :], stat[:, 0, :], gb_sb[:, 0, :], ALU.mult))
                add_parts(dve, nc.vector, groups[0:4], 0, u_fin)
                for i, group in enumerate(groups[4:], 4):
                    if not NCH <= i < NCH + POOL:
                        add_parts(dve, nc.vector, [group], 1, u_fin1)
                    add_parts(dve, nc.vector, [group], 0, u_fin)


_INS = (("x", "x"), ("src", "src"), ("dst", "dst"), ("attr16", "edge_attr_16"), ("attr4", "edge_attr_4"), ("weight", "edge_weight"),
        ("w_self", "L0_gnn_W_self"), ("w_nb", "L0_gnn_W_neighbor"), ("bias", "L0_gnn_bias"), ("w_up0", "L1_gnn_W_up0"),
        ("w_up1", "L1_gnn_W_up1"), ("m1", "L1_gnn_M1"), ("m2", "L1_gnn_M2"), ("m3", "L1_gnn_M3"), ("m4", "L1_gnn_M4"),
        ("w_lin0", "L1_gnn_W_lin0"), ("w_lin1", "L1_gnn_W_lin1"), ("w_sc0", "L1_gnn_Wsc0"), ("w_sc1", "L1_gnn_Wsc1"),
        ("wc0", "L1_gnn_Wc0"), ("wc1", "L1_gnn_Wc1"), ("w_b0", "L1_gnn_WB0"), ("w_b1", "L1_gnn_WB1"),
        ("gamma0", "L1_gnn_gamma0"), ("beta0", "L1_gnn_beta0"), ("gamma1", "L1_gnn_gamma1"))


def kernel(**inputs):
    import numpy as np
    import concourse.bacc as bacc
    from concourse.bass_utils import run_bass_kernel_spmd

    nc = bacc.Bacc("TRN2", target_bir_lowering=False, num_devices=1)
    arrays, args = {}, {}
    for arg, name in _INS:
        a = np.ascontiguousarray(inputs[name])
        arrays["in_" + name] = a
        args[arg] = nc.dram_tensor("in_" + name, a.shape, mybir.dt.from_np(a.dtype), kind="ExternalInput").ap()
    args["out"] = nc.dram_tensor("out_0", (N, D), F32, kind="ExternalOutput").ap()
    build(nc, **args)
    r = run_bass_kernel_spmd(nc, [arrays], core_ids=[0])
    return r.results[0]["out_0"]
```

```python
from contextlib import ExitStack

import concourse.bass as bass
from concourse import mybir

F32 = mybir.dt.float32
I32 = mybir.dt.int32
BF16 = mybir.dt.bfloat16
ALU = mybir.AluOpType
ACT = mybir.ActivationFunctionType
AX_X = mybir.AxisListType.X
ds = bass.ds

P = 128
N = 6250
E = 206250
D = 256
C = 64
R = 16
EPS = 1e-5

G = 4
SC = P * G
NU = -(-E // (2 * SC))
NSC = 2 * NU
EPAD = NU * 2 * SC
ETAIL = E - (NU - 1) * 2 * SC
ROUNDS = NU // 2
SROWS = NSC // 4
WU = 128
W = 32

T = 50
NPAD = T * P
LAST = N - (T - 2) * P
NCH = 5
TC = T // NCH
H = T // 2
HN = H * P
NT = T - 1
PAIRS = (2, 4, 4, 4, 4, 4, 2, 1)
BN = 320
assert sum(PAIRS) * 2 == T and max(PAIRS) * 2 <= TC
assert T == NCH * TC and TC % 2 == 0 and 0 < LAST < P and NT < ROUNDS - 1
assert NU % 2 == 0 and SROWS * 4 == NSC and SC // 2 < ETAIL < SC


def bc(ap, axis, n):
    ap = ap.unsqueeze(axis)
    shape = list(ap.shape)
    shape[axis] = n
    return ap.to_broadcast(shape)


def build(nc, x, src, dst, attr16, attr4, weight, w_self, w_nb, bias, w_up0, w_up1, m1, m2, m3, m4,
          w_lin0, w_lin1, w_sc0, w_sc1, wc0, wc1, w_b0, w_b1, gamma0, beta0, gamma1, out):
    h_tab = nc.dram_tensor("h_tab", [NPAD, D], F32).ap()
    up_tab = nc.dram_tensor("up_tab", [NPAD, D], F32).ap()
    x2_tab = nc.dram_tensor("x2_tab", [NPAD, D], F32).ap()
    h2t_tab = nc.dram_tensor("h2t_tab", [P, T * D], F32).ap()
    r12_tab = nc.dram_tensor("r12_tab", [NU, P, 8 * P], BF16).ap()
    rlow_tab = nc.dram_tensor("rlow_tab", [NU, C, 8 * P], BF16).ap()
    src_tail = nc.dram_tensor("src_tail", [2 * SC], I32).ap()
    dst_tail = nc.dram_tensor("dst_tail", [2 * SC], I32).ap()
    w_tail = nc.dram_tensor("w_tail", [2 * SC], F32).ap()
    a4_tail = nc.dram_tensor("a4_tail", [2 * SC, 4], F32).ap()
    a16_tail = nc.dram_tensor("a16_tail", [2 * SC, R], F32).ap()
    tails = ((src_tail, src), (dst_tail, dst), (w_tail, weight), (a4_tail, attr4), (a16_tail, attr16))

    E0 = (NU - 1) * 2 * SC

    def units(full, tail):
        if len(full.shape) == 1:
            return (full[0:E0].rearrange("(u j p g) -> u p j g", j=2, p=P, g=G),
                    tail.rearrange("(j p g) -> p j g", j=2, p=P))
        return (full[0:E0, :].rearrange("(u j p g) f -> u p j (g f)", j=2, p=P, g=G),
                tail.rearrange("(j p g) f -> p j (g f)", j=2, p=P))

    src_u, dst_u, w_u = units(src, src_tail), units(dst, dst_tail), units(weight, w_tail)
    a4_u, a16_u = units(attr4, a4_tail), units(attr16, a16_tail)

    def unit_of(view, u):
        if isinstance(u, int) and u == NU - 1:
            return view[1]
        return view[0][ds(u, 1), :, :, :].rearrange("o p j g -> (o p) j g")

    def row(ap):
        return ap.rearrange("p o n -> p (o n)")

    def rows(tab, t, n):
        return tab[ds(t * P, n * P), :].rearrange("(t p) d -> p t d", p=P)

    with ExitStack() as ctx:
        def sb(name, shape, dt=F32):
            return ctx.enter_context(nc.sbuf_tensor(name, shape, dt))

        def sem(name):
            return ctx.enter_context(nc.semaphore(name))

        acc = sb("acc", [P, 4, NPAD])
        work = sb("work", [P, T * D + 2560])
        mlp = sb("mlp", [P, 2560])
        ident = sb("ident", [P, P])
        ones = sb("ones", [P, P])
        win = sb("win", [P, WU])
        ws_sb = sb("ws_sb", [P, 2, D])
        wn_sb = sb("wn_sb", [P, 2, D])
        bias_sb = sb("bias_sb", [1, D])
        m1_sb = sb("m1_sb", [P, 4, P])
        m2_sb = sb("m2_sb", [P, P])
        m3_sb = sb("m3_sb", [P, 2, P])
        m4_sb = sb("m4_sb", [P, 4, C])
        m4_split = sb("m4_split", [P, 3, D], BF16)
        up_sb = sb("up_sb", [P, 2, P])
        sc_sb = sb("sc_sb", [P, 2, P])
        lin_sb = sb("lin_sb", [P, 3, 2, P])
        wb_sb = sb("wb_sb", [P, 2, P])
        wc_sb = sb("wc_sb", [P, 9])
        gb_sb = sb("gb_sb", [P, 3, C])
        base0_i = sb("base0_i", [1, NSC], I32)
        base_i = sb("base_i", [1, NSC], I32)
        base0_f = sb("base0_f", [P, NSC])
        base_f = sb("base_f", [P, NSC])
        npass = sb("npass", [1, 2], I32)
        mv = sb("mv", [P, T, 6])
        lnt = sb("lnt", [P, 6, TC])
        rstd = sb("rstd", [P, T])
        nbias = sb("nbias", [P, T])
        eps_sb = sb("eps_sb", [P, 1])
        small = sb("small", [P, 32])
        ps = ctx.enter_context(nc.psum_tensor("ps", [P, 8, 512], F32))

        X = acc[:, 2:4, :].rearrange("p q n -> p (q n)").rearrange("p (t d) -> p t d", d=D)

        s_zx = sem("s_zx")
        s_zw = sem("s_zw")
        s_xin = [sem(f"s_xin{c}") for c in range(NCH)]
        s_wts = sem("s_wts")
        s_wts2 = sem("s_wts2")
        s_tail = sem("s_tail")
        s_chk_in = sem("s_chk_in")
        s_v0 = sem("s_v0")
        s_ln = sem("s_ln")
        s_sq = sem("s_sq")
        s_lnt = sem("s_lnt")
        s_nb = sem("s_nb")
        s_h = sem("s_h")
        s_hst = sem("s_hst")
        s_id = sem("s_id")
        s_acc0 = sem("s_acc0")
        s_bn = sem("s_bn")
        s_chk = sem("s_chk")
        s_chk_ps = sem("s_chk_ps")

        h_st = work[:, 0:T * D].rearrange("p (t d) -> p t d", d=D)
        chk = mlp[0:SROWS, 0:4 * SC].rearrange("p (q e) -> p q e", q=4)
        chk_i = chk.bitcast(I32)
        cst = work[:, T * D:T * D + 8 * R]
        neg = work[:, T * D + 8 * R:T * D + 8 * R + 8].bitcast(I32)
        win_i = work[:, T * D + 256:T * D + 256 + WU].bitcast(I32)

        wts = [(ws_sb[:, :, :], w_self.rearrange("(k p) n -> p k n", p=P)), (bias_sb[:, :], bias.unsqueeze(0))]
        for g in range(8):
            wts.append((m1_sb[g * R:(g + 1) * R, g // 2, (g % 2) * C:(g % 2 + 1) * C], m1))
        wts2 = [(wn_sb[:, :, :], w_nb.rearrange("(k p) n -> p k n", p=P))]
        m4v = m4.rearrange("h (b c) -> h b c", b=4)
        for lo in range(2):
            r = slice(lo * C, (lo + 1) * C)
            wts += [(m2_sb[r, r], m2), (m3_sb[r, lo, 0:C], m3), (m3_sb[r, lo, C:P], m3)]
            wts2 += [(m4_sb[r, 0:2, :], m4v[:, 0:2, :]), (m4_sb[r, 2, :], m4v[:, 3, :]), (m4_sb[r, 3, :], m4v[:, 2, :])]
            wts2 += [(up_sb[r, 0, r], (w_up0, w_up1)[lo]), (up_sb[r, 1, r], w_up1),
                     (sc_sb[r, 0, r], (w_sc0, w_sc1)[lo]), (sc_sb[r, 1, r], w_sc1),
                     (wb_sb[r, 0, r], w_b0), (wb_sb[r, 1, r], w_b1),
                     (lin_sb[0:C, 0, lo, r], w_lin0), (lin_sb[C:P, 1, lo, r], w_lin1), (lin_sb[0:C, 2, lo, r], w_lin1),
                     (wc_sb[r, 0:5], wc0), (wc_sb[r, 5:9], wc1)]
        for i, v in enumerate((gamma0, beta0, gamma1)):
            wts2.append((gb_sb[:, i, :], v.unsqueeze(0).to_broadcast([P, C])))

        def ln_stats(t0, n, step, done):
            st = mv[:, t0:t0 + n, :]
            nc.vector.tensor_tensor(lnt[:, 0, 0:n], st[:, :, 1], st[:, :, 4], ALU.add).then_inc(s_lnt, 1)
            nc.vector.tensor_tensor(lnt[:, 2, 0:n], st[:, :, 2], st[:, :, 5], ALU.add).then_inc(s_lnt, 1)
            step(nc.vector.tensor_tensor(lnt[:, 1, 0:n], st[:, :, 1], st[:, :, 4], ALU.subtract))
            step(nc.vector.tensor_tensor(lnt[:, 3, 0:n], lnt[:, 1, 0:n], lnt[:, 1, 0:n], ALU.mult))
            nc.vector.scalar_tensor_tensor(out=lnt[:, 5, 0:n], in0=lnt[:, 3, 0:n], scalar=float(D) / 4, in1=lnt[:, 2, 0:n],
                                           op0=ALU.mult, op1=ALU.add).then_inc(done, 1)

        def ln_scale(t0, n, step, done):
            step(nc.vector.reciprocal(rstd[:, t0:t0 + n], rstd[:, t0:t0 + n]))
            nc.vector.scalar_tensor_tensor(out=nbias[:, t0:t0 + n], in0=lnt[:, 0, 0:n], scalar=-0.5,
                                           in1=rstd[:, t0:t0 + n], op0=ALU.mult, op1=ALU.mult).then_inc(done, 1)

        with nc.Block() as block:
            @block.sync
            def _(sp):
                sp.wait_ge(s_zx, 1)
                for c in range(NCH - 1):
                    sp.dma_start(X[:, c * TC:(c + 1) * TC, :], rows(x, c * TC, TC)).then_inc(s_xin[c], 16)
                c = (NCH - 1) * TC
                if c < T - 2:
                    sp.dma_start(X[:, c:T - 2, :], rows(x, c, T - 2 - c)).then_inc(s_xin[NCH - 1], 16)
                sp.dma_start(X[0:LAST, T - 2, :], x[(T - 2) * P:N, :]).then_inc(s_xin[NCH - 1], 16)
                sp.wait_ge(s_zw, 1)
                for to, of in wts:
                    sp.dma_start(to, of).then_inc(s_wts, 16)
                full = (SROWS - 1) * 4 * SC
                sp.dma_start(chk_i[0:SROWS - 1, :, :], dst[0:full].rearrange("(p q e) -> p q e", q=4, e=SC)).then_inc(s_chk_in, 16)
                left = E - full
                q = left // SC
                r = left % SC
                sp.dma_start(chk_i[SROWS - 1:SROWS, 0:q, :], dst[full:full + q * SC].rearrange("(o q e) -> o q e", o=1, q=q)).then_inc(s_chk_in, 16)
                for i in (q, q + 1):
                    sp.dma_start(chk_i[SROWS - 1:SROWS, i, 0:r], dst[E - r:E].unsqueeze(0)).then_inc(s_chk_in, 16)
                    sp.dma_start(chk_i[SROWS - 1:SROWS, i, r:SC], dst[E - (SC - r):E].unsqueeze(0)).then_inc(s_chk_in, 16)
                with nc.allow_non_contiguous_dma(reason="one number in 512"):
                    sp.dma_start(base0_i[:, 0:NSC - 1], dst[0:(NSC - 2) * SC + 1:SC].unsqueeze(0)).then_inc(s_chk_in, 16)
                sp.dma_start(base0_i[:, NSC - 1:NSC], dst[E0:E0 + 1].unsqueeze(0)).then_inc(s_chk_in, 16)
                for c in range(NCH):
                    for t0 in (c * TC, c * TC + TC // 2):
                        sp.wait_ge(s_h, t0 + TC // 2)
                        sp.dma_start(rows(h_tab, t0, TC // 2), h_st[:, t0:t0 + TC // 2, :]).then_inc(s_hst, 16)
                    if c == 0:
                        sp.wait_ge(s_tail, 16 * len(tails))
                        for tab, of in tails:
                            if len(tab.shape) == 1:
                                sp.dma_start(tab[0:ETAIL].unsqueeze(0), of[E0:E].unsqueeze(0)).then_inc(s_tail, 16)
                            else:
                                sp.dma_start(tab[0:ETAIL, :], of[E0:E, :]).then_inc(s_tail, 16)
                sp.wait_ge(s_wts, 16 * len(wts))
                sp.wait_ge(s_hst, 32 * NCH)
                sp.wait_ge(s_tail, 32 * len(tails))

            @block.gpsimd
            def _(pool):
                nc.gpsimd.iota(win_i, pattern=[[1, WU]], base=0, channel_multiplier=0).then_inc(s_id, 1)
                nc.gpsimd.memset(ident[:, :], 0.0).then_inc(s_id, 1)
                nc.gpsimd.memset(ones[:, :], 1.0).then_inc(s_id, 1)
                pool.wait_ge(s_id, 3)
                nc.gpsimd.affine_select(out=ident[:, :], in_=ident[:, :], compare_op=ALU.not_equal, fill=1.0, base=0,
                                        pattern=[[-1, P]], channel_multiplier=1).then_inc(s_id, 1)
                nc.gpsimd.tensor_copy(win[:, :], win_i).then_inc(s_id, 1)
                zeroed = (up_sb, sc_sb, lin_sb, wb_sb)
                for tile in zeroed:
                    nc.gpsimd.memset(tile[:], 0.0).then_inc(s_id, 1)
                pool.wait_ge(s_id, 5 + len(zeroed))
                for to, of in wts2:
                    pool.dma_start(to, of).then_inc(s_wts2, 16)
                nc.gpsimd.memset(acc[:, 0:2, :], 0.0).then_inc(s_acc0, 1)
                pool.wait_ge(s_wts2, 16 * len(wts2))

            @block.scalar
            def _(act):
                act.wait_ge(s_zw, 1)
                for tab, of in tails:
                    flat = tab if len(tab.shape) == 1 else tab.rearrange("e f -> (e f)")
                    n = 1 if len(tab.shape) == 1 else tab.shape[1]
                    fill = neg if tab is dst_tail else cst[:, 0:8].bitcast(I32) if tab is src_tail else cst[:, 0:8 * n]
                    act.dma_start(flat.rearrange("(p f) -> p f", p=P), fill).then_inc(s_tail, 16)
                for c in range(NCH):
                    t0 = c * TC
                    act.wait_ge(s_ln, c + 1)
                    nc.scalar.activation(rstd[:, t0:t0 + TC], lnt[:, 5, :], ACT.Sqrt, bias=eps_sb[:, 0:1],
                                         scale=1.0 / D).then_inc(s_sq, 1)
                    act.wait_ge(s_nb, c + 1)
                    with act.Fori(0, 2) as i:
                        for m in range(TC // 2):
                            t = i * (TC // 2) + (t0 + m)
                            nc.scalar.activation(row(h_st[:, ds(t, 1), :]), row(X[:, ds(t, 1), :]), ACT.Relu,
                                                 bias=nbias[:, ds(t, 1)], scale=rstd[:, ds(t, 1)]).then_inc(s_h, 1)

            @block.vector
            def _(dve):
                count = [0]

                def step(ins):
                    count[0] += 1
                    ins.then_inc(s_v0, 1)
                    dve.wait_ge(s_v0, count[0])

                step(nc.vector.memset(X[:, T - 2:T, :], 0.0))
                dve.sem_inc(s_zx, 1)
                for to, value in ((m1_sb[:], 0.0), (m2_sb[:], 0.0), (m3_sb[:], 0.0), (cst, 0.0), (neg, -1)):
                    nc.vector.memset(to, value).then_inc(s_v0, 1)
                count[0] += 5
                step(nc.vector.memset(eps_sb[:, :], EPS))
                dve.sem_inc(s_zw, 1)

                for c in range(NCH):
                    t0 = c * TC
                    dve.wait_ge(s_xin[c], 16 * (1 + (c == NCH - 1 and c * TC < T - 2)))
                    with dve.Fori(0, 2) as i:
                        for m in range(TC // 2):
                            t = i * (TC // 2) + (t0 + m)
                            nc.vector.bn_stats(row(mv[:, ds(t, 1), :]), row(X[:, ds(t, 1), :])).then_inc(s_bn, 1)
                    dve.wait_ge(s_bn, t0 + TC)
                    if c >= 1:
                        dve.wait_ge(s_nb, c)
                    ln_stats(t0, TC, step, s_ln)
                    dve.wait_ge(s_sq, c + 1)
                    ln_scale(t0, TC, step, s_nb)

                dve.wait_ge(s_chk_in, 16 * 8)
                first, high, low, bad = (small[0:SROWS, 4 * k:4 * k + 4] for k in range(4))
                high_u, low_u = small[0:SROWS, 16:18], small[0:SROWS, 18:20]
                nc.vector.tensor_copy(base_f[0:1, :], base0_i[:, :]).then_inc(s_chk, 1)
                nc.vector.tensor_copy(first, chk_i[:, :, 0]).then_inc(s_v0, 1)
                nc.vector.tensor_reduce(high, chk_i, AX_X, ALU.max).then_inc(s_v0, 1)
                nc.vector.tensor_reduce(low, chk_i, AX_X, ALU.min).then_inc(s_v0, 1)
                count[0] += 3
                dve.wait_ge(s_v0, count[0])
                nc.vector.tensor_tensor(high_u, high[:, 1:4:2], first[:, 0:4:2], ALU.subtract).then_inc(s_v0, 1)
                nc.vector.tensor_tensor(low_u, first[:, 0:4:2], low[:, 1:4:2], ALU.subtract).then_inc(s_v0, 1)
                count[0] += 2
                step(nc.vector.tensor_tensor(bad, high, first, ALU.subtract))
                step(nc.vector.tensor_tensor(low, first, low, ALU.subtract))
                nc.vector.tensor_scalar(high_u, high_u, float(WU), None, ALU.is_ge).then_inc(s_v0, 1)
                nc.vector.tensor_scalar(low_u, low_u, 0.0, None, ALU.is_gt).then_inc(s_v0, 1)
                nc.vector.tensor_scalar(bad, bad, float(W), None, ALU.is_ge).then_inc(s_v0, 1)
                count[0] += 3
                step(nc.vector.tensor_scalar(low, low, 0.0, None, ALU.is_gt))
                nc.vector.tensor_tensor(high_u, high_u, low_u, ALU.add).then_inc(s_v0, 1)
                count[0] += 1
                step(nc.vector.tensor_tensor(bad, bad, low, ALU.add))
                nc.vector.tensor_reduce(small[0:SROWS, 21:22], bad, AX_X, ALU.add).then_inc(s_v0, 1)
                count[0] += 1
                step(nc.vector.tensor_reduce(small[0:SROWS, 20:21], high_u, AX_X, ALU.add))
                nc.vector.tensor_tensor(small[0:SROWS, 20:21], small[0:SROWS, 20:21], small[0:SROWS, 21:22], ALU.add).then_inc(s_chk, 1)
                dve.wait_ge(s_chk_ps, 1)
                nc.vector.tensor_copy(base0_f[:, :], ps[:, 5, 0:NSC]).then_inc(s_v0, 1)
                count[0] += 1
                dve.wait_ge(s_chk_ps, 2)
                step(nc.vector.tensor_scalar(small[:, 22:24], ps[:, 4, 0:2], 1.0, None, ALU.min))
                nc.vector.tensor_scalar(small[:, 24:26], small[:, 22:24], -1.0, 1.0, ALU.mult, ALU.add).then_inc(s_v0, 1)
                count[0] += 1
                for layer, w in enumerate((WU, W)):
                    step(nc.vector.tensor_scalar(small[0:1, 26 + layer:27 + layer], small[0:1, 22 + layer:23 + layer],
                                                 float(-(-N // w) - 1), 1.0, ALU.mult, ALU.add))
                step(nc.vector.tensor_copy(npass[:, :], small[0:1, 26:28]))

            @block.tensor
            def _(pe):
                pe.wait_ge(s_id, 5)
                pe.wait_ge(s_chk, 1)
                nc.tensor.matmul(ps[:, 5, 0:NSC], ones[0:1, :], base_f[0:1, :], start=True, stop=True).then_inc(s_chk_ps, 1)
                pe.wait_ge(s_chk, 2)
                nc.tensor.matmul(ps[:, 4, 0:2], ones[0:SROWS, :], small[0:SROWS, 20:22], start=True, stop=True).then_inc(s_chk_ps, 1)

        rows_g = work[:, 0:2 * 8 * D].rearrange("p (s k d) -> p s k d", s=2, k=8)
        prod = work[:, 4096:7168].rearrange("p (j k b c) -> p j k b c", j=2, k=G, b=6)
        x1s = work[:, 7168:8704].rearrange("p (j v g c) -> p j v g c", j=2, v=3, g=G)
        y = work[:, 8704:8960].rearrange("p (g c) -> p g c", g=G)
        onehot = mlp[:, :].rearrange("p (s k a w) -> p s k a w", s=2, k=8, a=5)
        hot_u = work[:, 8192:10240].rearrange("p (s k w) -> p s k w", s=2, k=8)
        eq_u = mlp[:, 1536:2560].rearrange("p (k w) -> p k w", w=WU)
        rel = work[:, 10496:10504]
        idx = work[:, 10504:10520].bitcast(I32).rearrange("p (s k) -> p s k", s=2)
        dsti = work[:, 10520:10536].bitcast(I32).rearrange("p (s k) -> p s k", s=2)
        wgt = work[:, 10536:10552].rearrange("p (s k) -> p s k", s=2)
        sh = work[:, 10560:10624].rearrange("p (s k) -> p s k", s=2)
        r12 = work[:, 10624:11648].bitcast(BF16).rearrange("p (s a n) -> p s a n", s=2, a=2)
        r13 = work[:, 11648:12672].bitcast(BF16).rearrange("p (s a n) -> p s a n", s=2, a=2)
        rf = work[C:P, 12672:13696].rearrange("p (a n) -> p a n", a=2)
        rd = work[C:P, 13696:14720].rearrange("p (a n) -> p a n", a=2)
        xt_in, ht_in, hT = (work[:, 4096 + k * D:4096 + (k + 1) * D] for k in range(3))
        attr = mlp[:, 0:256].rearrange("p (s n) -> p s n", s=2)
        attr_t = mlp[:, 256:384]
        r1 = mlp[:, 512:1024]
        r2 = mlp[:, 1024:1536]

        def edge_syms(ph):
            return dict(
                idx=[sem(f"idx{ph}_{s}") for s in range(2)],
                edge=[sem(f"edge{ph}_{s}") for s in range(2)],
                rad=[sem(f"rad{ph}_{s}") for s in range(2)],
                rad_used=[sem(f"rad_used{ph}_{s}") for s in range(2)],
                got=[[sem(f"got{ph}_{s}{j}") for j in range(2)] for s in range(2)],
                rel=sem(f"rel{ph}"), eq=sem(f"eq{ph}"),
                hot=[sem(f"hot{ph}_{s}") for s in range(2)],
                summed=[[sem(f"summed{ph}_{s}{j}") for j in range(2)] for s in range(2)],
                added=[sem(f"added{ph}_{j}") for j in range(2)],
                base=sem(f"base{ph}"),
                settled=sem(f"settled{ph}"),
                fresh=sem(f"fresh{ph}"),
            )

        def passes(eng, layer):
            return eng.value_load(npass[0:1, layer:layer + 1], min_val=1, max_val=-(-N // (WU, W)[layer]))

        def load_units(sp, layer, S, edge_views, rads, edge_used, load_tile=None):
            def load(u, pz, k, s):
                use = pz * ROUNDS + k
                for j in range(2):
                    sp.wait_ge(S["got"][s][j], k * (16 * G))
                sp.dma_start(idx[:, s, :].rearrange("p (j g) -> p j g", g=G), unit_of(src_u, u)).then_inc(S["idx"][s], 16)
                for used in edge_used:
                    sp.wait_ge(used[s], use)
                for to, view in edge_views:
                    sp.dma_start(to[:, s, :].rearrange("p (j g) -> p j g", j=2), unit_of(view, u)).then_inc(S["edge"][s], 16)
                sp.wait_ge(S["rad_used"][s], use)
                for to, of in rads(u, s):
                    sp.dma_start(to, of).then_inc(S["rad"][s], 16)

            with sp.Fori(0, passes(sp, layer)) as pz:
                sp.wait_ge(S["fresh"], pz)
                sp.sem_inc(s_turn, 1)
                if load_tile:
                    with sp.Fori(0, NT - 1) as k:
                        for s in range(2):
                            load(k * 2 + s, pz, k, s)
                        load_tile(k, pz)
                    for s in range(2):
                        load((NT - 1) * 2 + s, pz, NT - 1, s)
                    load_tile(NT - 1, pz)
                with sp.Fori(NT if load_tile else 0, ROUNDS - 1) as k:
                    for s in range(2):
                        load(k * 2 + s, pz, k, s)
                for s in range(2):
                    load(NU - 2 + s, pz, ROUNDS - 1, s)
                sp.sem_inc(S["settled"], 1)

        def gather_units(pool, layer, S, table, taken, waiters):
            with pool.Fori(0, passes(pool, layer)) as pz:
                with pool.Fori(0, ROUNDS) as k:
                    for s in range(2):
                        use = pz * ROUNDS + k
                        pool.wait_ge(S["idx"][s], use * 16 + 16)
                        for j in range(2):
                            pool.wait_ge(taken[s][j], use)
                            pool.sem_inc(s_turn, 1)
                            for g in range(G):
                                q = j * G + g
                                pool.indirect_dma_start(
                                    out=rows_g[:, s, q, :], out_offset=None, in_=table,
                                    in_offset=bass.IndirectOffsetOnAxis(ap=idx[:, s, q:q + 1], axis=0),
                                ).then_inc(S["got"][s][j], 16)
                for s in range(2):
                    for j in range(2):
                        pool.wait_ge(S["got"][s][j], 16 * G * ROUNDS)
                pool.wait_ge(S["settled"], pz * waiters + waiters)
                pool.sem_inc(s_turn, 1)
                pool.dma_reset()
                for s in range(2):
                    for j in range(2):
                        pool.sem_clear(S["got"][s][j])
                pool.sem_inc(S["fresh"], 1)

        def hot_steps(dve, S, u, use, s, layer):
            def step_rel():
                dve.wait_ge(S["edge"][s], use * 32 + 32)
                base = (bc(base_f[:, ds(u * 2, 1)], 2, G).to_broadcast([P, 2, G]), bc(base_f[:, ds(u * 2, 2)], 2, G))[layer]
                nc.vector.tensor_tensor(rel.rearrange("p (j g) -> p j g", j=2), dsti[:, s, :].rearrange("p (j g) -> p j g", j=2),
                                        base, ALU.subtract).then_inc(S["rel"], 1)

            def step_eq(gu):
                to, w = ((eq_u, WU), (onehot[:, s, :, 4, :], W))[layer]
                dve.wait_ge(S["rel"], gu + 1)
                if layer == 1:
                    dve.wait_ge(S["summed"][s][1], use)
                nc.vector.tensor_tensor(to, bc(win[:, 0:w], 1, 8), bc(rel, 2, w), ALU.is_equal).then_inc(S["eq"], 1)

            def step_hot(gu):
                dve.wait_ge(S["eq"], gu + 1)
                if layer == 0:
                    dve.wait_ge(S["summed"][s][1], use)
                    nc.vector.tensor_tensor(hot_u[:, s, :, :], eq_u, bc(wgt[:, s, :], 2, WU), ALU.mult).then_inc(S["hot"][s], 1)
                else:
                    for j in range(2):
                        v = sh[:, s, 16 * j:16 * j + 16].rearrange("p (k a) -> p k a", a=4)
                        last = nc.vector.tensor_tensor(onehot[:, s, 4 * j:4 * j + 4, 0:4, :], bc(onehot[:, s, 4 * j:4 * j + 4, 4, :], 2, 4),
                                                       bc(v, 3, W), ALU.mult)
                    last.then_inc(S["hot"][s], 1)

            return step_rel, step_eq, step_hot

        def set_base(dve, S, layer, pz):
            w = float((WU, W)[layer])
            nc.vector.tensor_scalar(base_f[:, :], base_f[:, :], w, None, ALU.add).then_inc(S["base"], 1)
            nc.vector.tensor_scalar(base_i[:, :], base_i[:, :], w, None, ALU.add).then_inc(S["base"], 1)
            dve.wait_ge(S["base"], pz * 2 + 4)

        def first_base(dve, S, layer):
            nc.vector.tensor_scalar(base_f[:, :], base0_f[:, :], small[:, 24 + layer:25 + layer], None, ALU.mult).then_inc(S["base"], 1)
            dve.wait_ge(S["base"], 1)
            nc.vector.tensor_copy(base_i[:, :], base_f[0:1, :]).then_inc(S["base"], 1)
            dve.wait_ge(S["base"], 2)

        s_turn = sem("s_turn")

        S = edge_syms(1)
        at_ready, z1_ready, r1_ready, z2_ready, r2_ready, z3_ready, r3_ready = (
            sem(n) for n in ("at_ready", "z1_ready", "r1_ready", "z2_ready", "r2_ready", "z3_ready", "r3_ready"))

        def two(ap):
            return ap.rearrange("p a n -> p (a n)")

        def row_of(tab, u):
            return tab[ds(u, 1), :, :].rearrange("o p n -> (o p) n")

        r_part = sem("r_part")
        tile_in = sem("tile_in")
        tile_tp = sem("tile_tp")
        tile_ht = sem("tile_ht")
        tile_self = sem("tile_self")
        tile_x1 = sem("tile_x1")
        r3_stored = [sem(f"r3_stored{s}") for s in range(2)]

        with nc.Block() as block:
            @block.sync
            def _(sp):
                def load_tile(k, pz):
                    sp.wait_ge(tile_x1, pz * NT + k)
                    if isinstance(k, int):
                        sp.dma_start(xt_in[0:LAST, :], x[k * P:N, :]).then_inc(tile_in, 16)
                    else:
                        sp.dma_start(xt_in, x[ds(k * P, P), :]).then_inc(tile_in, 16)
                    sp.dma_start(ht_in, h_tab[ds(k * P, P), :]).then_inc(tile_in, 16)

                load_units(sp, 0, S, ((dsti, dst_u), (wgt, w_u)), 
                           lambda u, s: [(attr[:, s, :].rearrange("p (j n) -> p j n", j=2), unit_of(a16_u, u))], [S["hot"]], load_tile)

            @block.gpsimd
            def _(pool):
                gather_units(pool, 0, S, h_tab, S["summed"], 2)

            @block.vector
            def _(dve):
                first_base(dve, S, 0)
                with dve.Fori(0, passes(dve, 0)) as pz:
                    def hot(u, use, gu, s):
                        for part, arg in zip(hot_steps(dve, S, u, use, s, 0), ((), (gu,), (gu,))):
                            part(*arg)

                    def split(s, use, gu):
                        dve.wait_ge(r3_ready, gu * 2 + 2)
                        dve.wait_ge(r_part, gu * 3)
                        nc.vector.tensor_tensor(rd, rf, r12[C:P, s], ALU.subtract).then_inc(r_part, 1)
                        dve.wait_ge(r_part, gu * 3 + 1)
                        nc.vector.tensor_copy(r12[C:P, s], rd).then_inc(r_part, 1)
                        dve.wait_ge(r_part, gu * 3 + 2)
                        dve.wait_ge(r3_stored[s], use * 32)
                        nc.vector.tensor_tensor(r13[C:P, s], rd, r12[C:P, s], ALU.subtract).then_inc(r_part, 1)

                    def unit(k, s, last=False, tile=False, first=False):
                        use, gu = pz * ROUNDS + k, pz * NU + k * 2 + s
                        if not last:
                            hot(k * 2 + s + 1, use + s, gu + 1, 1 - s)
                            turned(gu + 1, use + s, 1 - s)
                        if not first:
                            split(1 - s, use - (1 - s), gu - 1)
                        b = dve.value_load(base_i[0:1, ds(k * 4 + 2 * s, 1)], min_val=0, max_val=N - 1)
                        dve.wait_ge(S["summed"][s][1], use + 1)
                        dve.wait_ge(S["added"][1 - s], use + s)
                        to = acc[:, 0:2, ds(b, WU)]
                        nc.vector.tensor_tensor(to, to, ps[:, 6 + s, 0:2 * WU].rearrange("p (h w) -> p h w", h=2),
                                                ALU.add).then_inc(S["added"][s], 1)
                        if tile:
                            done = pz * NT + k
                            if s == 0:
                                dve.wait_ge(tile_tp, done + 1)
                                dve.wait_ge(tile_self, done)
                                nc.vector.tensor_copy(hT, ps[:, 4, 0:D]).then_inc(tile_ht, 1)
                            else:
                                dve.wait_ge(tile_self, done + 1)
                                nc.vector.tensor_tensor(row(X[:, ds(k, 1), :]), xt_in, ps[:, 4, D:2 * D], ALU.add).then_inc(tile_x1, 1)

                    def turned(gu, use, s):
                        dve.wait_ge(S["rad_used"][s], use + 1)
                        dve.wait_ge(z1_ready, gu)
                        nc.vector.tensor_copy(attr_t, ps[:, 0, 0:P]).then_inc(at_ready, 1)

                    hot(0, pz * ROUNDS, pz * NU, 0)
                    turned(pz * NU, pz * ROUNDS, 0)
                    for s in range(2):
                        unit(0, s, tile=True, first=(s == 0))
                    with dve.Fori(1, NT) as k:
                        for s in range(2):
                            unit(k, s, tile=True)
                    with dve.Fori(NT, ROUNDS - 1) as k:
                        for s in range(2):
                            unit(k, s)
                    for s in range(2):
                        unit(ROUNDS - 1, s, last=(s == 1))
                    split(1, pz * ROUNDS + (ROUNDS - 1), pz * NU + (NU - 1))
                    dve.wait_ge(S["added"][1], pz * ROUNDS + ROUNDS)
                    set_base(dve, S, 0, pz)

            @block.tensor
            def _(pe):
                def turn(s, use, gu):
                    pe.wait_ge(S["rad"][s], use * 16 + 16)
                    pe.wait_ge(at_ready, gu)
                    nc.tensor.transpose(ps[:, 0, 0:P], attr[:, s, :], ident[:, :]).then_inc(S["rad_used"][s], 1)

                def sums(s, j, k, use):
                    pe.wait_ge(S["got"][s][j], k * (16 * G) + 16 * G)
                    if j == 0:
                        pe.wait_ge(S["hot"][s], use + 1)
                        pe.wait_ge(S["added"][s], use)
                    for g in range(G):
                        q = j * G + g
                        for half in range(2):
                            mm = nc.tensor.matmul(ps[:, 6 + s, half * WU:(half + 1) * WU], rows_g[:, s, q, half * P:(half + 1) * P],
                                                  hot_u[:, s, q, :], start=(q == 0 and half == 0), stop=(q == 7 and half == 1))
                    mm.then_inc(S["summed"][s][j], 1)

                def tile_part(k, s):
                    done = pz * NT + k
                    if s == 0:
                        pe.wait_ge(tile_in, done * 32 + 32)
                        pe.wait_ge(tile_x1, done)
                        for b in range(2):
                            mm = nc.tensor.transpose(ps[:, 4, b * P:(b + 1) * P], ht_in[:, b * P:(b + 1) * P], ident[:, :])
                        mm.then_inc(tile_tp, 1)
                    else:
                        pe.wait_ge(tile_ht, done + 1)
                        nc.tensor.matmul(ps[:, 4, D:2 * D], ones[0:1, :], bias_sb[:, :], start=True, stop=False)
                        for b in range(2):
                            mm = nc.tensor.matmul(ps[:, 4, D:2 * D], hT[:, b * P:(b + 1) * P], ws_sb[:, b, :], start=False, stop=(b == 1))
                        mm.then_inc(tile_self, 1)

                def unit(k, s, last=False, tile=False):
                    use, gu = pz * ROUNDS + k, pz * NU + k * 2 + s
                    pe.wait_ge(at_ready, gu + 1)
                    pe.wait_ge(r1_ready, gu)
                    for q in range(4):
                        mm = nc.tensor.matmul(ps[:, 1, q * P:(q + 1) * P], m1_sb[:, q, :], attr_t, start=True, stop=True)
                    mm.then_inc(z1_ready, 1)
                    sums(s, 0, k, use)
                    if not last:
                        turn(1 - s, use + s, gu + 1)
                    pe.wait_ge(r1_ready, gu + 1)
                    pe.wait_ge(r2_ready, gu)
                    nc.tensor.matmul(ps[:, 2, :], m2_sb[:, :], r1, start=True, stop=True).then_inc(z2_ready, 1)
                    if tile:
                        tile_part(k, s)
                    sums(s, 1, k, use)
                    pe.wait_ge(r2_ready, gu + 1)
                    pe.wait_ge(r3_ready, gu * 2)
                    for a in range(2):
                        nc.tensor.matmul(ps[:, 3 + 2 * a, :], m3_sb[:, a, :], r2, start=True, stop=True).then_inc(z3_ready, 1)

                with pe.Fori(0, passes(pe, 0)) as pz:
                    pe.wait_ge(S["fresh"], pz)
                    turn(0, pz * ROUNDS, pz * NU)
                    with pe.Fori(0, NT) as k:
                        for s in range(2):
                            unit(k, s, tile=True)
                    with pe.Fori(NT, ROUNDS - 1) as k:
                        for s in range(2):
                            unit(k, s)
                    for s in range(2):
                        unit(ROUNDS - 1, s, last=(s == 1))
                    pe.sem_inc(S["settled"], 1)

            @block.scalar
            def _(act):
                def store(u, s, gu):
                    act.wait_ge(r_part, gu * 3 + 3)
                    act.dma_start(row_of(r12_tab, u), two(r12[:, s])).then_inc(r3_stored[s], 16)
                    act.dma_start(row_of(rlow_tab, u), two(r13[C:P, s])).then_inc(r3_stored[s], 16)

                with act.Fori(0, passes(act, 0)) as pz:
                    def unit(k, s, first=False):
                        use, gu = pz * ROUNDS + k, pz * NU + k * 2 + s
                        act.wait_ge(z1_ready, gu + 1)
                        act.wait_ge(z2_ready, gu)
                        nc.scalar.activation(r1, ps[:, 1, :], ACT.Silu).then_inc(r1_ready, 1)
                        act.wait_ge(z2_ready, gu + 1)
                        act.wait_ge(z3_ready, gu * 2)
                        nc.scalar.activation(r2, ps[:, 2, :], ACT.Silu).then_inc(r2_ready, 1)
                        if not first:
                            store(k * 2 + s - 1, 1 - s, gu - 1)
                        act.wait_ge(r3_stored[s], use * 32)
                        act.wait_ge(r_part, gu * 3)
                        for a in range(2):
                            act.wait_ge(z3_ready, gu * 2 + (a + 1))
                            nc.scalar.activation(r12[:, s, a, :], ps[:, 3 + 2 * a, :], ACT.Silu)
                            nc.scalar.activation(rf[:, a, :], ps[C:P, 3 + 2 * a, :], ACT.Silu).then_inc(r3_ready, 1)

                    for s in range(2):
                        unit(0, s, first=(s == 0))
                    with act.Fori(1, ROUNDS) as k:
                        for s in range(2):
                            unit(k, s)
                    store(NU - 1, 1, pz * NU + (NU - 1))
                    for s in range(2):
                        act.wait_ge(r3_stored[s], pz * (32 * ROUNDS) + 32 * ROUNDS)

        t_agg = sem("t_agg")
        t_x2 = sem("t_x2")
        t_bn, t_v, t_ln, t_sq, t_nb = (sem(n) for n in ("t_bn", "t_v", "t_ln", "t_sq", "t_nb"))
        t_h = sem("t_h")
        t_tp = sem("t_tp")
        t_ht = sem("t_ht")
        t_up_ps = sem("t_up_ps")
        t_up = sem("t_up")
        t_st = [[sem(f"t_st{i}{s}") for s in range(2)] for i in range(2)]
        t_x2st = [sem(f"t_x2st{i}") for i in range(2)]
        CH = next(c for c in range(len(PAIRS) + 1) if 4 * sum(PAIRS[:c]) >= T)
        s_clear = sem("s_clear")

        stage = work[:, :].rearrange("p (a s t d) -> p a s t d", a=3, s=2, t=TC)
        h2p, h2t, ups = stage[:, 0], stage[:, 1], stage[:, 2]
        CHUNKS = len(PAIRS)
        before = [sum(PAIRS[:c]) for c in range(CHUNKS + 1)]

        def flat(ap):
            return ap.rearrange("p t d -> p (t d)")

        with nc.Block() as block:
            def store(sp, c):
                t0, n = 2 * before[c], 2 * PAIRS[c]
                sp.wait_ge(t_ht, before[c + 1])
                sp.dma_start(h2t_tab[:, t0 * D:(t0 + n) * D], flat(h2t[:, c % 2, 0:n])).then_inc(t_st[0][c % 2], 16)
                sp.wait_ge(t_up, before[c + 1])
                sp.dma_start(rows(up_tab, t0, n), ups[:, c % 2, 0:n]).then_inc(t_st[1][c % 2], 16)

            @block.sync
            def _(sp):
                for c in range(CHUNKS):
                    t0, n = 2 * before[c], 2 * PAIRS[c]
                    sp.wait_ge(t_x2, before[c + 1])
                    sp.dma_start(rows(x2_tab, t0, n), X[:, t0:t0 + n, :]).then_inc(t_x2st[c >= CH], 16)
                    if c >= 1:
                        store(sp, c - 1)
                store(sp, CHUNKS - 1)
                sp.wait_ge(t_x2st[0], 16 * CH)
                sp.wait_ge(t_x2st[1], 16 * (CHUNKS - CH))
                for i in range(2):
                    for s in range(2):
                        sp.wait_ge(t_st[i][s], 16 * ((CHUNKS + 1 - s) // 2))

            @block.gpsimd
            def _(pool):
                pool.wait_ge(t_nb, CH)
                pool.wait_ge(t_h, 4 * before[CH])
                pool.wait_ge(t_x2st[0], 16 * CH)
                nc.gpsimd.memset(acc[:, 2, :], 0.0).then_inc(s_clear, 1)
                pool.wait_ge(t_agg, T // 2)
                nc.gpsimd.memset(acc[:, 0:2, :], 0.0).then_inc(s_clear, 1)

            @block.tensor
            def _(pe):
                def neighbors(c):
                    for n in range(PAIRS[c]):
                        pair = before[c] + n
                        if pair >= 2:
                            pe.wait_ge(t_x2, pair - 1)
                        for half in range(2):
                            for k in range(2):
                                mm = nc.tensor.matmul(ps[:, pair % 2, half * D:(half + 1) * D],
                                                      acc[:, k, ds((pair * 2 + half) * P, P)], wn_sb[:, k, :],
                                                      start=(k == 0), stop=(k == 1))
                        mm.then_inc(t_agg, 1)

                neighbors(0)
                for c in range(CHUNKS):
                    if c + 1 < CHUNKS:
                        neighbors(c + 1)
                    for n in range(PAIRS[c] + 1):
                        if n < PAIRS[c]:
                            pair = before[c] + n
                            pe.wait_ge(t_h, pair * 4 + 4)
                            if pair >= 2:
                                pe.wait_ge(t_ht, pair - 1)
                            for m in range(4):
                                mm = nc.tensor.transpose(ps[:, 2 + pair % 2, m * P:(m + 1) * P],
                                                         h2p[:, c % 2, 2 * n + m // 2, (m % 2) * P:(m % 2 + 1) * P], ident[:, :])
                            mm.then_inc(t_tp, 1)
                        if n >= 1:
                            pair = before[c] + n - 1
                            pe.wait_ge(t_ht, pair + 1)
                            if pair >= 2:
                                pe.wait_ge(t_up, pair - 1)
                            for m in range(4):
                                mm = nc.tensor.matmul(ps[:, 4 + pair % 2, m * P:(m + 1) * P],
                                                      h2t[:, c % 2, 2 * n - 2 + m // 2, (m % 2) * P:(m % 2 + 1) * P], up_sb[:, m % 2, :],
                                                      start=True, stop=True)
                            mm.then_inc(t_up_ps, 1)

            @block.vector
            def _(dve):
                count = [0]

                def step(ins):
                    count[0] += 1
                    ins.then_inc(t_v, 1)
                    dve.wait_ge(t_v, count[0])

                step(nc.vector.memset(X[:, T - 1, :], 0.0))
                step(nc.vector.memset(small[:, 0:1], 0.0))
                step(nc.vector.memset(small[0:LAST, 0:1], 1.0))
                step(nc.vector.tensor_scalar(X[:, T - 2, :], X[:, T - 2, :], small[:, 0:1], None, ALU.mult))
                step(nc.vector.tensor_scalar(m4_sb[:, 2, :], m4_sb[:, 2, :], 3.0 ** -0.5, None, ALU.mult))

                def x2_of(c):
                    for n in range(PAIRS[c] + 1):
                        if n < PAIRS[c]:
                            pair = before[c] + n
                            dve.wait_ge(t_agg, pair + 1)
                            xt = flat(X[:, 2 * pair:2 * pair + 2, :])
                            nc.vector.tensor_tensor(xt, xt, ps[:, pair % 2, :], ALU.add).then_inc(t_x2, 1)
                        if n >= 1:
                            pair = before[c] + n - 1
                            dve.wait_ge(t_x2, pair + 1)
                            for t in (2 * pair, 2 * pair + 1):
                                nc.vector.bn_stats(mv[:, t, :], X[:, t, :]).then_inc(t_bn, 1)
                    dve.wait_ge(t_bn, 2 * before[c + 1])
                    if c >= 1:
                        dve.wait_ge(t_nb, c)
                    ln_stats(2 * before[c], 2 * PAIRS[c], step, t_ln)

                def ups_of(c):
                    if c >= 2:
                        dve.wait_ge(t_st[1][c % 2], 16 * (c // 2))
                    for n in range(PAIRS[c]):
                        pair = before[c] + n
                        dve.wait_ge(t_up_ps, pair + 1)
                        nc.vector.tensor_copy(flat(ups[:, c % 2, 2 * n:2 * n + 2, :]), ps[:, 4 + pair % 2, :]).then_inc(t_up, 1)

                def split_m4():
                    m4f = m4_sb.rearrange("p b c -> p (b c)")
                    step(nc.vector.tensor_copy(m4_split[:, 0, :], m4f))
                    step(nc.vector.tensor_tensor(m4f, m4f, m4_split[:, 0, :], ALU.subtract))
                    step(nc.vector.tensor_copy(m4_split[:, 1, :], m4f))
                    step(nc.vector.tensor_tensor(m4_split[0:C, 2, :], m4f[0:C, :], m4_split[0:C, 1, :], ALU.subtract))
                    step(nc.vector.tensor_copy(m4_split[C:P, 2, :], m4_split[C:P, 0, :]))

                for c in range(CHUNKS + 1):
                    if c == 1:
                        split_m4()
                    if c < CHUNKS:
                        x2_of(c)
                        dve.wait_ge(t_sq, c + 1)
                        ln_scale(2 * before[c], 2 * PAIRS[c], step, t_nb)
                    if c >= 1:
                        ups_of(c - 1)

            @block.scalar
            def _(act):
                def deviation(c):
                    act.wait_ge(t_ln, c + 1)
                    t0, n = 2 * before[c], 2 * PAIRS[c]
                    nc.scalar.activation(rstd[:, t0:t0 + n], lnt[:, 5, 0:n], ACT.Sqrt, bias=eps_sb[:, 0:1],
                                         scale=1.0 / D).then_inc(t_sq, 1)

                deviation(0)
                for c in range(CHUNKS):
                    t0 = 2 * before[c]
                    act.wait_ge(t_nb, c + 1)
                    if c >= 2:
                        act.wait_ge(t_tp, before[c - 1])
                    for i in range(2 * PAIRS[c]):
                        xt, ht = X[:, t0 + i, :], h2p[:, c % 2, i, :]
                        how = dict(bias=nbias[:, t0 + i:t0 + i + 1], scale=rstd[:, t0 + i:t0 + i + 1])
                        nc.scalar.activation(ht[:, 0:C], xt[:, 0:C], ACT.Relu, **how).then_inc(t_h, 1)
                        nc.scalar.activation(ht[:, C:D].rearrange("p (v c) -> p c v", v=3),
                                             xt[:, C:D].rearrange("p (c v) -> p c v", v=3), ACT.Relu, **how).then_inc(t_h, 1)
                    if c >= 2:
                        act.wait_ge(t_st[0][c % 2], 16 * (c // 2))
                        act.wait_ge(t_up_ps, before[c - 1])
                    for n in range(PAIRS[c]):
                        pair = before[c] + n
                        act.wait_ge(t_tp, pair + 1)
                        nc.scalar.activation(flat(h2t[:, c % 2, 2 * n:2 * n + 2, :]), ps[:, 2 + pair % 2, :], ACT.Copy).then_inc(t_ht, 1)
                        if n == min(2, PAIRS[c]) - 1 and c + 1 < CHUNKS:
                            deviation(c + 1)

        S3 = edge_syms(3)
        t_ready = [[sem(f"t_ready{s}{j}") for j in range(2)] for s in range(2)]
        S3["rad_used"] = [t_ready[s][1] for s in range(2)]
        prods = [[sem(f"prods{s}{j}") for j in range(2)] for s in range(2)]
        scaled = [[sem(f"scaled{s}{j}") for j in range(2)] for s in range(2)]
        y_part = sem("y_part")
        y_ready = [sem(f"y_ready{j}") for j in range(2)]
        add_one = sem("add_below")

        with nc.Block() as block:
            @block.sync
            def _(sp):
                load_units(sp, 1, S3, ((dsti, dst_u), (sh, a4_u)),
                           lambda u, s: [(two(r12[:, s]), row_of(r12_tab, u)), (two(r13[0:C, s]), row_of(r12_tab[:, 0:C, :], u)),
                                         (two(r13[C:P, s]), row_of(rlow_tab, u))],
                           [S3["hot"], [scaled[s][1] for s in range(2)]])

            @block.gpsimd
            def _(pool):
                gather_units(pool, 1, S3, up_tab, prods, 3)

            @block.scalar
            def _(act):
                with act.Fori(0, passes(act, 1)) as pz:
                    act.wait_ge(S3["fresh"], pz)
                    with act.Fori(0, ROUNDS) as k:
                        for s in range(2):
                            for j in range(2):
                                use, gu = pz * ROUNDS + k, pz * NU + k * 2 + s
                                if j == 0:
                                    act.wait_ge(S3["edge"][s], use * 32 + 32)
                                act.wait_ge(S3["got"][s][j], k * (16 * G) + 16 * G)
                                act.wait_ge(y_ready[j], gu)
                                for g in range(G):
                                    q = j * G + g
                                    for v in range(3):
                                        a = 4 * q + v + 1
                                        last = nc.scalar.activation(x1s[:, j, v, g, :], rows_g[:, s, q, (v + 1) * C:(v + 2) * C],
                                                                    ACT.Copy, scale=sh[:, s, a:a + 1])
                                last.then_inc(scaled[s][j], 1)
                    act.sem_inc(S3["settled"], 1)

            @block.tensor
            def _(pe):
                def radial(s, j, use):
                    if j == 0:
                        pe.wait_ge(S3["rad"][s], use * 48 + 48)
                    pe.wait_ge(prods[1 - s][j], use + s)
                    for g in range(G):
                        to = ps[:, 2 * j + g // 2, (g % 2) * D:(g % 2 + 1) * D]
                        col = ds((2 * j + g // 2) * P, P)
                        for i, r in enumerate((r12, r12, r13)):
                            mm = nc.tensor.matmul(to, r[:, s, g % 2, col], m4_split[:, i, :], start=(i == 0), stop=(i == 2))
                    mm.then_inc(t_ready[s][j], 1)

                def sums(s, j, use, gu):
                    pe.wait_ge(prods[s][j], use + 1)
                    if j == 0:
                        pe.wait_ge(S3["hot"][s], use + 1)
                    pe.wait_ge(S3["added"][j], gu)
                    bank = ps[:, 6 + j, :]
                    for g in range(G):
                        hot = onehot[:, s, j * G + g, :, :]
                        pair = prod[:, j, g, :, :].rearrange("p (b two) c -> p b (two c)", two=2)
                        nc.tensor.matmul(bank[:, 0:4 * W], pair[:, 2, :], hot[:, 1:5, :].rearrange("p a w -> p (a w)"),
                                         start=(g == 0), stop=False)
                        nc.tensor.matmul(bank[:, 4 * W:5 * W], pair[:, 0, :], hot[:, 0, :], start=False, stop=False)
                        mm = nc.tensor.matmul(bank[:, 5 * W:6 * W], pair[:, 1, :], hot[:, 0, :], start=False, stop=(g == G - 1))
                    mm.then_inc(S3["summed"][s][j], 1)

                with pe.Fori(0, passes(pe, 1)) as pz:
                    radial(0, 0, pz * ROUNDS)
                    with pe.Fori(0, ROUNDS - 1) as k:
                        for s in range(2):
                            for j in range(2):
                                use, gu = pz * ROUNDS + k, pz * NU + k * 2 + s
                                s1, j1 = (s, 1) if j == 0 else (1 - s, 0)
                                radial(s1, j1, use + (s if j else 0))
                                sums(s, j, use, gu)
                    for s in range(2):
                        for j in range(2):
                            use, gu = pz * ROUNDS + (ROUNDS - 1), pz * NU + (NU - 2 + s)
                            if (s, j) != (1, 1):
                                s1, j1 = (s, 1) if j == 0 else (1 - s, 0)
                                radial(s1, j1, use + (s if j else 0))
                            sums(s, j, use, gu)

            @block.vector
            def _(dve):
                first_base(dve, S3, 1)
                with dve.Fori(0, passes(dve, 1)) as pz:
                    dve.wait_ge(S3["fresh"], pz)
                    def products(s, j, k, use, gu):
                        t = ps[:, 2 * j:2 * j + 2, :].rearrange("p a (g b c) -> p (a g) b c", g=2, b=4)
                        up = rows_g[:, s, j * G:(j + 1) * G, :].rearrange("p g (b c) -> p g b c", b=4)
                        to = prod[:, j, :, :, :]
                        dve.wait_ge(scaled[s][j], use + 1)
                        dve.wait_ge(prods[(s + 1 - j) % 2][1 - j], use + (s if j == 0 else 1))
                        nc.vector.tensor_tensor(y, x1s[:, j, 0], x1s[:, j, 1], ALU.add).then_inc(y_part, 1)
                        dve.wait_ge(t_ready[s][j], use + 1)
                        dve.wait_ge(S3["got"][s][j], k * (16 * G) + 16 * G)
                        dve.wait_ge(S3["summed"][1 - s][j], use + s)
                        nc.vector.tensor_tensor(to[:, :, 0:6:5, :], t[:, :, 0:2, :], bc(up[:, :, 0, :], 2, 2), ALU.mult)
                        dve.wait_ge(y_part, gu * 2 + (j + 1))
                        nc.vector.tensor_tensor(y, y, x1s[:, j, 2], ALU.add).then_inc(y_ready[j], 1)
                        nc.vector.tensor_tensor(to[:, :, 1:4, :], bc(t[:, :, 3, :], 2, 3), up[:, :, 1:4, :], ALU.mult)
                        dve.wait_ge(y_ready[j], gu + 1)
                        nc.vector.tensor_tensor(to[:, :, 4, :], t[:, :, 2, :], y, ALU.mult).then_inc(prods[s][j], 1)

                    def add_window(u, use, gu, s, j):
                        b = dve.value_load(base_i[0:1, ds(u * 2 + j, 1)], min_val=0, max_val=N - 1)
                        dve.wait_ge(S3["summed"][s][j], use + 1)
                        dve.wait_ge(S3["added"][1 - j], gu + j)
                        sums = ps[:, 6 + j, 0:6 * W].rearrange("p (q w) -> p q w", q=6)
                        below, m0, both = acc[C:P, 0:3, ds(b, W)], acc[0:C, 0, ds(b, W)], acc[:, 0:3:2, ds(b, W)]
                        nc.vector.tensor_tensor(below, below, sums[C:P, 0:3, :], ALU.add).then_inc(add_one, 1)
                        nc.vector.tensor_tensor(m0, m0, sums[0:C, 3, :], ALU.add).then_inc(add_one, 1)
                        dve.wait_ge(add_one, gu * 4 + (2 * j + 2))
                        nc.vector.tensor_tensor(both, both, sums[:, 4:6, :], ALU.add).then_inc(S3["added"][j], 1)

                    def unit(k, s, first=False, last=False):
                        use, gu = pz * ROUNDS + k, pz * NU + k * 2 + s
                        if not last:
                            rel_, eq_, hot_ = hot_steps(dve, S3, k * 2 + s + 1, use + s, 1 - s, 1)
                            rel_()
                        products(s, 0, k, use, gu)
                        if not first:
                            add_window(k * 2 + s - 1, use - (1 - s), gu - 1, 1 - s, 1)
                        if not last:
                            eq_(gu + 1)
                        products(s, 1, k, use, gu)
                        if not last:
                            hot_(gu + 1)
                        add_window(k * 2 + s, use, gu, s, 0)

                    rel_, eq_, hot_ = hot_steps(dve, S3, 0, pz * ROUNDS, 0, 1)
                    rel_()
                    eq_(pz * NU)
                    hot_(pz * NU)
                    unit(0, 0, first=True)
                    unit(0, 1)
                    with dve.Fori(1, ROUNDS - 1) as k:
                        for s in range(2):
                            unit(k, s)
                    unit(ROUNDS - 1, 0)
                    unit(ROUNDS - 1, 1, last=True)
                    add_window(NU - 1, pz * ROUNDS + (ROUNDS - 1), pz * NU + (NU - 1), 1, 1)
                    dve.sem_inc(S3["settled"], 1)
                    dve.wait_ge(S3["added"][1], pz * NU + NU)
                    set_base(dve, S3, 1, pz)

        X2 = work[:, 0:T * D].rearrange("p (t d) -> p t d", d=D)
        spare = work[:, T * D:]
        el = [mlp, spare]
        a0 = [e[:, 0:BN] for e in el]
        sq = [e[:, BN:4 * BN].rearrange("p (v n) -> p v n", v=3) for e in el]
        hu = [e[:, 4 * BN:5 * BN] for e in el]
        hw = [e[:, 5 * BN:6 * BN] for e in el]
        hp = [e[:, 6 * BN:7 * BN] for e in el]
        h2s = [e[:, m * 2 * D:(m + 1) * 2 * D].rearrange("p (h d) -> p h d", h=2) for e in (mlp, spare[:, 4 * D:]) for m in range(2)]
        osq = spare[:, 0:12 * C].rearrange("p (s h d) -> p s h d", s=2, h=2)
        tot = mlp[:, 4 * D:4 * D + 8 * C].rearrange("p (h d) -> p h d", h=2)
        par = mlp[:, 1536:1536 + 2 * C].rearrange("p (a c) -> p a c", a=2)
        mean = mlp[:, 1664:1664 + C]
        stat = mlp[:, 1728:1728 + 2 * C].rearrange("p (a c) -> p a c", a=2)
        scl = mlp[:, 1856:1856 + D].rearrange("p (q c) -> p q c", q=4)
        O = acc[:, :, HN:].rearrange("p q (t h c) -> p q t h c", t=H, h=2)
        O0 = acc[:, 0, HN:].rearrange("p (n c) -> p n c", c=C)
        xsq = acc[:, 1, 0:HN]
        NB = HN // BN
        TH = H // NCH

        u_x2 = sem("u_x2")
        u_beta = sem("u_beta")
        u_lin = [sem(f"u_lin{s}") for s in range(2)]
        u_in = [sem(f"u_in{s}") for s in range(2)]
        u_el = [sem(f"u_el{s}") for s in range(2)]
        u_h2 = [sem(f"u_h2{m}") for m in range(4)]
        u_o = [sem(f"u_o{s}") for s in range(2)]
        u_cp = [sem(f"u_cp{s}") for s in range(2)]
        u_ad = [sem(f"u_ad{s}") for s in range(2)]
        u_v = sem("u_v")
        u_par = sem("u_par")
        u_mean = sem("u_mean")
        u_xc = sem("u_xc")
        u_xsq = sem("u_xsq")
        u_var = sem("u_var")
        u_st = sem("u_st")
        u_rt = sem("u_rt")
        u_fin = sem("u_fin")
        u_fin1 = sem("u_fin1")
        u_out = sem("u_out")

        h2v = h2t_tab.rearrange("p (h t d) -> p h t d", h=2, d=D)

        groups = [(n, h) for n in range(NCH) for h in range(2)]
        POOL = 4
        u_scl1 = sem("u_scl1")
        u_prod = sem("u_prod")
        u_prod_pool = sem("u_prod_pool")
        u_fin_pool = sem("u_fin_pool")
        prods_done = {u_prod: 0, u_prod_pool: 0}

        def add_parts(eng, ops, some, q, done):
            made = u_prod_pool if ops is nc.gpsimd else u_prod

            def parts(n, h):
                o = O[:, q:q + 1 + 2 * q, TH * n:TH * n + TH, h, :]
                xt = X2[:, h * H + TH * n:h * H + TH * n + TH, :]
                return o, xt[:, :, 0:C].unsqueeze(1) if q == 0 else xt[:, :, C:D].rearrange("p t (c v) -> p v t c", v=3)

            for m in range(len(some) + 1):
                if m < len(some):
                    o, _ = parts(*some[m])
                    ops.tensor_tensor(o, o, bc(bc(scl[:, q, :], 1, TH), 1, 1 + 2 * q), ALU.mult).then_inc(made, 1)
                    prods_done[made] += 1
                if m >= 1:
                    o, xt = parts(*some[m - 1])
                    eng.wait_ge(made, prods_done[made] - (m < len(some)))
                    ops.tensor_tensor(xt, xt, o, ALU.add).then_inc(done, 1)

        with nc.Block() as block:
            @block.sync
            def _(sp):
                sp.dma_start(X2, rows(x2_tab, 0, T)).then_inc(u_x2, 16)

                def load(i, m):
                    sp.dma_start(h2s[m], h2v[:, :, ds(i, 1), :].rearrange("p h o d -> p (h o) d")).then_inc(u_h2[m], 16)

                for s in range(2):
                    sp.wait_ge(u_el[s], 9 * NB // 2)
                for m in range(4):
                    load(m, m)
                with sp.Fori(1, H // 4) as r:
                    for m in range(4):
                        sp.wait_ge(u_o[m % 2], r * 2 + (m // 2 - 1))
                        load(r * 4 + m, m)
                for i in range(H // 4 * 4, H):
                    sp.wait_ge(u_o[i % 2], i // 2 - 1)
                    load(i, i % 4)
                stores = 1
                for n in range(NCH):
                    for h in range(2):
                        i = 2 * n + h
                        pooled = min(max(i + 1 - NCH, 0), POOL)
                        if pooled:
                            sp.wait_ge(u_fin_pool, pooled)
                        sp.wait_ge(u_fin1, i + 1 - pooled)
                        sp.wait_ge(u_fin, i + 1)
                        t = h * H + n * TH
                        m = min(TH, T - 2 - t)
                        if m > 0:
                            stores += 1
                            sp.dma_start(out[t * P:(t + m) * P, :].rearrange("(t p) d -> p t d", p=P), X2[:, t:t + m, :]).then_inc(u_out, 16)
                sp.dma_start(out[(T - 2) * P:N, :], X2[0:LAST, T - 2, :]).then_inc(u_out, 16)
                sp.wait_ge(u_out, 16 * stores)

            @block.gpsimd
            def _(pool):
                pool.wait_ge(u_x2, 16)
                nc.gpsimd.tensor_tensor(X2[:, :, 0:C], X2[:, :, 0:C], bc(gb_sb[:, 1, :], 1, T), ALU.add).then_inc(u_beta, 1)
                pool.wait_ge(u_scl1, 1)
                add_parts(pool, nc.gpsimd, groups[NCH:NCH + POOL], 1, u_fin_pool)

            @block.tensor
            def _(pe):
                with pe.Fori(0, NB // 2) as k:
                    for s in range(2):
                        n = (k * 2 + s) * BN
                        pe.wait_ge(u_el[s], k * 9)
                        for q, parts in enumerate((((0, 0),), ((0, 1),), ((1, 1), (2, 2)), ((2, 1),))):
                            for h in range(2):
                                for b, wl in parts:
                                    mm = nc.tensor.matmul(ps[:, 4 * s + q, 0:BN], lin_sb[:, wl, h, :], acc[:, b, ds(n + h * HN, BN)],
                                                          start=(h == 0 and (b, wl) == parts[0]), stop=(h == 1 and (b, wl) == parts[-1]))
                        mm.then_inc(u_lin[s], 1)
                for s in range(2):
                    pe.wait_ge(u_el[s], 9 * NB // 2)

                def pair(i, k, s):
                    o = ps[:, s, :].rearrange("p (h d) -> p h d", h=2)
                    pe.wait_ge(u_cp[s], k * 2)
                    for q in range(4):
                        nc.tensor.matmul(o[:, :, q * C:(q + 1) * C], acc[:, q, ds(i * P, P)], wb_sb[:, min(q, 1), :],
                                         start=(q == 0), stop=False)
                    pe.wait_ge(u_h2[i % 4], i // 4 * 16 + 16)
                    for h in range(2):
                        for b in range(2):
                            mm = nc.tensor.matmul(o[:, h, b * P:(b + 1) * P], h2s[i % 4][:, h, b * P:(b + 1) * P], sc_sb[:, b, :],
                                                  start=False, stop=(h == 1 and b == 1))
                    mm.then_inc(u_o[s], 1)

                for k in range(H // 2):
                    for s in range(2):
                        pair(k * 2 + s, k, s)
                pair(H - 1, H // 2, 0)
                pe.wait_ge(u_par, 1)
                nc.tensor.matmul(ps[:, 4, 0:C], ones[:, :], par[:, 0, :], start=True, stop=True).then_inc(u_mean, 1)
                pe.wait_ge(u_par, 2)
                nc.tensor.matmul(ps[:, 5, 0:C], ones[:, :], par[:, 1, :], start=True, stop=True).then_inc(u_var, 1)
                pe.wait_ge(u_par, 3)
                nc.tensor.matmul(ps[:, 6, 0:C], ones[:, :], par[:, 0, :], start=True, stop=True).then_inc(u_var, 1)

            @block.scalar
            def _(act):
                with act.Fori(0, NB // 2) as k:
                    for s in range(2):
                        act.wait_ge(u_lin[s], k + 1)
                        act.wait_ge(u_el[s], k * 9)
                        b = 4 * s

                        def line(to, slope, offset):
                            nc.scalar.activation(to, ps[:, b, 0:BN], ACT.Identity, scale=wc_sb[:, slope:slope + 1],
                                                 bias=wc_sb[:, offset:offset + 1]).then_inc(u_in[s], 1)

                        nc.scalar.activation(a0[s], ps[:, b, 0:BN], ACT.Copy).then_inc(u_in[s], 1)
                        line(hu[s], 3, 1)
                        line(hp[s], 7, 6)
                        nc.scalar.activation(sq[s], ps[:, b + 1:b + 4, 0:BN], ACT.Square).then_inc(u_in[s], 1)
                        line(hw[s], 4, 2)

                for s in range(2):
                    act.wait_ge(u_el[s], 9 * NB // 2)

                def pair(i, k, s):
                    o = ps[:, s, :].rearrange("p (h q c) -> p q h c", h=2, q=4)
                    act.wait_ge(u_o[s], k + 1)
                    act.wait_ge(u_ad[s], k * 2)
                    nc.scalar.activation(osq[:, s, :, :], ps[:, s, :].rearrange("p (h d) -> p h d", h=2)[:, :, C:D],
                                         ACT.Square).then_inc(u_cp[s], 1)
                    nc.scalar.activation(O[:, :, ds(i, 1), :, :].rearrange("p q o h c -> p (q o) h c"), o, ACT.Copy).then_inc(u_cp[s], 1)

                with act.Fori(0, H // 2) as k:
                    for s in range(2):
                        pair(k * 2 + s, k, s)
                pair(H - 1, H // 2, 0)
                act.wait_ge(u_st, 1)
                nc.scalar.activation(stat[:, 1, :], stat[:, 1, :], ACT.Sqrt, bias=eps_sb[:, 0:1]).then_inc(u_rt, 1)
                act.wait_ge(u_xc, 1)
                nc.scalar.activation(xsq, acc[:, 0, HN:], ACT.Square).then_inc(u_xsq, 1)
                act.wait_ge(u_st, 2)
                nc.scalar.activation(stat[:, 0, :], stat[:, 0, :], ACT.Sqrt, bias=eps_sb[:, 0:1]).then_inc(u_rt, 1)

            @block.vector
            def _(dve):
                with dve.Fori(0, NB // 2) as k:
                    for s in range(2):
                        b = 4 * s
                        L = ds((k * 2 + s) * BN, BN)

                        def after(m):
                            dve.wait_ge(u_el[s], k * 9 + m)

                        vv, gq = sq[s][:, 0, :], sq[s][:, 1, :]
                        dve.wait_ge(u_in[s], k * 5 + 2)
                        nc.vector.tensor_tensor(hu[s], hu[s], a0[s], ALU.mult).then_inc(u_el[s], 1)
                        dve.wait_ge(u_in[s], k * 5 + 3)
                        nc.vector.tensor_tensor(hp[s], hp[s], a0[s], ALU.mult).then_inc(u_el[s], 1)
                        after(1)
                        nc.vector.scalar_tensor_tensor(out=hu[s], in0=hu[s], scalar=wc_sb[:, 0:1], in1=a0[s],
                                                       op0=ALU.add, op1=ALU.mult).then_inc(u_el[s], 1)
                        dve.wait_ge(u_in[s], k * 5 + 4)
                        nc.vector.tensor_tensor(vv, vv, sq[s][:, 1, :], ALU.add).then_inc(u_el[s], 1)
                        after(4)
                        nc.vector.tensor_tensor(vv, vv, sq[s][:, 2, :], ALU.add).then_inc(u_el[s], 1)
                        dve.wait_ge(u_in[s], k * 5 + 5)
                        after(5)
                        nc.vector.tensor_tensor(hw[s], hw[s], vv, ALU.mult).then_inc(u_el[s], 1)
                        nc.vector.scalar_tensor_tensor(out=gq, in0=vv, scalar=wc_sb[:, 8:9], in1=hp[s],
                                                       op0=ALU.mult, op1=ALU.add).then_inc(u_el[s], 1)
                        after(6)
                        nc.vector.tensor_tensor(acc[:, 0, L], hu[s], hw[s], ALU.add).then_inc(u_el[s], 1)
                        after(7)
                        nc.vector.scalar_tensor_tensor(out=acc[:, 1:4, L], in0=bc(gq, 1, 3), scalar=wc_sb[:, 5:6],
                                                       in1=ps[:, b + 1:b + 4, 0:BN], op0=ALU.add, op1=ALU.mult).then_inc(u_el[s], 1)
                for s in range(2):
                    dve.wait_ge(u_el[s], 9 * NB // 2)
                nc.vector.memset(tot[:, :, :], 0.0).then_inc(u_v, 1)
                dve.wait_ge(u_v, 1)

                def pair(i, k, s):
                    dve.wait_ge(u_cp[s], k * 2 + 2)
                    dve.wait_ge(u_ad[1 - s], k * 2 + 2 * s)
                    nc.vector.tensor_tensor(tot[:, :, 0:C], tot[:, :, 0:C],
                                            O[:, 0, ds(i, 1), :, :].rearrange("p o h c -> p (o h) c"), ALU.add).then_inc(u_ad[s], 1)
                    nc.vector.tensor_tensor(tot[:, :, C:D], tot[:, :, C:D], osq[:, s, :, :], ALU.add).then_inc(u_ad[s], 1)

                with dve.Fori(0, H // 2) as k:
                    for s in range(2):
                        pair(k * 2 + s, k, s)
                pair(H - 1, H // 2, 0)
                dve.wait_ge(u_ad[0], 2 * (H // 2) + 2)
                dve.wait_ge(u_cp[0], 2 * (H // 2) + 2)
                dve.wait_ge(u_cp[1], 2 * (H // 2))
                count = [1]

                def step(ins):
                    count[0] += 1
                    ins.then_inc(u_v, 1)
                    dve.wait_ge(u_v, count[0])

                nc.vector.tensor_tensor(par[:, 0, :], tot[:, 0, 0:C], tot[:, 1, 0:C], ALU.add).then_inc(u_par, 1)
                step(nc.vector.tensor_tensor(tot[:, 0, C:D], tot[:, 0, C:D], tot[:, 1, C:D], ALU.add))
                nc.vector.tensor_reduce(par[:, 1, :], tot[:, 0, C:D].rearrange("p (v c) -> p c v", v=3), AX_X, ALU.add).then_inc(u_par, 1)
                dve.wait_ge(u_par, 2)
                dve.wait_ge(u_mean, 1)
                nc.vector.tensor_scalar(mean, ps[:, 4, 0:C], 1.0 / N, None, ALU.mult).then_inc(u_v, 1)
                count[0] += 1
                dve.wait_ge(u_var, 1)
                nc.vector.tensor_scalar(stat[:, 1, :], ps[:, 5, 0:C], 1.0 / (3 * N), None, ALU.mult).then_inc(u_st, 1)
                dve.wait_ge(u_v, count[0])
                step(nc.vector.tensor_tensor(O0, O0, bc(mean, 1, T), ALU.subtract))
                step(nc.vector.memset(O[:, 0, H - 1, 1, :], 0.0))
                nc.vector.tensor_scalar(O[:, 0, H - 2, 1, :], O[:, 0, H - 2, 1, :], small[:, 0:1], None, ALU.mult).then_inc(u_xc, 1)
                dve.wait_ge(u_rt, 1)
                step(nc.vector.reciprocal(stat[:, 1, :], stat[:, 1, :]))
                nc.vector.tensor_tensor(scl[:, 1, :], stat[:, 1, :], gb_sb[:, 2, :], ALU.mult).then_inc(u_scl1, 1)
                dve.wait_ge(u_scl1, 1)
                dve.wait_ge(u_x2, 16)
                dve.wait_ge(u_beta, 1)
                add_parts(dve, nc.vector, groups[0:2], 1, u_fin1)
                dve.wait_ge(u_xsq, 1)
                nc.vector.tensor_reduce(par[:, 0, :], xsq.rearrange("p (n c) -> p c n", c=C), AX_X, ALU.add).then_inc(u_par, 1)
                add_parts(dve, nc.vector, groups[2:3], 1, u_fin1)
                dve.wait_ge(u_var, 2)
                nc.vector.tensor_scalar(stat[:, 0, :], ps[:, 6, 0:C], 1.0 / N, None, ALU.mult).then_inc(u_st, 1)
                add_parts(dve, nc.vector, groups[3:4], 1, u_fin1)
                dve.wait_ge(u_rt, 2)
                step(nc.vector.reciprocal(stat[:, 0, :], stat[:, 0, :]))
                step(nc.vector.tensor_tensor(scl[:, 0, :], stat[:, 0, :], gb_sb[:, 0, :], ALU.mult))
                add_parts(dve, nc.vector, groups[0:4], 0, u_fin)
                for i, group in enumerate(groups[4:], 4):
                    if not NCH <= i < NCH + POOL:
                        add_parts(dve, nc.vector, [group], 1, u_fin1)
                    add_parts(dve, nc.vector, [group], 0, u_fin)


_INS = (("x", "x"), ("src", "src"), ("dst", "dst"), ("attr16", "edge_attr_16"), ("attr4", "edge_attr_4"), ("weight", "edge_weight"),
        ("w_self", "L0_gnn_W_self"), ("w_nb", "L0_gnn_W_neighbor"), ("bias", "L0_gnn_bias"), ("w_up0", "L1_gnn_W_up0"),
        ("w_up1", "L1_gnn_W_up1"), ("m1", "L1_gnn_M1"), ("m2", "L1_gnn_M2"), ("m3", "L1_gnn_M3"), ("m4", "L1_gnn_M4"),
        ("w_lin0", "L1_gnn_W_lin0"), ("w_lin1", "L1_gnn_W_lin1"), ("w_sc0", "L1_gnn_Wsc0"), ("w_sc1", "L1_gnn_Wsc1"),
        ("wc0", "L1_gnn_Wc0"), ("wc1", "L1_gnn_Wc1"), ("w_b0", "L1_gnn_WB0"), ("w_b1", "L1_gnn_WB1"),
        ("gamma0", "L1_gnn_gamma0"), ("beta0", "L1_gnn_beta0"), ("gamma1", "L1_gnn_gamma1"))


def kernel(**inputs):
    import numpy as np
    import concourse.bacc as bacc
    from concourse.bass_utils import run_bass_kernel_spmd

    nc = bacc.Bacc("TRN2", target_bir_lowering=False, num_devices=1)
    arrays, args = {}, {}
    for arg, name in _INS:
        a = np.ascontiguousarray(inputs[name])
        arrays["in_" + name] = a
        args[arg] = nc.dram_tensor("in_" + name, a.shape, mybir.dt.from_np(a.dtype), kind="ExternalInput").ap()
    args["out"] = nc.dram_tensor("out_0", (N, D), F32, kind="ExternalOutput").ap()
    build(nc, **args)
    r = run_bass_kernel_spmd(nc, [arrays], core_ids=[0])
    return r.results[0]["out_0"]
```
